# Optimizing a Trainium2 kernel written in Bass

```python
import numpy as np
import jax
import jax.numpy as jnp

def _softmax(x, axis=-1):
    return jax.nn.softmax(x, axis=axis)

def _gelu(x):
    return jax.nn.gelu(x, approximate=True)

def _silu(x):
    return jax.nn.silu(x)

def _sigmoid(x):
    return jax.nn.sigmoid(x)

def _layernorm(x, axis=-1, eps=1e-05):
    m = jnp.mean(x, axis=axis, keepdims=True)
    v = jnp.var(x, axis=axis, keepdims=True)
    return (x - m) / jnp.sqrt(v + eps)

def _scatter_add(tgt, idx, src, axis=0):
    return tgt.at[idx].add(src)

def _segment_sum(src, seg, n):
    return jax.ops.segment_sum(src, seg, n)
kernel_name = 'mk_xattn_ffn_d2_seqx_r8_d7dbec'

def setup_inputs(seed: int=0):
    np.random.seed(seed)
    _w = jnp.asarray

    def _rec_inputs():
        import jax
        import jax.numpy as jnp
        _rk = jax.random.key(seed)
        x = -0.0003929 + 0.9999 * jax.random.normal(jax.random.fold_in(_rk, 1), (1, 1024, 128), jnp.float32)
        _lenS = 1024 - jax.random.randint(jax.random.fold_in(_rk, 7), (1,), 0, max(1, 1024 // 4) + 1, jnp.int32)
        _lenS2 = 6404 - jax.random.randint(jax.random.fold_in(_rk, 8), (1,), 0, max(1, 6404 // 4) + 1, jnp.int32)
        _ctx_1024P = jax.random.normal(jax.random.fold_in(_rk, 11), (1, 16, 128), jnp.float32)
        _ctx_1024c = jax.random.dirichlet(jax.random.fold_in(_rk, 511), 0.3 * jnp.ones((16,), jnp.float32), (1, 6404))
        _ctx_1024t = jnp.einsum('bsk,bkd->bsd', _ctx_1024c, _ctx_1024P)
        _ctx_1024t = _ctx_1024t * jax.lax.rsqrt(jnp.mean(jnp.square(_ctx_1024t)) + 1e-12) * 0.953939
        ctx_1024 = 2.81802e-05 + 1.00001 * (_ctx_1024t + 0.3 * jax.random.normal(jax.random.fold_in(_rk, 611), (1, 6404, 128), jnp.float32))
        fside_1xSxS2_0 = 0.000675642 + 1.00031 * jax.random.normal(jax.random.fold_in(_rk, 12), (1, 1024, 6404), jnp.float32)
        return (x, ctx_1024, fside_1xSxS2_0)
    x, ctx_1024, fside_1xSxS2_0 = _rec_inputs()

    def _L0_xattn_setup():
        import jax, jax.numpy as jnp
        import numpy as np
        import math
        D = 128
        B, S = (8, 256)

        def _proj(x, W1, b1, W2, b2):
            h = jnp.einsum('bsd,od->bso', x, W1) + b1
            return jnp.einsum('bsd,od->bso', h, W2) + b2
        key = jax.random.key(seed)
        ks = jax.random.split(key, 8)
        q = jax.random.normal(ks[0], (B, S, D), dtype=jnp.float32)
        k = jax.random.normal(ks[1], (B, S, D), dtype=jnp.float32)
        v1 = jax.random.normal(ks[2], (B, S, D), dtype=jnp.float32)
        mask = jax.random.normal(ks[3], (1, S, S), dtype=jnp.float32)
        lim = 1.0 / math.sqrt(D)
        W1 = jax.random.uniform(ks[4], (D, D), jnp.float32, -lim, lim)
        b1 = jax.random.uniform(ks[5], (D,), jnp.float32, -lim, lim)
        W2 = jax.random.uniform(ks[6], (D, D), jnp.float32, -lim, lim)
        b2 = jax.random.uniform(ks[7], (D,), jnp.float32, -lim, lim)
        return {'q': q, 'k': k, 'v1': v1, 'mask': mask, 'W1': W1, 'b1': b1, 'W2': W2, 'b2': b2}
    _L0_xattn_all = _L0_xattn_setup()
    _L0_xattn_in = {k: v for k, v in _L0_xattn_all.items() if k in ('W1', 'b1', 'W2', 'b2')}
    del _L0_xattn_all

    def _L0_ffn_setup():
        import jax, jax.numpy as jnp
        import numpy as np
        B, S, D = (2, 64, 128)
        E, K, I = (16, 8, 128)
        I_SH = 128
        ROUTE_SCALE = 2.826
        key = jax.random.key(seed)
        ks = jax.random.split(key, 8)
        s = 0.02
        return {'x': jax.random.normal(ks[0], (B, S, D), dtype=jnp.float32), 'gate_w': jax.random.normal(ks[1], (E, D), dtype=jnp.float32) * s, 'expert_bias': jnp.zeros((E,), dtype=jnp.float32), 'w_gate': jax.random.normal(ks[2], (E, I, D), dtype=jnp.float32) * s, 'w_up': jax.random.normal(ks[3], (E, I, D), dtype=jnp.float32) * s, 'w_down': jax.random.normal(ks[4], (E, D, I), dtype=jnp.float32) * s, 'shared_gate_w': jax.random.normal(ks[5], (I_SH, D), dtype=jnp.float32) * s, 'shared_up_w': jax.random.normal(ks[6], (I_SH, D), dtype=jnp.float32) * s, 'shared_down_w': jax.random.normal(ks[7], (D, I_SH), dtype=jnp.float32) * s}
    _L0_ffn_all = _L0_ffn_setup()
    _L0_ffn_in = {k: v for k, v in _L0_ffn_all.items() if k in ('gate_w', 'expert_bias', 'w_gate', 'w_up', 'w_down', 'shared_gate_w', 'shared_up_w', 'shared_down_w')}
    del _L0_ffn_all

    def _L1_xattn_setup():
        import jax, jax.numpy as jnp
        import numpy as np
        DIM = 128
        NUM_HEADS = 16
        HEAD_DIM = DIM // NUM_HEADS
        key = jax.random.key(seed)
        ks = jax.random.split(key, 11)
        B, N, C = (2, 256, DIM)
        s = 1.0 / np.sqrt(C)
        inp = {'q': jax.random.normal(ks[0], (B, N, C), jnp.float32), 'k': jax.random.normal(ks[1], (B, N, C), jnp.float32), 'v': jax.random.normal(ks[2], (B, N, C), jnp.float32), 'Wq': jax.random.normal(ks[3], (C, C), jnp.float32) * s, 'bq': jnp.zeros((C,), jnp.float32), 'Wk': jax.random.normal(ks[4], (C, C), jnp.float32) * s, 'bk': jnp.zeros((C,), jnp.float32), 'Wv': jax.random.normal(ks[5], (C, C), jnp.float32) * s, 'bv': jnp.zeros((C,), jnp.float32), 'Wo': jax.random.normal(ks[6], (C, C), jnp.float32) * s, 'bo': jnp.zeros((C,), jnp.float32)}
        return inp
    _L1_xattn_all = _L1_xattn_setup()
    _L1_xattn_in = {k: v for k, v in _L1_xattn_all.items() if k in ('Wq', 'bq', 'Wk', 'bk', 'Wv', 'bv', 'Wo', 'bo')}
    del _L1_xattn_all

    def _L1_ffn_setup():
        import jax, jax.numpy as jnp
        import numpy as np
        B, S, D = (4, 256, 128)
        P = 9
        DM = D // 4
        EPS = 1e-05

        def _mix(x, mix_kernel):
            xp = jnp.pad(x, ((0, 0), (1, 1), (0, 0)))
            return mix_kernel[0] * xp[:, :-2] + mix_kernel[1] * xp[:, 1:-1] + mix_kernel[2] * xp[:, 2:]

        def _layernorm(h, gamma, beta):
            mu = jnp.mean(h, axis=-1, keepdims=True)
            var = jnp.var(h, axis=-1, keepdims=True)
            return (h - mu) * jax.lax.rsqrt(var + EPS) * gamma + beta
        key = jax.random.key(seed)
        ks = jax.random.split(key, 12)
        sc_in = 1.0 / np.sqrt(D)
        sc_mid = 1.0 / np.sqrt(DM)
        return {'x': jax.random.normal(ks[0], (B, S, D), dtype=jnp.float32), 'mix_kernel': jax.random.normal(ks[1], (3, D), dtype=jnp.float32) * 0.5, 'W1': jax.random.normal(ks[2], (P, D, DM), dtype=jnp.float32) * sc_in, 'b1': jnp.zeros((P, DM), dtype=jnp.float32), 'W2': jax.random.normal(ks[3], (P, DM, D), dtype=jnp.float32) * sc_mid, 'b2': jnp.zeros((P, D), dtype=jnp.float32), 'Wo1': jax.random.normal(ks[4], (D, DM), dtype=jnp.float32) * sc_in, 'bo1': jnp.zeros((DM,), dtype=jnp.float32), 'Wo2': jax.random.normal(ks[5], (DM, P), dtype=jnp.float32) * sc_mid, 'bo2': jnp.zeros((P,), dtype=jnp.float32), 'gamma': jnp.ones((D,), dtype=jnp.float32), 'beta': jnp.zeros((D,), dtype=jnp.float32)}
    _L1_ffn_all = _L1_ffn_setup()
    _L1_ffn_in = {k: v for k, v in _L1_ffn_all.items() if k in ('mix_kernel', 'W1', 'b1', 'W2', 'b2', 'Wo1', 'bo1', 'Wo2', 'bo2', 'gamma', 'beta')}
    del _L1_ffn_all
    return {'x': x, 'ctx_1024': ctx_1024, 'fside_1xSxS2_0': fside_1xSxS2_0, 'L0_xattn_W1': _L0_xattn_in['W1'], 'L0_xattn_b1': _L0_xattn_in['b1'], 'L0_xattn_W2': _L0_xattn_in['W2'], 'L0_xattn_b2': _L0_xattn_in['b2'], 'L0_ffn_gate_w': _L0_ffn_in['gate_w'], 'L0_ffn_expert_bias': _L0_ffn_in['expert_bias'], 'L0_ffn_w_gate': _L0_ffn_in['w_gate'], 'L0_ffn_w_up': _L0_ffn_in['w_up'], 'L0_ffn_w_down': _L0_ffn_in['w_down'], 'L0_ffn_shared_gate_w': _L0_ffn_in['shared_gate_w'], 'L0_ffn_shared_up_w': _L0_ffn_in['shared_up_w'], 'L0_ffn_shared_down_w': _L0_ffn_in['shared_down_w'], 'L1_xattn_Wq': _L1_xattn_in['Wq'], 'L1_xattn_bq': _L1_xattn_in['bq'], 'L1_xattn_Wk': _L1_xattn_in['Wk'], 'L1_xattn_bk': _L1_xattn_in['bk'], 'L1_xattn_Wv': _L1_xattn_in['Wv'], 'L1_xattn_bv': _L1_xattn_in['bv'], 'L1_xattn_Wo': _L1_xattn_in['Wo'], 'L1_xattn_bo': _L1_xattn_in['bo'], 'L1_ffn_mix_kernel': _L1_ffn_in['mix_kernel'], 'L1_ffn_W1': _L1_ffn_in['W1'], 'L1_ffn_b1': _L1_ffn_in['b1'], 'L1_ffn_W2': _L1_ffn_in['W2'], 'L1_ffn_b2': _L1_ffn_in['b2'], 'L1_ffn_Wo1': _L1_ffn_in['Wo1'], 'L1_ffn_bo1': _L1_ffn_in['bo1'], 'L1_ffn_Wo2': _L1_ffn_in['Wo2'], 'L1_ffn_bo2': _L1_ffn_in['bo2'], 'L1_ffn_gamma': _L1_ffn_in['gamma'], 'L1_ffn_beta': _L1_ffn_in['beta']}

def reference(x, ctx_1024, fside_1xSxS2_0, L0_xattn_W1, L0_xattn_b1, L0_xattn_W2, L0_xattn_b2, L0_ffn_gate_w, L0_ffn_expert_bias, L0_ffn_w_gate, L0_ffn_w_up, L0_ffn_w_down, L0_ffn_shared_gate_w, L0_ffn_shared_up_w, L0_ffn_shared_down_w, L1_xattn_Wq, L1_xattn_bq, L1_xattn_Wk, L1_xattn_bk, L1_xattn_Wv, L1_xattn_bv, L1_xattn_Wo, L1_xattn_bo, L1_ffn_mix_kernel, L1_ffn_W1, L1_ffn_b1, L1_ffn_W2, L1_ffn_b2, L1_ffn_Wo1, L1_ffn_bo1, L1_ffn_Wo2, L1_ffn_bo2, L1_ffn_gamma, L1_ffn_beta):
    import jax
    import jax.numpy as jnp

    def _L0_xattn_ref(q, k, v1, mask, W1, b1, W2, b2):
        import jax, jax.numpy as jnp
        import numpy as np
        import math
        D = 128
        B, S = (8, 256)

        def _proj(x, W1, b1, W2, b2):
            h = jnp.einsum('bsd,od->bso', x, W1) + b1
            return jnp.einsum('bsd,od->bso', h, W2) + b2
        qp = _proj(q, W1, b1, W2, b2)
        kp = _proj(k, W1, b1, W2, b2)
        scale = 1.0 / math.sqrt(qp.shape[-1])
        qk = jnp.einsum('bqd,bkd->bqk', qp, kp) * scale
        qk = qk + mask
        attn = jax.nn.softmax(qk, axis=-1)
        return jnp.einsum('bqk,bkd->bqd', attn, v1)

    def _L0_ffn_ref(x, gate_w, expert_bias, w_gate, w_up, w_down, shared_gate_w, shared_up_w, shared_down_w):
        import jax, jax.numpy as jnp
        import numpy as np
        B, S, D = (2, 64, 128)
        E, K, I = (16, 8, 128)
        I_SH = 128
        ROUTE_SCALE = 2.826
        gates = jnp.einsum('bsd,ed->bse', x, gate_w)
        scores = jax.nn.sigmoid(gates.astype(jnp.float32))
        sel_scores = scores + expert_bias
        _, inds = jax.lax.top_k(sel_scores, K)
        selected = jnp.take_along_axis(scores, inds, axis=-1)
        selected = selected / selected.sum(axis=-1, keepdims=True)
        selected = selected * ROUTE_SCALE
        onehot = jax.nn.one_hot(inds, E, dtype=selected.dtype)
        combine = jnp.einsum('bske,bsk->bse', onehot, selected)
        hg = jnp.einsum('bsd,eid->bsei', x, w_gate)
        hu = jnp.einsum('bsd,eid->bsei', x, w_up)
        h = jax.nn.silu(hg) * hu
        ye = jnp.einsum('bsei,edi->bsed', h, w_down)
        y = jnp.einsum('bsed,bse->bsd', ye, combine).astype(x.dtype)
        g = jnp.einsum('bsd,id->bsi', x, shared_gate_w)
        u = jnp.einsum('bsd,id->bsi', x, shared_up_w)
        y = y + jnp.einsum('bsi,di->bsd', jax.nn.silu(g) * u, shared_down_w)
        return y

    def _L1_xattn_ref(q, k, v, Wq, bq, Wk, bk, Wv, bv, Wo, bo):
        import jax, jax.numpy as jnp
        import numpy as np
        DIM = 128
        NUM_HEADS = 16
        HEAD_DIM = DIM // NUM_HEADS
        B, Nq, C = q.shape
        Nkv = k.shape[1]
        H, D = (NUM_HEADS, HEAD_DIM)
        qh = (q @ Wq.T + bq).reshape(B, Nq, H, D).transpose(0, 2, 1, 3)
        kh = (k @ Wk.T + bk).reshape(B, Nkv, H, D).transpose(0, 2, 1, 3)
        vh = (v @ Wv.T + bv).reshape(B, Nkv, H, D).transpose(0, 2, 1, 3)
        scale = D ** (-0.5)
        attn = jax.nn.softmax(jnp.einsum('bhqd,bhkd->bhqk', qh, kh) * scale, axis=-1)
        out = jnp.einsum('bhqk,bhkd->bhqd', attn, vh)
        out = out.transpose(0, 2, 1, 3).reshape(B, Nq, C)
        return out @ Wo.T + bo

    def _L1_ffn_ref(x, mix_kernel, W1, b1, W2, b2, Wo1, bo1, Wo2, bo2, gamma, beta):
        import jax, jax.numpy as jnp
        import numpy as np
        B, S, D = (4, 256, 128)
        P = 9
        DM = D // 4
        EPS = 1e-05

        def _mix(x, mix_kernel):
            xp = jnp.pad(x, ((0, 0), (1, 1), (0, 0)))
            return mix_kernel[0] * xp[:, :-2] + mix_kernel[1] * xp[:, 1:-1] + mix_kernel[2] * xp[:, 2:]

        def _layernorm(h, gamma, beta):
            mu = jnp.mean(h, axis=-1, keepdims=True)
            var = jnp.var(h, axis=-1, keepdims=True)
            return (h - mu) * jax.lax.rsqrt(var + EPS) * gamma + beta
        x_mixed = _mix(x, mix_kernel)
        h = jnp.einsum('bsd,pdm->bspm', x_mixed, W1) + b1
        stacked_paths = jnp.einsum('bspm,pmd->bspd', h, W2) + b2
        scores = jnp.tanh(x_mixed @ Wo1 + bo1) @ Wo2 + bo2
        idx = jnp.argmax(scores, axis=-1)
        weights = jax.nn.one_hot(idx, P, dtype=stacked_paths.dtype)
        collapsed = jnp.einsum('bspd,bsp->bsd', stacked_paths, weights)
        return _layernorm(x + collapsed, gamma, beta)
    x = x + _L0_xattn_ref(_layernorm(x, axis=-1), ctx_1024, ctx_1024, fside_1xSxS2_0, L0_xattn_W1, L0_xattn_b1, L0_xattn_W2, L0_xattn_b2)
    x = x + _L0_ffn_ref(_layernorm(x, axis=-1), L0_ffn_gate_w, L0_ffn_expert_bias, L0_ffn_w_gate, L0_ffn_w_up, L0_ffn_w_down, L0_ffn_shared_gate_w, L0_ffn_shared_up_w, L0_ffn_shared_down_w)
    x = x + _L1_xattn_ref(_layernorm(x, axis=-1), ctx_1024, ctx_1024, L1_xattn_Wq, L1_xattn_bq, L1_xattn_Wk, L1_xattn_bk, L1_xattn_Wv, L1_xattn_bv, L1_xattn_Wo, L1_xattn_bo)
    x = x + _L1_ffn_ref(_layernorm(x, axis=-1), L1_ffn_mix_kernel, L1_ffn_W1, L1_ffn_b1, L1_ffn_W2, L1_ffn_b2, L1_ffn_Wo1, L1_ffn_bo1, L1_ffn_Wo2, L1_ffn_bo2, L1_ffn_gamma, L1_ffn_beta)
    return x

_drawn_inputs = setup_inputs


def setup_inputs(seed=0):
    import zlib

    import numpy as np

    out = dict(_drawn_inputs(seed))
    spreads = {'L0_ffn_expert_bias': (0.0, 0.324),
     'L1_xattn_bq': (0.0, 0.1),
     'L1_xattn_bk': (0.0, 0.8),
     'L1_xattn_bv': (0.0, 0.1),
     'L1_xattn_bo': (0.0, 0.1),
     'L1_ffn_b1': (0.0, 0.1),
     'L1_ffn_b2': (0.0, 0.1),
     'L1_ffn_bo1': (0.0, 0.1),
     'L1_ffn_bo2': (0.0, 0.1),
     'L1_ffn_gamma': (1.0, 0.2),
     'L1_ffn_beta': (0.0, 0.1)}
    factors = {'L0_xattn_b1': 8.0,
     'L0_xattn_b2': 5.793,
     'L0_ffn_gate_w': 4.049,
     'L0_ffn_w_gate': 2.961,
     'L0_ffn_w_up': 3.304,
     'L0_ffn_w_down': 2.96,
     'L0_ffn_shared_gate_w': 3.68,
     'L0_ffn_shared_up_w': 3.237,
     'L0_ffn_shared_down_w': 4.959}
    for name, (base, spread) in spreads.items():
        noise = np.random.default_rng([zlib.crc32(name.encode()), seed]).standard_normal(out[name].shape)
        drawn = base * np.exp(spread * noise) if base else spread * noise
        out[name] = jnp.asarray(drawn.astype(out[name].dtype))
    for name, factor in factors.items():
        out[name] = (out[name] * factor).astype(out[name].dtype)
    return out
```

```python
from contextlib import ExitStack

import concourse.bass as bass
from concourse import mybir

F32 = mybir.dt.float32
BF16 = mybir.dt.bfloat16
U32 = mybir.dt.uint32
ALU = mybir.AluOpType
ACT = mybir.ActivationFunctionType
AX_X = mybir.AxisListType.X

P = 128
D = 128
S = 1024
ST = S // P
NK = 6404
KF = NK // P
KR = NK - KF * P
KT = KF + 1
BANK = 512
NCH = NK // BANK
CR = NK - NCH * BANK
EPS = 1e-5
LOWEST = -3.0e38


class Link:

    def __init__(self, eng, sem):
        self.eng, self.sem, self.base, self.n = eng, sem, 0, 0

    def __call__(self, ins):
        self.n += 1
        ins.then_inc(self.sem, 1)
        self.eng.wait_ge(self.sem, self.base + self.n)

    def enter(self, i, per):
        self.start = self.base + self.n
        self.per = per
        self.base, self.n = self.start + i * per, 0

    def leave(self, passes):
        assert self.n == self.per, (self.n, self.per)
        self.base, self.n = self.start + passes * self.per, 0


def layer_norm_stats(nc, link, src, stats, mv, var, tiles, ready):
    for t in range(tiles):
        link(nc.vector.bn_stats(out=stats[:, t, :], in_=src[:, t, :]))
    for t in range(tiles):
        link(nc.vector.bn_aggr(out=mv[:, t, :], in_=stats[:, t, :]))
    nc.vector.tensor_scalar(var[:, :], mv[:, :, 1], EPS, None, ALU.add).then_inc(ready, 1)


def layer_norm_apply(nc, link, dst, src, mv, rstd, tiles, ready):
    link(nc.vector.reciprocal(rstd[:, :], rstd[:, :]))
    for t in range(tiles):
        nc.vector.tensor_scalar(dst[:, t, :], src[:, t, :], mv[:, t, 0:1], rstd[:, t:t + 1],
                                ALU.subtract, ALU.mult).then_inc(ready, 1)


def cross_attention_0(nc, g, a):
    SCALE = float(D) ** -0.5
    MS = 2
    SB = 3
    TB = 3
    GROUPS = [list(range(4 * i, min(4 * i + 4, KT))) for i in range((KT + 3) // 4)]
    NG = len(GROUPS)
    with ExitStack() as ctx:
        def sb(name, shape, dt=F32):
            return ctx.enter_context(nc.sbuf_tensor(name, shape, dt))

        def sem(name):
            return ctx.enter_context(nc.semaphore(name))

        ctx_nat = sb("a0_ctx", [P, KT, D])
        kT = sb("a0_kT", [P, NK])
        ms = sb("a0_ms", [P, MS, NK])
        pr = sb("a0_pr", [P, MS, NK])
        chunk = sb("a0_chunk", [P, 2, 4, D])
        chunkT = sb("a0_chunkT", [P, 2, BANK])
        hT = sb("a0_hT", [P, 2, BANK])
        pT = sb("a0_pT", [P, TB, BANK])
        w_nat = sb("a0_w", [P, 2, D])
        wT = sb("a0_wT", [P, 2, D])
        bias = sb("a0_bias", [P, 2])
        xn = sb("a0_xn", [P, ST, D])
        xnT = sb("a0_xnT", [P, S])
        q1T = sb("a0_q1T", [P, S])
        qT = sb("a0_qT", [P, S])
        oT = sb("a0_oT", [P, 2, P])
        stats = sb("a0_stats", [P, ST, 6])
        mv = sb("a0_mv", [P, ST, 2])
        rstd = sb("a0_rstd", [P, ST])
        cmax = sb("a0_cmax", [P, 2, NCH + 1])
        nmax = sb("a0_nmax", [P, 2])
        total = sb("a0_total", [P, 2])
        rtotal = sb("a0_rtotal", [P, 2])
        q_tile = sb("a0_q_tile", [P, 2, P])
        ps = g["ps"]
        x = g["x"]
        q_tile_ready = sem("a0_q_tile_ready")

        x_in, w_in, ctx_in = sem("a0_x_in"), sem("a0_w_in"), sem("a0_ctx_in")
        chunk_in = [sem(f"a0_chunk_in{i}") for i in range(2)]
        mask_in = [sem(f"a0_mask_in{i}") for i in range(MS)]
        ident_made = sem("a0_ident_made")
        w_turned, w_kept = sem("a0_w_turned"), sem("a0_w_kept")
        var_ready, std_ready, xn_ready = sem("a0_var"), sem("a0_std"), sem("a0_xn_ready")
        xn_turned, xnT_kept = sem("a0_xn_turned"), sem("a0_xnT_kept")
        q1_ready, q1_kept, q_ready, q_kept = sem("a0_q1"), sem("a0_q1k"), sem("a0_q"), sem("a0_qk")
        chunk_turned, chunkT_kept = sem("a0_ct"), sem("a0_ck")
        h_ready, h_kept, k_ready, k_kept = sem("a0_h"), sem("a0_hk"), sem("a0_k"), sem("a0_kk")
        scores_ready, scores_masked = sem("a0_s"), sem("a0_sm")
        max_ready, probs_ready = sem("a0_max"), sem("a0_probs")
        probs_turned, pT_kept, pv_done = sem("a0_pt"), sem("a0_ptk"), sem("a0_pv")
        out_ready, oT_kept, out_turned, x_done = sem("a0_o"), sem("a0_ok"), sem("a0_ot"), sem("a0_xd")
        dve_step, pool_step, dve_passed = sem("a0_dve_step"), sem("a0_pool_step"), sem("a0_dve_passed")

        block = ctx.enter_context(nc.Block())
        FREE = 2

        def turned_rows(kt):
            return P if kt < KF else KR

        @block.sync
        def _(sp):
            sp.dma_start(x[:, :, :], a["x"][0].rearrange("(t p) d -> p t d", p=P)).then_inc(x_in, 16)
            sp.dma_start(w_nat[:, 0, :], a["L0_xattn_W1"]).then_inc(w_in, 16)
            sp.dma_start(w_nat[:, 1, :], a["L0_xattn_W2"]).then_inc(w_in, 16)
            sp.dma_start(bias[:, 0:1], a["L0_xattn_b1"].rearrange("(p o) -> p o", o=1)).then_inc(w_in, 16)
            sp.dma_start(bias[:, 1:2], a["L0_xattn_b2"].rearrange("(p o) -> p o", o=1)).then_inc(w_in, 16)
            ctx_rows = a["ctx_1024"][0]

            def load_chunk(c, slot):
                sp.dma_start(chunk[:, slot, :, :],
                             ctx_rows[bass.ds(c * BANK, BANK), :].rearrange("(n p) d -> p n d", p=P)
                             ).then_inc(chunk_in[slot], 16)

            def load_mask(t, slot):
                sp.dma_start(ms[:, slot, :], a["fside_1xSxS2_0"][0][bass.ds(t * P, P), :]
                             ).then_inc(mask_in[slot], 16)

            for c in range(2):
                load_chunk(c, c)
            load_mask(0, 0)
            sp.dma_start(ctx_nat[:, 0:KF, :],
                         ctx_rows[0:KF * P, :].rearrange("(n p) d -> p n d", p=P)).then_inc(ctx_in, 16)
            sp.dma_start(ctx_nat[0:KR, KF, :], ctx_rows[KF * P:NK, :]).then_inc(ctx_in, 16)
            load_mask(1, 1)
            with sp.Fori(1, NCH // 2) as i:
                for slot in range(2):
                    sp.wait_ge(chunk_turned, 2 * i + slot - 1)
                    load_chunk(2 * i + slot, slot)
            sp.wait_ge(chunk_turned, NCH - 1)
            sp.dma_start(chunk[:, 0, 0:2, :],
                         ctx_rows[NCH * BANK:KF * P, :].rearrange("(n p) d -> p n d", p=P)
                         ).then_inc(chunk_in[0], 16)
            sp.dma_start(chunk[0:KR, 0, 2, :], ctx_rows[KF * P:NK, :]).then_inc(chunk_in[0], 16)
            with sp.Fori(1, ST // 2) as i:
                for slot in range(2):
                    sp.wait_ge(probs_ready, 2 * i + slot - 1)
                    load_mask(2 * i + slot, slot)

        @block.gpsimd
        def _(pool):
            link = Link(pool, pool_step)
            for ident in (g["ident"], g["identb"]):
                link(nc.gpsimd.memset(ident[:, :], 0.0))
                nc.gpsimd.affine_select(out=ident[:, :], in_=ident[:, :], compare_op=ALU.not_equal,
                                        fill=1.0, base=0, pattern=[[-1, P]],
                                        channel_multiplier=1).then_inc(ident_made, 1)

        @block.tensor
        def _(pe):
            ident = g["ident"]
            pe.sem_inc(h_ready, FREE)
            pe.sem_inc(k_ready, FREE)
            pe.wait_ge(ident_made, 2)
            pe.wait_ge(w_in, 64)
            for j in range(2):
                mm = pe.transpose(ps[7][:, j * D:(j + 1) * D], w_nat[:, j, :], ident[:, :])
            mm.then_inc(w_turned, 1)
            pe.wait_ge(w_kept, 1)

            def turn_chunk(c, slot, tiles):
                for j, rows in enumerate(tiles):
                    mm = pe.transpose(ps[slot][:, j * P:j * P + rows], chunk[0:rows, slot, j, :],
                                      ident[0:rows, 0:rows])
                mm.then_inc(chunk_turned, 1)

            def project(c, slot, w, src, src_kept, bank, ready, n):
                pe.wait_ge(src_kept, c + 1 + FREE)
                pe.matmul(ps[bank + slot][:, 0:n], wT[:, w, :], src[:, slot, 0:n],
                          start=True, stop=True).then_inc(ready, 1)

            with pe.Fori(0, NCH // 2) as i:
                for slot in range(2):
                    pe.wait_ge(chunk_in[slot], 16 * i + 16)
                    pe.wait_ge(chunkT_kept, 2 * i + FREE)
                    turn_chunk(2 * i + slot, slot, [P] * 4)
                for slot in range(2):
                    pe.wait_ge(h_kept, 2 * i + FREE)
                    project(2 * i + slot, slot, 0, chunkT, chunkT_kept, 2, h_ready, BANK)
                for slot in range(2):
                    pe.wait_ge(k_kept, 2 * i + FREE)
                    project(2 * i + slot, slot, 1, hT, h_kept, 4, k_ready, BANK)
            pe.wait_ge(chunk_in[0], 16 * (NCH // 2) + 32)
            turn_chunk(NCH, 0, [P] * (KF - 4 * NCH) + [KR])
            project(NCH, 0, 0, chunkT, chunkT_kept, 2, h_ready, CR)
            project(NCH, 0, 1, hT, h_kept, 4, k_ready, CR)

            pe.wait_ge(xn_ready, ST)
            for t in range(ST):
                if t % 4 == 0:
                    pe.wait_ge(k_kept, NCH + 1 + FREE)
                mm = pe.transpose(ps[6 + t // 4][:, (t % 4) * P:(t % 4 + 1) * P], xn[:, t, :], ident[:, :])
                if t % 4 == 3:
                    mm.then_inc(xn_turned, 1)
            for w, src, kept, ready in ((0, xnT, xnT_kept, q1_ready), (1, q1T, q1_kept, q_ready)):
                for j in range(2):
                    pe.wait_ge(kept, j + 1)
                    pe.matmul(ps[6 + j][:, :], wT[:, w, :], src[:, j * BANK:(j + 1) * BANK],
                              start=True, stop=True).then_inc(ready, 1)
            pe.wait_ge(q_kept, 2)

            def scores(t, slot, first=False):
                pe.wait_ge(q_tile_ready, t + 1)
                for c in range(NCH + 1):
                    n = BANK if c < NCH else CR
                    if c >= SB:
                        pe.wait_ge(scores_masked, t * (NCH + 1) + c - SB + 1)
                    elif not first:
                        pe.wait_ge(scores_masked, t * (NCH + 1))
                    pe.matmul(ps[c % SB][:, 0:n], q_tile[:, slot, :], kT[:, c * BANK:c * BANK + n],
                              start=True, stop=True).then_inc(scores_ready, 1)

            def turn_probs(t, slot, gi):
                for j, kt in enumerate(GROUPS[gi]):
                    rows = turned_rows(kt)
                    mm = pe.transpose(ps[SB + gi % TB][0:rows, j * P:(j + 1) * P],
                                      pr[:, slot, kt * P:kt * P + rows], ident[:, :])
                mm.then_inc(probs_turned, 1)

            def weigh(t, slot, first=False):
                pe.wait_ge(probs_ready, t + 1)
                for gi in range(NG + 1):
                    if gi < NG:
                        if gi >= TB:
                            pe.wait_ge(pT_kept, t * NG + gi - TB + 1)
                        elif not first:
                            pe.wait_ge(pT_kept, t * NG)
                        turn_probs(t, slot, gi)
                    if gi >= 1:
                        pe.wait_ge(pT_kept, t * NG + gi)
                        for j, kt in enumerate(GROUPS[gi - 1]):
                            rows = turned_rows(kt)
                            if kt == 0 and not first:
                                pe.wait_ge(x_done, t - 1)
                            mm = pe.matmul(ps[6 + slot][:, 0:P], ctx_nat[0:rows, kt, :],
                                           pT[0:rows, (gi - 1) % TB, j * P:(j + 1) * P],
                                           start=(kt == 0), stop=(kt == KT - 1))
                        mm.then_inc(pv_done, 1)
                pe.wait_ge(oT_kept, t + 1)
                pe.transpose(ps[6 + slot][:, 0:P], oT[:, slot, :], ident[:, :]).then_inc(out_turned, 1)

            pe.wait_ge(ctx_in, 32)
            scores(0, 0, first=True)
            scores(1, 1)
            weigh(0, 0, first=True)
            scores(2, 0)
            weigh(1, 1)
            scores(3, 1)
            with pe.Fori(1, ST // 2 - 1) as i:
                for slot in range(2):
                    weigh(2 * i + slot, slot)
                    scores(2 * i + slot + 2, slot)
            for slot in range(2):
                weigh(ST - 2 + slot, slot)

        @block.vector
        def _(dve):
            link = Link(dve, dve_step)
            dve.sem_inc(chunkT_kept, FREE)
            dve.wait_ge(w_turned, 1)
            dve.tensor_copy(wT[:, :, :], ps[7][:, 0:2 * D].rearrange("p (j d) -> p j d", j=2)).then_inc(w_kept, 1)

            dve.wait_ge(x_in, 16)
            layer_norm_stats(nc, link, x, stats, mv, rstd, ST, var_ready)
            dve.wait_ge(std_ready, 1)
            layer_norm_apply(nc, link, xn, x, mv, rstd, ST, xn_ready)

            def keep_chunk(c, slot, n):
                dve.wait_ge(chunk_turned, c + 1)
                dve.wait_ge(h_ready, c - slot + FREE)
                dve.tensor_copy(chunkT[:, slot, 0:n], ps[slot][:, 0:n]).then_inc(chunkT_kept, 1)

            with dve.Fori(0, NCH // 2) as i:
                for slot in range(2):
                    keep_chunk(2 * i + slot, slot, BANK)
            keep_chunk(NCH, 0, CR)

            for j in range(2):
                dve.wait_ge(xn_turned, j + 1)
                dve.tensor_copy(xnT[:, j * BANK:(j + 1) * BANK], ps[6 + j][:, :]).then_inc(xnT_kept, 1)
            for j in range(2):
                dve.wait_ge(q1_ready, j + 1)
                dve.tensor_scalar(q1T[:, j * BANK:(j + 1) * BANK], ps[6 + j][:, :], bias[:, 0:1], None,
                                  ALU.add).then_inc(q1_kept, 1)
            for j in range(2):
                dve.wait_ge(q_ready, j + 1)
                dve.tensor_scalar(qT[:, j * BANK:(j + 1) * BANK], ps[6 + j][:, :], bias[:, 1:2], SCALE,
                                  ALU.add, ALU.mult).then_inc(q_kept, 1)
            dve.wait_ge(q_kept, 2)
            for t in range(2):
                dve.tensor_copy(q_tile[:, t, :], qT[:, t * P:(t + 1) * P]).then_inc(q_tile_ready, 1)

            def mask(t, slot):
                dve.wait_ge(mask_in[slot], 16 * mask_no(t, slot))
                for c in range(NCH + 1):
                    n = BANK if c < NCH else CR
                    at = slice(c * BANK, c * BANK + n)
                    wait_alone(dve, scores_ready, t * (NCH + 1) + c + 1, dve_passed)
                    dve.tensor_tensor_reduce(ms[:, slot, at], ps[c % SB][:, 0:n], ms[:, slot, at], 1.0, LOWEST,
                                             ALU.add, ALU.max, cmax[:, slot, c:c + 1]).then_inc(scores_masked, 1)
                dve.wait_ge(scores_masked, (t + 1) * (NCH + 1))
                dve.tensor_reduce(nmax[:, slot:slot + 1], cmax[:, slot, :], AX_X, ALU.max,
                                  negate=True).then_inc(max_ready, 1)

            def mask_no(t, slot):
                return t // 2 + 1 if isinstance(t, int) else mask_pass[0] + 1

            mask_pass = [None]

            def next_queries(t, slot):
                dve.wait_ge(scores_ready, (t - 1) * (NCH + 1))
                dve.tensor_copy(q_tile[:, slot, :], qT[:, bass.ds(t * P, P)]).then_inc(q_tile_ready, 1)

            def keep_probs(t, slot):
                for gi in range(NG):
                    full = sum(kt < KF for kt in GROUPS[gi])
                    dve.wait_ge(probs_turned, t * NG + gi + 1)
                    if gi >= TB:
                        dve.wait_ge(pv_done, t * NG + gi - TB + 1)
                    else:
                        dve.wait_ge(pv_done, t * NG)
                    cp = dve.tensor_copy(pT[:, gi % TB, 0:full * P], ps[SB + gi % TB][:, 0:full * P])
                    if full < len(GROUPS[gi]):
                        cp = dve.tensor_copy(pT[0:KR, gi % TB, full * P:(full + 1) * P],
                                             ps[SB + gi % TB][0:KR, full * P:(full + 1) * P])
                    cp.then_inc(pT_kept, 1)
                dve.wait_ge(pv_done, (t + 1) * NG)
                dve.tensor_copy(oT[:, slot, :], ps[6 + slot][:, 0:P]).then_inc(oT_kept, 1)
                dve.wait_ge(out_turned, t + 1)
                link(nc.vector.reciprocal(rtotal[:, slot:slot + 1], total[:, slot:slot + 1]))
                xt = x[:, bass.ds(t, 1), :].rearrange("p t d -> p (t d)")
                dve.scalar_tensor_tensor(out=xt, in0=ps[6 + slot][:, 0:P], scalar=rtotal[:, slot:slot + 1],
                                         in1=xt, op0=ALU.mult, op1=ALU.add).then_inc(x_done, 1)

            mask(0, 0)
            mask(1, 1)
            for t in range(2):
                next_queries(t + 2, t)
                keep_probs(t, t)
                mask(t + 2, t)
            with dve.Fori(1, ST // 2 - 1) as i:
                link.enter(i - 1, 2)
                mask_pass[0] = i + 1
                for slot in range(2):
                    next_queries(2 * i + slot + 2, slot)
                    keep_probs(2 * i + slot, slot)
                    mask(2 * i + slot + 2, slot)
                link.leave(ST // 2 - 2)
            for slot in range(2):
                keep_probs(ST - 2 + slot, slot)

        @block.scalar
        def _(act):
            act.sem_inc(h_kept, FREE)
            act.sem_inc(k_kept, FREE)
            act.wait_ge(var_ready, 1)
            nc.scalar.activation(rstd[:, :], rstd[:, :], ACT.Sqrt).then_inc(std_ready, 1)

            def keep(c, slot, n):
                act.wait_ge(h_ready, c + 1 + FREE)
                act.wait_ge(k_ready, c - slot + FREE)
                nc.scalar.activation(hT[:, slot, 0:n], ps[2 + slot][:, 0:n], ACT.Identity,
                                     bias=bias[:, 0:1]).then_inc(h_kept, 1)

            def keep_k(c, slot, n):
                act.wait_ge(k_ready, c + 1 + FREE)
                nc.scalar.activation(kT[:, bass.ds(c * BANK, n)], ps[4 + slot][:, 0:n], ACT.Identity,
                                     bias=bias[:, 1:2]).then_inc(k_kept, 1)

            with act.Fori(0, NCH // 2) as i:
                for slot in range(2):
                    keep(2 * i + slot, slot, BANK)
                for slot in range(2):
                    keep_k(2 * i + slot, slot, BANK)
            keep(NCH, 0, CR)
            keep_k(NCH, 0, CR)

            def exps(t, slot, first=False):
                act.wait_ge(max_ready, t + 1)
                if not first:
                    act.wait_ge(probs_turned, (t - 1) * NG)
                    act.wait_ge(x_done, t - 1)
                nc.scalar.activation(pr[:, slot, :], ms[:, slot, :], ACT.Exp, bias=nmax[:, slot:slot + 1],
                                     accum_out=total[:, slot:slot + 1]).then_inc(probs_ready, 1)

            for t in range(2):
                exps(t, t, first=True)
            with act.Fori(1, ST // 2) as i:
                for slot in range(2):
                    exps(2 * i + slot, slot)


def wait(eng, sem, value):
    if not isinstance(value, int) or value > 0:
        eng.wait_ge(sem, value)


def wait_alone(eng, sem, value, passed):
    eng.wait_ge(sem, value)
    if not isinstance(value, int):
        eng.sem_inc(passed, 1)


def moe_ffn_0(nc, g, a):
    E = 16
    EA = E + 1
    TOPK = 8
    ROUTE_SCALE = 2.826
    PARTS = 3
    with ExitStack() as ctx:
        def sb(name, shape, dt=F32):
            return ctx.enter_context(nc.sbuf_tensor(name, shape, dt))

        def sem(name):
            return ctx.enter_context(nc.semaphore(name))

        w_nat = sb("m_w", [P, 2, 3, D])
        wT = sb("m_wT", [P, 2, 3, D])
        router = sb("m_router", [E, D])
        routerT = sb("m_routerT", [P, E])
        bias = sb("m_bias", [P, E])
        xn = sb("m_xn", [P, ST, D])
        xnT = sb("m_xnT", [P, S])
        stats = sb("m_stats", [P, ST, 6])
        mv = sb("m_mv", [P, ST, 2])
        rstd = sb("m_rstd", [P, ST])
        prob = sb("m_prob", [P, ST, E])
        sel = sb("m_sel", [P, ST, E])
        top = sb("m_top", [P, ST, TOPK])
        rest = sb("m_rest", [P, ST, E])
        weight = sb("m_weight", [P, ST, EA])
        wsum = sb("m_wsum", [P, ST])
        left = sb("m_left", [P, ST, EA])
        split = sb("m_split", [P, ST, P], BF16)
        splitT = sb("m_splitT", [P, S], BF16)
        pick = sb("m_pick", [P, EA, P], BF16)
        silu = sb("m_silu", [P, 2, BANK])
        h = sb("m_h", [P, 2, BANK])
        hw = sb("m_hw", [P, 2, BANK])
        yT = sb("m_yT", [P, S])
        ps, x = g["ps"], g["x"]
        ident, identb = g["ident"], g["identb"]

        w_in = [sem(f"m_w_in{i}") for i in range(2)]
        small_in = sem("m_small_in")
        pool_made = sem("m_pool_made")
        var_ready, std_ready, xn_ready = sem("m_var"), sem("m_std"), sem("m_xn_ready")
        xn_turned, xnT_kept = sem("m_xn_turned"), sem("m_xnT_kept")
        router_turned, router_kept = sem("m_rt"), sem("m_rk")
        logits_ready, prob_ready, split_ready = sem("m_logits"), sem("m_prob_ready"), sem("m_split_ready")
        split_turned, split_kept = sem("m_split_turned"), sem("m_split_kept")
        w_turned, w_kept = sem("m_w_turned"), sem("m_w_kept")
        gate_ready, up_ready, spread_ready = sem("m_gate"), sem("m_up"), sem("m_spread")
        silu_ready, h_ready, hw_ready = sem("m_silu_ready"), sem("m_h_ready"), sem("m_hw_ready")
        down_done, y_kept, y_turned = sem("m_down"), sem("m_yk"), sem("m_yt")
        dve_step, pool_step = sem("m_dve_step"), sem("m_pool_step")

        block = ctx.enter_context(nc.Block())

        @block.sync
        def _(sp):
            def load(e, slot):
                for j, name in enumerate(("L0_ffn_w_gate", "L0_ffn_w_up", "L0_ffn_w_down")):
                    src = a[name][bass.ds(e, 1), :, :].rearrange("e p d -> (e p) d")
                    sp.dma_start(w_nat[:, slot, j, :], src).then_inc(w_in[slot], 16)

            load(0, 0)
            sp.dma_start(router[:, :], a["L0_ffn_gate_w"]).then_inc(small_in, 16)
            sp.dma_start(bias[:, :], a["L0_ffn_expert_bias"].partition_broadcast(P)).then_inc(small_in, 16)
            load(1, 1)
            with sp.Fori(1, E // 2) as i:
                for slot in range(2):
                    sp.wait_ge(w_turned, 2 * i + slot - 1)
                    load(2 * i + slot, slot)
            sp.wait_ge(w_turned, E - 1)
            for j, name in enumerate(("L0_ffn_shared_gate_w", "L0_ffn_shared_up_w", "L0_ffn_shared_down_w")):
                sp.dma_start(w_nat[:, 0, j, :], a[name]).then_inc(w_in[0], 16)

        @block.gpsimd
        def _(pool):
            link = Link(pool, pool_step)
            nc.gpsimd.memset(split[:, :, :], 0.0).then_inc(pool_made, 1)
            nc.gpsimd.memset(weight[:, :, :], 1.0).then_inc(pool_made, 1)
            link(nc.gpsimd.memset(pick[:, :, :], 0.0))
            for part in range(PARTS):
                made = nc.gpsimd.affine_select(out=pick[:, :, :], in_=pick[:, :, :],
                                               compare_op=ALU.not_equal, fill=1.0, base=-part * EA,
                                               pattern=[[-1, EA], [0, P]], channel_multiplier=1)
                if part < PARTS - 1:
                    link(made)
            made.then_inc(pool_made, 1)

        @block.tensor
        def _(pe):
            pe.wait_ge(small_in, 32)
            pe.transpose(ps[2][:, 0:E], router[:, :], ident[0:E, 0:E]).then_inc(router_turned, 1)
            pe.wait_ge(xn_ready, ST)
            for t in range(ST):
                mm = pe.transpose(ps[t // 4][:, (t % 4) * P:(t % 4 + 1) * P], xn[:, t, :], ident[:, :])
                if t % 4 == 3:
                    mm.then_inc(xn_turned, 1)
            pe.wait_ge(router_kept, 1)
            pe.wait_ge(xnT_kept, 2)
            for t in range(ST):
                mm = pe.matmul(ps[3][:, t * E:(t + 1) * E], xnT[:, t * P:(t + 1) * P], routerT[:, :],
                               start=True, stop=True)
            mm.then_inc(logits_ready, 1)

            def turn_weights(e, slot, loads):
                wait(pe, w_in[slot], 48 * loads)
                wait(pe, w_kept, e)
                for j in range(3):
                    mm = pe.transpose(ps[7][:, j * D:(j + 1) * D], w_nat[:, slot, j, :], ident[:, :])
                mm.then_inc(w_turned, 1)

            def up(e, slot, half):
                n = 2 * e + half
                tok = slice(half * BANK, (half + 1) * BANK)
                if half == 0:
                    pe.wait_ge(w_kept, e + 1)
                wait(pe, silu_ready, n - 1)
                pe.matmul(ps[2 + half][:, :], wT[:, slot, 0, :], xnT[:, tok], start=True, stop=True
                          ).then_inc(gate_ready, 1)
                wait(pe, h_ready, n - 1)
                pe.matmul(ps[4 + half][:, :], wT[:, slot, 1, :], xnT[:, tok], start=True, stop=True
                          ).then_inc(up_ready, 1)
                wait(pe, hw_ready, n)
                pe.matmul(ps[6][:, :], pick[:, bass.ds(e, 1), :].rearrange("p e m -> p (e m)"),
                          splitT[:, tok], start=True, stop=True).then_inc(spread_ready, 1)

            def down(n, slot, half, first=False, last=False):
                pe.wait_ge(hw_ready, n + 1)
                pe.matmul(ps[half][:, :], wT[:, slot, 2, :], hw[:, half, :], start=first, stop=last,
                          skip_group_check=True).then_inc(down_done, 1)

            turn_weights(0, 0, 1)
            pe.wait_ge(split_ready, 1)
            for t in range(ST):
                mm = pe.transpose(ps[6][:, :].bitcast(BF16)[:, t * P:(t + 1) * P], split[:, t, :],
                                  identb[:, :])
            mm.then_inc(split_turned, 1)
            pe.wait_ge(split_kept, 1)
            pe.wait_ge(pool_made, 3)
            pe.wait_ge(prob_ready, 1)
            up(0, 0, 0)
            turn_weights(1, 1, 1)
            up(0, 0, 1)
            down(0, 0, 0, first=True)

            def expert(e, slot, loads, first=False, last=False):
                up(e, slot, 0)
                if not last:
                    turn_weights(e + 1, 1 - slot, loads)
                down(2 * e - 1, 1 - slot, 1, first=first)
                up(e, slot, 1)
                down(2 * e, slot, 0, last=last)

            expert(1, 1, 2, first=True)
            with pe.Fori(1, E // 2) as i:
                for k in range(2):
                    expert(2 * i + k, k, i + 1 + k)
            expert(E, 0, 0, last=True)
            down(2 * E + 1, 0, 1, last=True)
            for t in range(ST):
                if t % 4 == 0:
                    pe.wait_ge(y_kept, t // 4 + 1)
                mm = pe.transpose(ps[2 + t // 4][:, (t % 4) * P:(t % 4 + 1) * P],
                                  yT[:, t * P:(t + 1) * P], ident[:, :])
                if t % 4 == 3:
                    mm.then_inc(y_turned, 1)

        @block.scalar
        def _(act):
            act.wait_ge(var_ready, 1)
            nc.scalar.activation(rstd[:, :], rstd[:, :], ACT.Sqrt).then_inc(std_ready, 1)
            act.wait_ge(logits_ready, 1)
            nc.scalar.activation(prob[:, :, :], ps[3][:, 0:ST * E].rearrange("p (t e) -> p t e", e=E),
                                 ACT.Sigmoid).then_inc(prob_ready, 1)

            def keep_weights(e, slot):
                act.wait_ge(w_turned, e + 1)
                wait(act, down_done, 2 * e - 2)
                nc.scalar.activation(wT[:, slot, :, :], ps[7][:, 0:3 * D].rearrange("p (j d) -> p j d", d=D),
                                     ACT.Copy).then_inc(w_kept, 1)

            def gate(n, half):
                act.wait_ge(gate_ready, n + 1)
                wait(act, h_ready, n - 1)
                nc.scalar.activation(silu[:, half, :], ps[2 + half][:, :], ACT.Silu).then_inc(silu_ready, 1)

            keep_weights(0, 0)
            gate(0, 0)
            keep_weights(1, 1)
            gate(1, 1)
            gate(2, 0)
            keep_weights(2, 0)
            gate(3, 1)
            with act.Fori(1, E // 2) as i:
                for k in range(2):
                    e = 2 * i + k
                    gate(2 * e, 0)
                    keep_weights(e + 1, 1 - k)
                    gate(2 * e + 1, 1)
            gate(2 * E, 0)
            gate(2 * E + 1, 1)

        @block.vector
        def _(dve):
            link = Link(dve, dve_step)
            dve.wait_ge(router_turned, 1)
            nc.vector.tensor_copy(routerT[:, :], ps[2][:, 0:E]).then_inc(router_kept, 1)
            layer_norm_stats(nc, link, x, stats, mv, rstd, ST, var_ready)
            dve.wait_ge(std_ready, 1)
            layer_norm_apply(nc, link, xn, x, mv, rstd, ST, xn_ready)
            for j in range(2):
                dve.wait_ge(xn_turned, j + 1)
                nc.vector.tensor_copy(xnT[:, j * BANK:(j + 1) * BANK], ps[j][:, :]).then_inc(xnT_kept, 1)

            dve.wait_ge(prob_ready, 1)
            dve.wait_ge(small_in, 32)
            link(nc.vector.tensor_tensor(sel[:, :, :], prob[:, :, :],
                                         bias[:, :].unsqueeze(1).to_broadcast([P, ST, E]), ALU.add))
            for t in range(ST):
                link(nc.vector.max(out=top[:, t, :], in_=sel[:, t, :]))
            for t in range(ST):
                link(nc.vector.match_replace(out=rest[:, t, :], in_to_replace=top[:, t, :],
                                             in_values=sel[:, t, :], imm_value=LOWEST))
            link(nc.vector.tensor_tensor(rest[:, :, :], rest[:, :, :], sel[:, :, :], ALU.not_equal))
            dve.wait_ge(pool_made, 2)
            link(nc.vector.tensor_tensor(weight[:, :, 0:E], prob[:, :, :], rest[:, :, :], ALU.mult))
            link(nc.vector.tensor_reduce(wsum[:, :], weight[:, :, 0:E], AX_X, ALU.add))
            link(nc.vector.reciprocal(wsum[:, :], wsum[:, :]))
            link(nc.vector.tensor_scalar(wsum[:, :], wsum[:, :], ROUTE_SCALE, None, ALU.mult))
            link(nc.vector.tensor_tensor(weight[:, :, 0:E], weight[:, :, 0:E],
                                         wsum[:, :].unsqueeze(2).to_broadcast([P, ST, E]), ALU.mult))
            link(nc.vector.tensor_copy(split[:, :, 0:EA], weight[:, :, :]))
            link(nc.vector.tensor_tensor(left[:, :, :], weight[:, :, :], split[:, :, 0:EA], ALU.subtract))
            link(nc.vector.tensor_copy(split[:, :, EA:2 * EA], left[:, :, :]))
            nc.vector.tensor_tensor(split[:, :, 2 * EA:3 * EA], left[:, :, :], split[:, :, EA:2 * EA],
                                    ALU.subtract).then_inc(split_ready, 1)
            dve.wait_ge(split_turned, 1)
            nc.vector.tensor_copy(splitT[:, :], ps[6][:, :].bitcast(BF16)).then_inc(split_kept, 1)

            def combine(n, half):
                dve.wait_ge(silu_ready, n + 1)
                dve.wait_ge(up_ready, n + 1)
                wait(dve, hw_ready, n - 1)
                nc.vector.tensor_tensor(h[:, half, :], silu[:, half, :], ps[4 + half][:, :], ALU.mult
                                        ).then_inc(h_ready, 1)
                dve.wait_ge(h_ready, n + 1)
                dve.wait_ge(spread_ready, n + 1)
                wait(dve, down_done, n - 1)
                nc.vector.tensor_tensor(hw[:, half, :], h[:, half, :], ps[6][:, :], ALU.mult
                                        ).then_inc(hw_ready, 1)

            for n in range(4):
                combine(n, n % 2)
            with dve.Fori(1, E // 2) as i:
                for k in range(4):
                    combine(4 * i + k, k % 2)
            for n in range(2 * E, 2 * EA):
                combine(n, n % 2)
            for j in range(2):
                dve.wait_ge(down_done, 2 * E + 1 + j)
                nc.vector.tensor_copy(yT[:, j * BANK:(j + 1) * BANK], ps[j][:, :]).then_inc(y_kept, 1)
            for j in range(2):
                dve.wait_ge(y_turned, j + 1)
                half = x[:, 4 * j:4 * j + 4, :]
                link(nc.vector.tensor_tensor(half, ps[2 + j][:, :].rearrange("p (t d) -> p t d", d=D),
                                             half, ALU.add))


HEADS = 16
HD = D // HEADS
PAIRS = HEADS // 2
SLOT = P // 2
PARTS = 3
K_PARTS = [(0, 0, 3), (1, 3, 2), (2, 5, 1)]
Q_PARTS = [(0, (0, 3, 5)), (1, (1, 4)), (2, (2,))]
MAX_ROW = 6 * HD


def head_rows(tile, blocks, count=1):
    return tile[:, :, blocks * HD:(blocks + count) * HD]


def project_keys(nc, g, a):
    GT = BANK // P
    with ExitStack() as ctx:
        def sb(name, shape, dt=F32):
            return ctx.enter_context(nc.sbuf_tensor(name, shape, dt))

        def sem(name):
            return ctx.enter_context(nc.semaphore(name))

        chunk = sb("p_chunk", [P, 2, GT, D])
        chunkT = sb("p_chunkT", [P, 2, BANK])
        kf = sb("p_kf", [P, 2, GT * HEADS, HD])
        left = sb("p_left", [P, 2, GT * HEADS, HD])
        kn = [sb(f"p_kn{i}", [P, GT * HEADS, SLOT], BF16) for i in range(2)]
        w_nat = sb("p_w", [P, 3, D])
        wT = sb("p_wT", [P, 3, D])
        bias = sb("p_bias", [P, 3, D])
        xn = sb("p_xn", [P, ST, D])
        xnT = sb("p_xnT", [P, S])
        qf = sb("p_qf", [P, ST * HEADS, HD])
        qleft = sb("p_qleft", [P, ST * HEADS, HD])
        stats = sb("p_stats", [P, ST, 6])
        mv = sb("p_mv", [P, ST, 2])
        rstd = sb("p_rstd", [P, ST])
        ps, x, kT, vn, qn = g["ps"], g["x"], g["kT"], g["vn"], g["qn"]
        ident, identb = g["ident"], g["identb"]

        small_in = sem("p_small_in")
        chunk_in = [sem(f"p_chunk_in{i}") for i in range(2)]
        var_ready, std_ready, xn_ready = sem("p_var"), sem("p_std"), sem("p_xn_ready")
        w_turned, w_kept = sem("p_w_turned"), sem("p_w_kept")
        xn_turned, xnT_kept = sem("p_xn_turned"), sem("p_xnT_kept")
        q_ready, q_kept = sem("p_q_ready"), sem("p_q_kept")
        made = sem("p_made")
        chunk_turned, chunkT_kept = sem("p_ct"), sem("p_ck")
        kv_ready, k_kept, v_kept = sem("p_kv"), sem("p_k_kept"), sem("p_v_kept")
        part0, left_ready, part1, part2 = sem("p_part0"), sem("p_left_ready"), sem("p_part1"), sem("p_part2")
        keys_turned = sem("p_keys_turned")
        kT_kept = [sem("p_kT_kept_act"), sem("p_kT_kept_dve")]
        dve_step = sem("p_dve_step")

        block = ctx.enter_context(nc.Block())
        CHUNKS = NCH + 1
        LAST_TILES = KT - GT * NCH

        @block.sync
        def _(sp):
            ctx_rows = a["ctx_1024"][0]

            def load_chunk(c, slot):
                sp.dma_start(chunk[:, slot, :, :],
                             ctx_rows[bass.ds(c * BANK, BANK), :].rearrange("(n p) d -> p n d", p=P)
                             ).then_inc(chunk_in[slot], 16)

            for j, name in enumerate(("q", "k", "v")):
                sp.dma_start(w_nat[:, j, :], a[f"L1_xattn_W{name}"]).then_inc(small_in, 16)
                sp.dma_start(bias[:, j, :], a[f"L1_xattn_b{name}"].partition_broadcast(P)).then_inc(small_in, 16)
            for c in range(2):
                load_chunk(c, c)
            with sp.Fori(1, NCH // 2) as i:
                for slot in range(2):
                    sp.wait_ge(chunk_turned, 2 * i + slot - 1)
                    load_chunk(2 * i + slot, slot)
            sp.wait_ge(chunk_turned, NCH - 1)
            sp.dma_start(chunk[:, 0, 0:LAST_TILES - 1, :],
                         ctx_rows[NCH * BANK:KF * P, :].rearrange("(n p) d -> p n d", p=P)
                         ).then_inc(chunk_in[0], 16)
            sp.dma_start(chunk[0:KR, 0, LAST_TILES - 1, :], ctx_rows[KF * P:NK, :]).then_inc(chunk_in[0], 16)

        @block.gpsimd
        def _(pool):
            for i in range(2):
                nc.gpsimd.memset(kn[i][:, :, MAX_ROW:MAX_ROW + PARTS], 1.0).then_inc(made, 1)
                nc.gpsimd.memset(kn[i][:, :, MAX_ROW + PARTS:SLOT], 0.0).then_inc(made, 1)
            nc.gpsimd.memset(qn[:, :, MAX_ROW:SLOT], 0.0).then_inc(made, 1)
            nc.gpsimd.memset(vn[:, :, :, HD:HD + 1], 1.0).then_inc(made, 1)

        @block.tensor
        def _(pe):
            pe.sem_inc(keys_turned, 1)
            pe.wait_ge(small_in, 96)
            for j in range(3):
                mm = pe.transpose(ps[7][:, j * D:(j + 1) * D], w_nat[:, j, :], ident[:, :])
            mm.then_inc(w_turned, 1)
            pe.wait_ge(xn_ready, ST)
            for t in range(ST):
                mm = pe.transpose(ps[4 + t // 4][:, (t % 4) * P:(t % 4 + 1) * P], xn[:, t, :], ident[:, :])
                if t % 4 == 3:
                    mm.then_inc(xn_turned, 1)
            pe.wait_ge(w_kept, 1)
            pe.wait_ge(xnT_kept, 2)
            for t in range(ST):
                mm = pe.matmul(ps[6 + t // 4][:, (t % 4) * D:(t % 4 + 1) * D], xnT[:, t * P:(t + 1) * P],
                               wT[:, 0, :], start=True, stop=True)
                if t % 4 == 3:
                    mm.then_inc(q_ready, 1)

            def turn_chunk(c, slot, tiles):
                wait(pe, chunkT_kept, c - slot)
                for j, rows in enumerate(tiles):
                    mm = pe.transpose(ps[slot][:, j * P:j * P + rows], chunk[0:rows, slot, j, :],
                                      ident[0:rows, 0:rows])
                mm.then_inc(chunk_turned, 1)

            def project(c, slot, tiles):
                pe.wait_ge(chunkT_kept, c + 1)
                wait(pe, k_kept, c)
                wait(pe, v_kept, c)
                for j, rows in enumerate(tiles):
                    mm = pe.matmul(ps[2 + j // 2][0:rows, (j % 2) * 2 * D:(j % 2 + 1) * 2 * D],
                                   chunkT[:, slot, j * P:j * P + rows], wT[:, 1:3, :], start=True, stop=True)
                mm.then_inc(kv_ready, 1)

            def turn_keys(c, slot, tiles):
                pe.wait_ge(part2, c + 1 + 1)
                pe.wait_ge(part1, c + 1 + 1)
                for b in range(PAIRS // 2):
                    wait(pe, kT_kept[b % 2], 2 * c + b // 2 - 1)
                    for i in range(2):
                        for j, rows in enumerate(tiles):
                            pair = 2 * b + i
                            h0 = j * HEADS + 2 * pair
                            mm = pe.transpose(
                                ps[4 + b][:, :].bitcast(BF16)[:, i * BANK + j * P:i * BANK + j * P + rows],
                                kn[slot][0:rows, h0:h0 + 2, :].rearrange("p h r -> p (h r)"),
                                identb[0:rows, 0:rows])
                    mm.then_inc(keys_turned, 1)

            pe.wait_ge(q_kept, 2)
            full = [P] * GT
            last = [P] * (LAST_TILES - 1) + [KR]
            pe.wait_ge(chunk_in[0], 16)
            turn_chunk(0, 0, full)
            project(0, 0, full)
            pe.wait_ge(chunk_in[1], 16)
            turn_chunk(1, 1, full)

            def chunks(i):
                for slot in range(2):
                    c = 2 * i + slot
                    project(c + 1, 1 - slot, full)
                    pe.wait_ge(chunk_in[slot], 16 * i + 32)
                    turn_chunk(c + 2, slot, full)
                    turn_keys(c, slot, full)

            chunks(0)
            with pe.Fori(1, NCH // 2 - 1) as i:
                chunks(i)
            c = NCH - 2
            project(c + 1, 1, full)
            pe.wait_ge(chunk_in[0], 16 * (NCH // 2) + 32)
            turn_chunk(NCH, 0, last)
            turn_keys(c, 0, full)
            project(NCH, 0, last)
            turn_keys(NCH - 1, 1, full)
            turn_keys(NCH, 0, last)

        def put_rows(tiles):
            return [(0, GT, P)] if tiles == GT else [(0, tiles - 1, P), (tiles - 1, 1, KR)]

        @block.scalar
        def _(act):
            act.wait_ge(var_ready, 1)
            nc.scalar.activation(rstd[:, :], rstd[:, :], ACT.Sqrt).then_inc(std_ready, 1)
            act.sem_inc(part1, 1)
            act.wait_ge(made, 6)

            def parts(c, slot, tiles):
                act.wait_ge(k_kept, c + 1)
                wait(act, keys_turned, (PAIRS // 2) * (c - 1) + 1)
                for first, n, rows in put_rows(tiles):
                    hs = slice(first * HEADS, (first + n) * HEADS)
                    ins = nc.scalar.activation(
                        kn[slot][0:rows, hs, 0:3 * HD].rearrange("p h (r d) -> p h r d", d=HD),
                        kf[0:rows, slot, hs, :].unsqueeze(2).to_broadcast([rows, n * HEADS, 3, HD]), ACT.Copy)
                ins.then_inc(part0, 1)
                act.wait_ge(left_ready, c + 1)
                for first, n, rows in put_rows(tiles):
                    hs = slice(first * HEADS, (first + n) * HEADS)
                    ins = nc.scalar.activation(
                        kn[slot][0:rows, hs, 3 * HD:5 * HD].rearrange("p h (r d) -> p h r d", d=HD),
                        left[0:rows, slot, hs, :].unsqueeze(2).to_broadcast([rows, n * HEADS, 2, HD]), ACT.Copy)
                ins.then_inc(part1, 1)

            def keep(c, n):
                for b in (0, 2):
                    act.wait_ge(keys_turned, (PAIRS // 2) * c + b + 1 + 1)
                    nc.scalar.activation(
                        kT[:, 2 * b:2 * b + 2, bass.ds(c * BANK, n)],
                        ps[4 + b][:, :].bitcast(BF16).rearrange("p (i n) -> p i n", i=2)[:, :, 0:n],
                        ACT.Copy).then_inc(kT_kept[0], 1)

            parts(0, 0, GT)
            with act.Fori(0, NCH // 2 - 1) as i:
                for slot in range(2):
                    parts(2 * i + slot + 1, 1 - slot, GT)
                    keep(2 * i + slot, BANK)
            parts(NCH - 1, 1, GT)
            keep(NCH - 2, BANK)
            parts(NCH, 0, LAST_TILES)
            keep(NCH - 1, BANK)
            keep(NCH, CR)

        @block.vector
        def _(dve):
            link = Link(dve, dve_step)
            dve.sem_inc(part2, 1)
            dve.wait_ge(w_turned, 1)
            nc.vector.tensor_copy(wT[:, :, :], ps[7][:, 0:3 * D].rearrange("p (j d) -> p j d", d=D)
                                  ).then_inc(w_kept, 1)
            layer_norm_stats(nc, link, x, stats, mv, rstd, ST, var_ready)
            dve.wait_ge(std_ready, 1)
            layer_norm_apply(nc, link, xn, x, mv, rstd, ST, xn_ready)
            for j in range(2):
                dve.wait_ge(xn_turned, j + 1)
                nc.vector.tensor_copy(xnT[:, j * BANK:(j + 1) * BANK], ps[4 + j][:, :]).then_inc(xnT_kept, 1)
            dve.wait_ge(made, 6)
            for j in range(2):
                dve.wait_ge(q_ready, j + 1)
                half = qf[:, j * 4 * HEADS:(j + 1) * 4 * HEADS, :].rearrange("p (t h) d -> p t (h d)", t=4)
                nc.vector.tensor_tensor(half, ps[6 + j][:, :].rearrange("p (t d) -> p t d", d=D),
                                        bias[:, 0:1, :].to_broadcast([P, 4, D]), ALU.add).then_inc(q_kept, 1)
            dve.wait_ge(q_kept, 2)
            link(nc.vector.tensor_scalar(qf[:, :, :], qf[:, :, :], float(HD) ** -0.5, None, ALU.mult))

            def q_put(part, src):
                for blk in Q_PARTS[part][1]:
                    for hg in range(HEADS // 4):
                        link(nc.vector.tensor_copy(
                            qn[:, hg * ST * 4:(hg + 1) * ST * 4, blk * HD:(blk + 1) * HD]
                            .rearrange("p (t h) d -> p t h d", h=4),
                            src[:, :, :].rearrange("p (t h) d -> p t h d", h=HEADS)[:, :, 4 * hg:4 * hg + 4, :]))

            def q_left(part, src):
                blk = Q_PARTS[part][1][0]
                for hg in range(HEADS // 4):
                    link(nc.vector.tensor_tensor(
                        qleft[:, :, :].rearrange("p (t h) d -> p t h d", h=HEADS)[:, :, 4 * hg:4 * hg + 4, :],
                        src[:, :, :].rearrange("p (t h) d -> p t h d", h=HEADS)[:, :, 4 * hg:4 * hg + 4, :],
                        qn[:, hg * ST * 4:(hg + 1) * ST * 4, blk * HD:(blk + 1) * HD]
                        .rearrange("p (t h) d -> p t h d", h=4), ALU.subtract))

            q_put(0, qf)
            q_left(0, qf)
            q_put(1, qleft)
            q_left(1, qleft)
            q_put(2, qleft)

            def keep_chunk(c, slot, n):
                dve.wait_ge(chunk_turned, c + 1)
                wait(dve, kv_ready, c - slot)
                nc.vector.tensor_copy(chunkT[:, slot, 0:n], ps[slot][:, 0:n]).then_inc(chunkT_kept, 1)

            def keep_kv(c, slot, tiles):
                dve.wait_ge(kv_ready, c + 1)
                wait(dve, part2, c - 1 + 1)
                wait(dve, part1, c - 1 + 1)
                todo = []
                for first, n, rows in put_rows(tiles):
                    while n > 0:
                        m = min(n, 2 - first % 2)
                        todo.append((first, m, rows))
                        first, n = first + m, n - m
                for what in range(2):
                    for first, m, rows in todo:
                        src = ps[2 + first // 2][0:rows, (first % 2) * 2 * D:(first % 2 + m) * 2 * D].rearrange(
                            "p (j w d) -> p j w d", w=2, d=D)[:, :, what, :]
                        b = bias[0:rows, 1 + what:2 + what, :].to_broadcast([rows, m, D])
                        if what == 0:
                            dst = kf[0:rows, slot, first * HEADS:(first + m) * HEADS, :].rearrange(
                                "p (j h) d -> p j (h d)", h=HEADS)
                            ins = nc.vector.tensor_tensor(dst, src, b, ALU.add)
                        else:
                            dst = vn[0:rows, bass.ds(c * GT + first, m), :, 0:HD]
                            ins = nc.vector.tensor_tensor(
                                dst, src.rearrange("p j (h d) -> p j h d", d=HD),
                                b.rearrange("p j (h d) -> p j h d", d=HD), ALU.add)
                    ins.then_inc((k_kept, v_kept)[what], 1)

            def leave(c, slot, tiles):
                dve.wait_ge(part0, c + 1)
                for first, n, rows in put_rows(tiles):
                    hs = slice(first * HEADS, (first + n) * HEADS)
                    ins = nc.vector.tensor_tensor(left[0:rows, slot, hs, :], kf[0:rows, slot, hs, :],
                                                  kn[slot][0:rows, hs, 0:HD], ALU.subtract)
                ins.then_inc(left_ready, 1)

            def third(c, slot, tiles):
                dve.wait_ge(part1, c + 1 + 1)
                for first, n, rows in put_rows(tiles):
                    hs = slice(first * HEADS, (first + n) * HEADS)
                    ins = nc.vector.tensor_tensor(kn[slot][0:rows, hs, 5 * HD:6 * HD], left[0:rows, slot, hs, :],
                                                  kn[slot][0:rows, hs, 3 * HD:4 * HD], ALU.subtract)
                ins.then_inc(part2, 1)

            def keep(c, n):
                for b in (1, 3):
                    dve.wait_ge(keys_turned, (PAIRS // 2) * c + b + 1 + 1)
                    nc.vector.tensor_copy(
                        kT[:, 2 * b:2 * b + 2, bass.ds(c * BANK, n)],
                        ps[4 + b][:, :].bitcast(BF16).rearrange("p (i n) -> p i n", i=2)[:, :, 0:n]
                    ).then_inc(kT_kept[1], 1)

            keep_chunk(0, 0, BANK)
            keep_kv(0, 0, GT)
            keep_chunk(1, 1, BANK)
            leave(0, 0, GT)
            third(0, 0, GT)
            with dve.Fori(0, NCH // 2 - 1) as i:
                for slot in range(2):
                    c = 2 * i + slot
                    keep_kv(c + 1, 1 - slot, GT)
                    keep_chunk(c + 2, slot, BANK)
                    leave(c + 1, 1 - slot, GT)
                    third(c + 1, 1 - slot, GT)
                    keep(c, BANK)
            c = NCH - 2
            keep_kv(c + 1, 1, GT)
            keep_chunk(c + 2, 0, CR)
            leave(c + 1, 1, GT)
            third(c + 1, 1, GT)
            keep(c, BANK)
            keep_kv(NCH, 0, LAST_TILES)
            leave(NCH, 0, LAST_TILES)
            third(NCH, 0, LAST_TILES)
            keep(NCH - 1, BANK)
            keep(NCH, CR)


def cross_attention_1(nc, g, a):
    HG = 4
    QT = BANK // P
    QH = S // BANK
    ROWS = HG * QT
    PIECES = 16
    PN = -(-NK // PIECES)
    MB = 4
    STEPS = HG * KT
    SB, PB, VB = 3, 12, 3
    TILES = 3
    PER = TILES * HG
    HEAD = 2
    MAXB, SCB, ACC = 0, 4, 7
    assert PER % SB == 0 and PER % PB == 0 and TILES % VB == 0 and HEAD + ROWS * TILES + 1 == KT
    with ExitStack() as ctx:
        def sb(name, shape, dt=F32):
            return ctx.enter_context(nc.sbuf_tensor(name, shape, dt))

        def sem(name):
            return ctx.enter_context(nc.semaphore(name))

        qa = sb("x_qa", [P, HG, BANK], BF16)
        qb = sb("x_qb", [P, QH, HG, BANK], BF16)
        probs = sb("x_probs", [P, PB, BANK])
        vt = sb("x_vt", [P, VB, HG, 32])
        cmax = sb("x_cmax", [P, ROWS, PIECES])
        nmax = sb("x_nmax", [P, ROWS])
        mleft = sb("x_mleft", [P, ROWS])
        oT = sb("x_oT", [P, BANK])
        rtotal = sb("x_rtotal", [P, QT, HG])
        ps, big = g["ps"], g["big"]
        kT, vn, qn, on = g["kT"], g["vn"], g["qn"], g["on"]
        ident, identb = g["ident"], g["identb"]
        kT_flat = kT[:, :, :].rearrange("p a k -> p (a k)")
        qa_flat = qa[:, :, :].rearrange("p h q -> p (h q)")

        zeroed = sem("x_zeroed")
        qa_turned, qa_kept, qb_turned, qb_kept = sem("x_qat"), sem("x_qak"), sem("x_qbt"), sem("x_qbk")
        piece_ready, piece_maxed, max_split = sem("x_piece"), sem("x_maxed"), sem("x_max_split")
        scores_ready, probs_ready, pv_done = sem("x_scores"), sem("x_probs_ready"), sem("x_pv")
        v_ready, oT_kept, o_turned, o_done = sem("x_v"), sem("x_oT_kept"), sem("x_o_turned"), sem("x_o_done")
        dve_step = sem("x_dve_step")
        pe_passed, pool_passed = sem("x_pe_passed"), sem("x_pool_passed")

        block = ctx.enter_context(nc.Block())

        def tile_rows(kt):
            return P if kt < KF else KR

        @block.gpsimd
        def _(pool):
            nc.gpsimd.memset(vt[:, :, :, :], 0.0).then_inc(zeroed, 1)
            nc.gpsimd.memset(qa[:, :, :], 0.0).then_inc(zeroed, 1)
            nc.gpsimd.memset(qb[:, :, :, :], 0.0).then_inc(zeroed, 1)
            pool.wait_ge(zeroed, 3)

            def fetch(u, hg, kt, slot, rows=P):
                back = HG * (kt - VB + 1)
                wait_alone(pool, pv_done, u * STEPS + 1 + (max(back, 0) if isinstance(back, int) else back),
                           pool_passed)
                nc.gpsimd.tensor_copy(
                    vt[0:rows, slot, :, 0:HD + 1],
                    vn[0:rows, bass.ds(kt, 1), bass.ds(hg * HG, HG), :].rearrange("p t h d -> p (t h) d")
                ).then_inc(v_ready, 1)

            with pool.Fori(0, HEADS // HG) as hg:
                for qh in range(QH):
                    u = hg * QH + qh
                    for kt in range(VB):
                        fetch(u, hg, kt, kt)
                    with pool.Fori(1, KT // VB - 1) as i:
                        for j in range(VB):
                            fetch(u, hg, VB * i + j, j)
                    for kt in range(KT - VB, KT):
                        fetch(u, hg, kt, kt % VB, tile_rows(kt))

        @block.tensor
        def _(pe):
            pe.sem_inc(pv_done, 1)

            def turn_queries(u, bank, done):
                for pair in range(HG // 2):
                    for t in range(QT):
                        at = (u * QT + t) * HG + 2 * pair
                        mm = pe.transpose(
                            ps[bank][:, :].bitcast(BF16)[:, (pair * QT + t) * P:(pair * QT + t + 1) * P],
                            qn[:, bass.ds(at, 2), :].rearrange("p h r -> p (h r)"), identb[:, :])
                mm.then_inc(done, 1)

            def piece(u, hg, half, r, j):
                row = half * (ROWS // 2) + r
                pe.wait_ge(piece_maxed, (u * ROWS + row) * PIECES + j + 1)
                pe.matmul(ps[MAXB + j % MB][:, 0:PN], qa_flat[:, bass.ds(row * P, P)],
                          kT_flat[:, bass.ds((hg * 2 + half) * NK + min(j * PN, NK - PN), PN)],
                          start=True, stop=True).then_inc(piece_ready, 1)

            def score(u, qh, hg, n, kt, s, rows=P):
                h = s % HG
                back = n - SB + 1
                value = u * STEPS + 1 + (max(back, 0) if isinstance(back, int) else back)
                if rows < P:
                    wait_alone(pe, probs_ready, value, pe_passed)
                else:
                    pe.wait_ge(probs_ready, value)
                pe.matmul(ps[SCB + s % SB][0:rows, :],
                          kT_flat[:, bass.ds((hg * 2 + h // 2) * NK + kt * P, rows)],
                          qb[:, qh, h, :], start=True, stop=True).then_inc(scores_ready, 1)

            def weigh(u, kt, s, rows=P):
                if isinstance(kt, int) and kt == 0:
                    wait_alone(pe, o_done, u + 1, pe_passed)
                for h in range(HG):
                    pe.matmul(ps[ACC][32 * h:32 * h + 32, :], vt[0:rows, s % VB, h, :],
                              probs[0:rows, (s * HG + h) % PB, :], start=isinstance(kt, int) and kt == 0,
                              stop=isinstance(kt, int) and kt == KT - 1,
                              skip_group_check=True).then_inc(pv_done, 1)

            def unit(u, qh, hg, next_u=None, next_hg=None, after=None):
                pe.wait_ge(qb_kept, 2 * u + 2)
                for kt in range(HEAD):
                    for h in range(HG):
                        score(u, qh, hg, kt * HG + h, kt, kt * HG + h)
                    if kt > 0:
                        weigh(u, kt - 1, kt - 1)
                if next_u is not None:
                    wait_alone(pe, qa_kept, 2 * next_u + 2, pe_passed)
                with pe.Fori(0, 2) as half:
                    with pe.Fori(0, ROWS // 2) as r:
                        i = half * (ROWS // 2) + r
                        pieces = 0
                        for k in range(TILES):
                            s = HEAD + k
                            for h in range(HG):
                                score(u, qh, hg, i * PER + s * HG + h, i * TILES + s, s * HG + h)
                                while next_u is not None and (k * HG + h + 1) * PIECES > pieces * PER:
                                    piece(next_u, next_hg, half, r, pieces)
                                    pieces += 1
                            weigh(u, i * TILES + s - 1, s - 1)
                for h in range(HG):
                    score(u, qh, hg, (KT - 1) * HG + h, KT - 1, (KT - 1) * HG + h, KR)
                weigh(u, KT - 2, KT - 2)
                if next_u is not None:
                    wait_alone(pe, max_split, next_u + 1, pe_passed)
                    turn_queries(next_u, MAXB, qb_turned)
                if after is not None:
                    turn_queries(after, MAXB + 2, qa_turned)
                wait_alone(pe, probs_ready, (u + 1) * STEPS + 1, pe_passed)
                weigh(u, KT - 1, KT - 1, KR)
                pe.wait_ge(oT_kept, u + 1)
                for t in range(QT):
                    mm = pe.transpose(ps[ACC][:, t * P:(t + 1) * P], oT[:, t * P:(t + 1) * P], ident[:, :])
                mm.then_inc(o_turned, 1)

            turn_queries(0, MAXB, qa_turned)
            pe.wait_ge(qa_kept, 2)
            with pe.Fori(0, 2) as half:
                with pe.Fori(0, ROWS // 2) as r:
                    for j in range(PIECES):
                        piece(0, 0, half, r, j)
            pe.wait_ge(max_split, 1)
            turn_queries(0, MAXB, qb_turned)
            turn_queries(1, MAXB + 2, qa_turned)
            G = HEADS // HG
            with pe.Fori(0, G - 1) as hg:
                unit(hg * QH, 0, hg, hg * QH + 1, hg, hg * QH + 2)
                unit(hg * QH + 1, 1, hg, hg * QH + 2, hg + 1, hg * QH + 3)
            unit((G - 1) * QH, 0, G - 1, (G - 1) * QH + 1, G - 1)
            unit((G - 1) * QH + 1, 1, G - 1)

        def padded(q, half):
            return q[SLOT * half:SLOT * half + SLOT, half:HG:2, :]

        def turned(bank, half):
            return ps[bank][SLOT * half:SLOT * half + SLOT, :].bitcast(BF16).rearrange(
                "p (a q) -> p a q", a=HG // 2)

        @block.scalar
        def _(act):
            def keep_queries(u, qh, q, bank, done, kept):
                act.wait_ge(done, u + 1)
                nc.scalar.activation(padded(q, 1), turned(bank, 1), ACT.Copy).then_inc(kept, 1)

            def exp(u, n, s, rows=P):
                act.wait_ge(scores_ready, u * STEPS + n + 1)
                if s % HG == 0:
                    back = n + HG - PB
                    act.wait_ge(pv_done, u * STEPS + 1 + (max(back, 0) if isinstance(back, int) else back))
                if s % HG == 1:
                    act.wait_ge(v_ready, u * KT + (n - 1) // HG + 1 if isinstance(n, int) else
                                u * KT + v_at[0] + s // HG + 1)
                nc.scalar.activation(probs[0:rows, s % PB, :], ps[SCB + s % SB][0:rows, :], ACT.Exp
                                     ).then_inc(probs_ready, 1)

            v_at = [None]

            def unit(u, nxt=True, after=True):
                for n in range(PER):
                    exp(u, n, n)
                with act.Fori(1, STEPS // PER - 1) as i:
                    v_at[0] = i * TILES
                    for s in range(PER):
                        exp(u, i * PER + s, s)
                for n in range(STEPS - PER, STEPS):
                    exp(u, n, n, tile_rows(n // HG))

            act.sem_inc(probs_ready, 1)
            act.wait_ge(zeroed, 3)
            keep_queries(0, 0, qa, MAXB, qa_turned, qa_kept)
            keep_queries(0, 0, qb[:, 0], MAXB, qb_turned, qb_kept)
            keep_queries(1, 1, qa, MAXB + 2, qa_turned, qa_kept)
            G = HEADS // HG

            def between(u, qh, last=False):
                keep_queries(u + 1, 1 - qh, qb[:, 1 - qh], MAXB, qb_turned, qb_kept)
                if not last:
                    keep_queries(u + 2, qh, qa, MAXB + 2, qa_turned, qa_kept)

            with act.Fori(0, G - 1) as hg:
                for qh in range(QH):
                    unit(hg * QH + qh)
                    between(hg * QH + qh, qh)
            unit((G - 1) * QH)
            between((G - 1) * QH, 0, last=True)
            unit((G - 1) * QH + 1)

        @block.vector
        def _(dve):
            link = Link(dve, dve_step)

            def keep_queries(u, q, bank, done, kept):
                dve.wait_ge(done, u + 1)
                nc.vector.tensor_copy(padded(q, 0), turned(bank, 0)).then_inc(kept, 1)

            def maxima(u):
                with dve.Fori(0, ROWS) as row:
                    for j in range(PIECES):
                        dve.wait_ge(piece_ready, (u * ROWS + row) * PIECES + j + 1)
                        nc.vector.tensor_reduce(
                            cmax[:, bass.ds(row, 1), j:j + 1].rearrange("p r j -> p (r j)"),
                            ps[MAXB + j % MB][:, 0:PN], AX_X, ALU.max).then_inc(piece_maxed, 1)
                dve.wait_ge(piece_maxed, (u + 1) * ROWS * PIECES + MB)
                link(nc.vector.tensor_reduce(nmax[:, :], cmax[:, :, :], AX_X, ALU.max, negate=True))

                def row_of(part):
                    return qn[:, bass.ds(u * ROWS, ROWS), MAX_ROW + part:MAX_ROW + part + 1].rearrange(
                        "p (t h) o -> p h (t o)", h=HG)

                def by_head(v):
                    return v[:, :].rearrange("p (h t) -> p h t", h=HG)

                link(nc.vector.tensor_copy(row_of(0), by_head(nmax)))
                link(nc.vector.tensor_tensor(by_head(mleft), by_head(nmax), row_of(0), ALU.subtract))
                link(nc.vector.tensor_copy(row_of(1), by_head(mleft)))
                nc.vector.tensor_tensor(row_of(2), by_head(mleft), row_of(1), ALU.subtract
                                        ).then_inc(max_split, 1)

            def outputs(u, qh, hg):
                dve.wait_ge(pv_done, (u + 1) * STEPS + 1)
                nc.vector.tensor_copy(oT[:, :], ps[ACC][:, :]).then_inc(oT_kept, 1)
                dve.wait_ge(o_turned, u + 1)
                o = ps[ACC][:, :].rearrange("p (t h r) -> p t h r", t=QT, h=HG)
                link(nc.vector.reciprocal(rtotal[:, :, :], o[:, :, :, HD:HD + 1].rearrange("p t h o -> p t (h o)")))
                nc.vector.tensor_tensor(
                    on[:, qh * QT:(qh + 1) * QT, bass.ds(hg * HG, HG), :], o[:, :, :, 0:HD],
                    rtotal[:, :, :].unsqueeze(3).to_broadcast([P, QT, HG, HD]), ALU.mult).then_inc(o_done, 1)

            dve.sem_inc(piece_maxed, MB)
            dve.sem_inc(o_done, 1)
            dve.wait_ge(zeroed, 3)
            keep_queries(0, qa, MAXB, qa_turned, qa_kept)
            maxima(0)
            keep_queries(0, qb[:, 0], MAXB, qb_turned, qb_kept)
            keep_queries(1, qa, MAXB + 2, qa_turned, qa_kept)
            G = HEADS // HG

            def unit(u, qh, hg, last=False):
                maxima(u + 1)
                keep_queries(u + 1, qb[:, 1 - qh], MAXB, qb_turned, qb_kept)
                outputs(u, qh, hg)
                if not last:
                    keep_queries(u + 2, qa, MAXB + 2, qa_turned, qa_kept)

            PER_UNIT = 5
            with dve.Fori(0, G - 1) as hg:
                link.enter(hg, QH * PER_UNIT)
                for qh in range(QH):
                    unit(hg * QH + qh, qh, hg)
            link.leave(G - 1)
            unit((G - 1) * QH, 0, G - 1, last=True)
            outputs((G - 1) * QH + 1, 1, G - 1)


def moe_by_argmax(nc, g, a, out):
    PATHS, DM = 9, D // 4
    LOADS = 14
    HW = PATHS * DM
    KC = [(0, P), (P, P), (2 * P, HW + PATHS - 2 * P)]
    with ExitStack() as ctx:
        def sb(name, shape, dt=F32):
            return ctx.enter_context(nc.sbuf_tensor(name, shape, dt))

        def sem(name):
            return ctx.enter_context(nc.semaphore(name))

        wo_nat = sb("f_wo", [P, D])
        woT = sb("f_woT", [P, D])
        bo = sb("f_bo", [P, 1, D])
        onT = sb("f_onT", [P, S])
        y = sb("f_y", [P, ST, D])
        yT = sb("f_yT", [P, S + 2])
        mixw = sb("f_mixw", [P, 3])
        mixT = sb("f_mixT", [P, S])
        w1 = sb("f_w1", [P, HW + DM])
        b1 = sb("f_b1", [P, HW + DM])
        w2 = sb("f_w2", [P, 3, D])
        wo2 = sb("f_wo2", [DM, PATHS])
        bo2 = sb("f_bo2", [P, 1, PATHS])
        gb = sb("f_gb", [P, 2, D])
        hid = sb("f_hid", [P, ST, HW + DM])
        tanhT = sb("f_tanhT", [DM, S])
        score = sb("f_score", [P, ST, PATHS])
        top = sb("f_top", [P, ST, 8])
        top_at = sb("f_top_at", [P, ST, 8], U32)
        best = sb("f_best", [P, ST])
        iota = sb("f_iota", [P, PATHS])
        kept = sb("f_kept", [P, ST, HW + PATHS])
        keptT = sb("f_keptT", [P, 2, 3, P])
        z = sb("f_z", [P, ST, D])
        stats = sb("f_stats", [P, ST, 6])
        mv = sb("f_mv", [P, ST, 2])
        rstd = sb("f_rstd", [P, ST])
        ps, x, on, ident = g["ps"], g["x"], g["on"], g["ident"]

        small_in, made = sem("f_small_in"), sem("f_made")
        wo_turned, wo_kept, on_turned, onT_kept = sem("f_wt"), sem("f_wk"), sem("f_ot"), sem("f_ok")
        attn_ready = sem("f_attn")
        var_ready, std_ready, y_ready = sem("f_var"), sem("f_std"), sem("f_y_ready")
        y_turned, yT_kept, mix_ready = sem("f_yt"), sem("f_yk"), sem("f_mix")
        hid_ready, hid_kept, tanh_ready = sem("f_hid_ready"), sem("f_hid_kept"), sem("f_tanh")
        tanh_turned, tanhT_kept, score_ready = sem("f_tt"), sem("f_tk"), sem("f_score_ready")
        chosen, kept_turned, keptT_kept = sem("f_chosen"), sem("f_kt"), sem("f_kk")
        path_done, var2_ready, std2_ready = sem("f_path"), sem("f_var2"), sem("f_std2")
        normed, out_ready, out_done = sem("f_normed"), sem("f_out_ready"), sem("f_out_done")
        dve_step = sem("f_dve_step")

        block = ctx.enter_context(nc.Block())

        @block.sync
        def _(sp):
            loads = [
                (wo_nat[:, :], a["L1_xattn_Wo"]),
                (bo[:, 0, :], a["L1_xattn_bo"].partition_broadcast(P)),
                (mixw[:, :], a["L1_ffn_mix_kernel"].rearrange("j d -> d j")),
                (w1[:, 0:HW].rearrange("d (p m) -> d p m", p=PATHS), a["L1_ffn_W1"].rearrange("p d m -> d p m")),
                (w1[:, HW:HW + DM], a["L1_ffn_Wo1"]),
                (b1[:, 0:HW], a["L1_ffn_b1"].rearrange("p m -> (p m)").partition_broadcast(P)),
                (b1[:, HW:HW + DM], a["L1_ffn_bo1"].partition_broadcast(P)),
                (w2[:, 0:2, :], a["L1_ffn_W2"].rearrange("p m d -> (p m) d")[0:2 * P, :].rearrange(
                    "(c k) d -> k c d", k=P)),
                (w2[0:HW - 2 * P, 2, :], a["L1_ffn_W2"].rearrange("p m d -> (p m) d")[2 * P:HW, :]),
                (w2[HW - 2 * P:HW - 2 * P + PATHS, 2, :], a["L1_ffn_b2"]),
                (wo2[:, :], a["L1_ffn_Wo2"]),
                (bo2[:, 0, :], a["L1_ffn_bo2"].partition_broadcast(P)),
                (gb[:, 0, :], a["L1_ffn_gamma"].partition_broadcast(P)),
                (gb[:, 1, :], a["L1_ffn_beta"].partition_broadcast(P)),
            ]
            assert len(loads) == LOADS
            with nc.allow_non_contiguous_dma(reason="small weights"):
                for dst, src in loads:
                    sp.dma_start(dst, src).then_inc(small_in, 16)
            out_v = out.rearrange("b (t p) d -> p (b t) d", p=P)
            for j in range(2):
                sp.wait_ge(out_ready, j + 1)
                sp.dma_start(out_v[:, 4 * j:4 * j + 4, :], z[:, 4 * j:4 * j + 4, :]).then_inc(out_done, 16)
            sp.wait_ge(out_done, 32)

        @block.gpsimd
        def _(pool):
            nc.gpsimd.memset(yT[:, 0:1], 0.0).then_inc(made, 1)
            nc.gpsimd.memset(yT[:, S + 1:S + 2], 0.0).then_inc(made, 1)
            nc.gpsimd.iota(iota[:, :], pattern=[[1, PATHS]], base=0, channel_multiplier=0,
                           allow_small_or_imprecise_dtypes=True).then_inc(made, 1)

        @block.tensor
        def _(pe):
            pe.wait_ge(small_in, 16 * LOADS)
            pe.transpose(ps[2][:, 0:D], wo_nat[:, :], ident[:, :]).then_inc(wo_turned, 1)
            for t in range(ST):
                mm = pe.transpose(ps[t // 4][:, (t % 4) * P:(t % 4 + 1) * P],
                                  on[:, t, :, :].rearrange("p h d -> p (h d)"), ident[:, :])
                if t % 4 == 3:
                    mm.then_inc(on_turned, 1)
            pe.wait_ge(wo_kept, 1)
            for t in range(ST):
                if t % 4 == 0:
                    pe.wait_ge(onT_kept, t // 4 + 1)
                mm = pe.matmul(ps[4 + t // 4][:, (t % 4) * D:(t % 4 + 1) * D], onT[:, t * P:(t + 1) * P],
                               woT[:, :], start=True, stop=True)
                if t % 4 == 3:
                    mm.then_inc(attn_ready, 1)
            pe.wait_ge(y_ready, ST)
            for t in range(ST):
                mm = pe.transpose(ps[t // 4][:, (t % 4) * P:(t % 4 + 1) * P], y[:, t, :], ident[:, :])
                if t % 4 == 3:
                    mm.then_inc(y_turned, 1)
            pe.wait_ge(mix_ready, 1)
            for t in range(ST):
                if t >= 4:
                    pe.wait_ge(hid_kept, t - 3)
                pe.matmul(ps[t % 4][:, 0:HW + DM], mixT[:, t * P:(t + 1) * P], w1[:, :], start=True,
                          stop=True).then_inc(hid_ready, 1)
            for t in range(ST):
                pe.wait_ge(tanh_ready, t + 1)
                mm = pe.transpose(ps[4 + t // 4][0:DM, (t % 4) * P:(t % 4 + 1) * P], hid[:, t, HW:HW + DM],
                                  ident[:, :])
                if t % 4 == 3:
                    mm.then_inc(tanh_turned, 1)
            for t in range(ST):
                if t % 4 == 0:
                    pe.wait_ge(tanhT_kept, t // 4 + 1)
                mm = pe.matmul(ps[6][:, t * PATHS:(t + 1) * PATHS], tanhT[:, t * P:(t + 1) * P], wo2[:, :],
                               start=True, stop=True)
            mm.then_inc(score_ready, 1)

            def turn_kept(t):
                pe.wait_ge(chosen, t + 1)
                wait(pe, keptT_kept, t - 1)
                for c, (k0, k) in enumerate(KC):
                    mm = pe.transpose(ps[t % 2][0:k, c * P:(c + 1) * P], kept[:, t, k0:k0 + k], ident[:, :])
                mm.then_inc(kept_turned, 1)

            turn_kept(0)
            for t in range(ST):
                if t + 1 < ST:
                    turn_kept(t + 1)
                pe.wait_ge(keptT_kept, t + 1)
                for c, (k0, k) in enumerate(KC):
                    mm = pe.matmul(ps[4 + t // 4][:, (t % 4) * D:(t % 4 + 1) * D], keptT[0:k, t % 2, c, :],
                                   w2[0:k, c, :], start=(c == 0), stop=(c == 2))
                mm.then_inc(path_done, 1)

        @block.scalar
        def _(act):
            act.wait_ge(var_ready, 1)
            nc.scalar.activation(rstd[:, :], rstd[:, :], ACT.Sqrt).then_inc(std_ready, 1)
            for t in range(ST):
                act.wait_ge(hid_kept, t + 1)
                nc.scalar.activation(hid[:, t, HW:HW + DM], hid[:, t, HW:HW + DM], ACT.Tanh
                                     ).then_inc(tanh_ready, 1)
            for t in range(ST):
                act.wait_ge(kept_turned, t + 1)
                wait(act, path_done, t - 1)
                nc.scalar.activation(keptT[:, t % 2, 0:2, :], ps[t % 2][:, 0:2 * P].rearrange(
                    "p (c q) -> p c q", c=2), ACT.Copy)
                k = KC[2][1]
                nc.scalar.activation(keptT[0:k, t % 2, 2, :], ps[t % 2][0:k, 2 * P:3 * P], ACT.Copy
                                     ).then_inc(keptT_kept, 1)
            act.wait_ge(var2_ready, 1)
            nc.scalar.activation(rstd[:, :], rstd[:, :], ACT.Sqrt).then_inc(std2_ready, 1)

        @block.vector
        def _(dve):
            link = Link(dve, dve_step)

            def tiles_of(bank):
                return ps[bank][:, :].rearrange("p (t d) -> p t d", d=D)

            dve.wait_ge(wo_turned, 1)
            nc.vector.tensor_copy(woT[:, :], ps[2][:, 0:D]).then_inc(wo_kept, 1)
            for j in range(2):
                dve.wait_ge(on_turned, j + 1)
                nc.vector.tensor_copy(onT[:, j * BANK:(j + 1) * BANK], ps[j][:, :]).then_inc(onT_kept, 1)
            dve.wait_ge(small_in, 16 * LOADS)
            link(nc.vector.tensor_tensor(x[:, :, :], x[:, :, :], bo[:, :, :].to_broadcast([P, ST, D]), ALU.add))
            for j in range(2):
                dve.wait_ge(attn_ready, j + 1)
                half = x[:, 4 * j:4 * j + 4, :]
                link(nc.vector.tensor_tensor(half, tiles_of(4 + j), half, ALU.add))
            layer_norm_stats(nc, link, x, stats, mv, rstd, ST, var_ready)
            dve.wait_ge(std_ready, 1)
            layer_norm_apply(nc, link, y, x, mv, rstd, ST, y_ready)
            for j in range(2):
                dve.wait_ge(y_turned, j + 1)
                nc.vector.tensor_copy(yT[:, 1 + j * BANK:1 + (j + 1) * BANK], ps[j][:, :]).then_inc(yT_kept, 1)
            dve.wait_ge(yT_kept, 2)
            dve.wait_ge(made, 3)
            link(nc.vector.tensor_scalar(mixT[:, :], yT[:, 1:S + 1], mixw[:, 1:2], None, ALU.mult))
            link(nc.vector.scalar_tensor_tensor(out=mixT[:, :], in0=yT[:, 0:S], scalar=mixw[:, 0:1],
                                                in1=mixT[:, :], op0=ALU.mult, op1=ALU.add))
            nc.vector.scalar_tensor_tensor(out=mixT[:, :], in0=yT[:, 2:S + 2], scalar=mixw[:, 2:3],
                                           in1=mixT[:, :], op0=ALU.mult, op1=ALU.add).then_inc(mix_ready, 1)
            for t in range(ST):
                dve.wait_ge(hid_ready, t + 1)
                nc.vector.tensor_tensor(hid[:, t, :], ps[t % 4][:, 0:HW + DM], b1[:, :], ALU.add
                                        ).then_inc(hid_kept, 1)
            for j in range(2):
                dve.wait_ge(tanh_turned, j + 1)
                nc.vector.tensor_copy(tanhT[:, j * BANK:(j + 1) * BANK], ps[4 + j][0:DM, :]).then_inc(tanhT_kept, 1)
            dve.wait_ge(score_ready, 1)
            link(nc.vector.tensor_tensor(score[:, :, :], ps[6][:, 0:ST * PATHS].rearrange(
                "p (t e) -> p t e", e=PATHS), bo2[:, :, :].to_broadcast([P, ST, PATHS]), ALU.add))
            for t in range(ST):
                link(nc.vector.max(out=top[:, t, :], in_=score[:, t, :]))
            for t in range(ST):
                link(nc.vector.max_index(out=top_at[:, t, :], in_max=top[:, t, :], in_values=score[:, t, :]))
            link(nc.vector.tensor_copy(best[:, :], top_at[:, :, 0]))
            link(nc.vector.tensor_tensor(kept[:, :, HW:HW + PATHS],
                                         iota[:, :].unsqueeze(1).to_broadcast([P, ST, PATHS]),
                                         best[:, :].unsqueeze(2).to_broadcast([P, ST, PATHS]), ALU.is_equal))
            dve.wait_ge(hid_kept, ST)
            for t in range(ST):
                nc.vector.tensor_tensor(
                    kept[:, t, 0:HW].rearrange("p (e m) -> p e m", e=PATHS),
                    hid[:, t, 0:HW].rearrange("p (e m) -> p e m", e=PATHS),
                    kept[:, t, HW:HW + PATHS].unsqueeze(2).to_broadcast([P, PATHS, DM]), ALU.mult
                ).then_inc(chosen, 1)
            for j in range(2):
                dve.wait_ge(path_done, 4 * j + 4)
                link(nc.vector.tensor_tensor(z[:, 4 * j:4 * j + 4, :], tiles_of(4 + j),
                                             y[:, 4 * j:4 * j + 4, :], ALU.add))
            layer_norm_stats(nc, link, z, stats, mv, rstd, ST, var2_ready)
            dve.wait_ge(std2_ready, 1)
            layer_norm_apply(nc, link, z, z, mv, rstd, ST, normed)
            dve.wait_ge(normed, ST)
            for j in range(2):
                half = z[:, 4 * j:4 * j + 4, :]
                link(nc.vector.tensor_tensor(half, half, gb[:, 0:1, :].to_broadcast([P, 4, D]), ALU.mult))
                link(nc.vector.tensor_tensor(half, half, gb[:, 1:2, :].to_broadcast([P, 4, D]), ALU.add))
                nc.vector.tensor_tensor(half, half, x[:, 4 * j:4 * j + 4, :], ALU.add).then_inc(out_ready, 1)


def build(nc, a, out, stop=None):
    with ExitStack() as ctx:
        big = ctx.enter_context(nc.psum_tensor("banks", [P, 8, BANK], F32))
        g = {
            "x": ctx.enter_context(nc.sbuf_tensor("x_sb", [P, ST, D], F32)),
            "ident": ctx.enter_context(nc.sbuf_tensor("ident", [P, P], F32)),
            "identb": ctx.enter_context(nc.sbuf_tensor("identb", [P, P], BF16)),
            "big": big, "ps": [big[:, i, :] for i in range(8)],
        }
        cross_attention_0(nc, g, a)
        if stop != "x1":
            moe_ffn_0(nc, g, a)
        if stop not in ("x1", "x2"):
            g["on"] = ctx.enter_context(nc.sbuf_tensor("o_nat", [P, ST, HEADS, HD], F32))
            with ExitStack() as attn:
                g["kT"] = attn.enter_context(nc.sbuf_tensor("kT", [P, PAIRS, NK], BF16))
                g["vn"] = attn.enter_context(nc.sbuf_tensor("v_nat", [P, KT, HEADS, HD + 1], F32))
                g["qn"] = attn.enter_context(nc.sbuf_tensor("q_nat", [P, ST * HEADS, SLOT], BF16))
                project_keys(nc, g, a)
                if stop != "prep": cross_attention_1(nc, g, a)
            if stop is None:
                moe_by_argmax(nc, g, a, out)
                return
        s = ctx.enter_context(nc.semaphore("out_done"))
        with nc.Block() as block:
            @block.sync
            def _(sp):
                src = g["on"][:, :, :, :].rearrange("p t h d -> p t (h d)") if stop == "o" else g["x"][:, :, :]
                sp.dma_start(out.rearrange("(t p) d -> p t d", p=P), src).then_inc(s, 16)
                sp.wait_ge(s, 16)


def kernel(**inputs):
    import numpy as _np
    import concourse.bacc as _bacc
    from concourse import mybir as _mybir
    from concourse.bass_utils import run_bass_kernel_spmd as _run

    nc = _bacc.Bacc("TRN2", target_bir_lowering=False, num_devices=1)
    arrays, args = {}, {}
    for name, value in inputs.items():
        arrays[f"in_{name}_dram"] = _np.ascontiguousarray(value)
        args[name] = nc.dram_tensor(f"in_{name}_dram", arrays[f"in_{name}_dram"].shape,
                                    _mybir.dt.from_np(arrays[f"in_{name}_dram"].dtype),
                                    kind="ExternalInput").ap()
    out = nc.dram_tensor("out_0_dram", (1, S, D), _mybir.dt.float32, kind="ExternalOutput").ap()
    build(nc, args, out)
    r = _run(nc, [arrays], core_ids=[0])
    return r.results[0]["out_0_dram"]
```

```python
from contextlib import ExitStack

import concourse.bass as bass
from concourse import mybir

F32 = mybir.dt.float32
BF16 = mybir.dt.bfloat16
U32 = mybir.dt.uint32
ALU = mybir.AluOpType
ACT = mybir.ActivationFunctionType
AX_X = mybir.AxisListType.X

P = 128
D = 128
S = 1024
ST = S // P
NK = 6404
KF = NK // P
KR = NK - KF * P
KT = KF + 1
BANK = 512
NCH = NK // BANK
CR = NK - NCH * BANK
EPS = 1e-5
LOWEST = -3.0e38


class Link:

    def __init__(self, eng, sem):
        self.eng, self.sem, self.base, self.n = eng, sem, 0, 0

    def __call__(self, ins):
        self.n += 1
        ins.then_inc(self.sem, 1)
        self.eng.wait_ge(self.sem, self.base + self.n)

    def enter(self, i, per):
        self.start = self.base + self.n
        self.per = per
        self.base, self.n = self.start + i * per, 0

    def leave(self, passes):
        assert self.n == self.per, (self.n, self.per)
        self.base, self.n = self.start + passes * self.per, 0


def layer_norm_stats(nc, link, src, stats, mv, var, tiles, ready):
    for t in range(tiles):
        link(nc.vector.bn_stats(out=stats[:, t, :], in_=src[:, t, :]))
    for t in range(tiles):
        link(nc.vector.bn_aggr(out=mv[:, t, :], in_=stats[:, t, :]))
    nc.vector.tensor_scalar(var[:, :], mv[:, :, 1], EPS, None, ALU.add).then_inc(ready, 1)


def layer_norm_apply(nc, link, dst, src, mv, rstd, tiles, ready):
    link(nc.vector.reciprocal(rstd[:, :], rstd[:, :]))
    for t in range(tiles):
        nc.vector.tensor_scalar(dst[:, t, :], src[:, t, :], mv[:, t, 0:1], rstd[:, t:t + 1],
                                ALU.subtract, ALU.mult).then_inc(ready, 1)


def cross_attention_0(nc, g, a):
    SCALE = float(D) ** -0.5
    MS = 2
    SB = 3
    TB = 3
    GROUPS = [list(range(4 * i, min(4 * i + 4, KT))) for i in range((KT + 3) // 4)]
    NG = len(GROUPS)
    with ExitStack() as ctx:
        def sb(name, shape, dt=F32):
            return ctx.enter_context(nc.sbuf_tensor(name, shape, dt))

        def sem(name):
            return ctx.enter_context(nc.semaphore(name))

        ctx_nat = sb("a0_ctx", [P, KT, D])
        kT = sb("a0_kT", [P, NK])
        ms = sb("a0_ms", [P, MS, NK])
        pr = sb("a0_pr", [P, MS, NK])
        chunk = sb("a0_chunk", [P, 2, 4, D])
        chunkT = sb("a0_chunkT", [P, 2, BANK])
        hT = sb("a0_hT", [P, 2, BANK])
        pT = sb("a0_pT", [P, TB, BANK])
        w_nat = sb("a0_w", [P, 2, D])
        wT = sb("a0_wT", [P, 2, D])
        bias = sb("a0_bias", [P, 2])
        xn = sb("a0_xn", [P, ST, D])
        xnT = sb("a0_xnT", [P, S])
        q1T = sb("a0_q1T", [P, S])
        qT = sb("a0_qT", [P, S])
        oT = sb("a0_oT", [P, 2, P])
        stats = sb("a0_stats", [P, ST, 6])
        mv = sb("a0_mv", [P, ST, 2])
        rstd = sb("a0_rstd", [P, ST])
        cmax = sb("a0_cmax", [P, 2, NCH + 1])
        nmax = sb("a0_nmax", [P, 2])
        total = sb("a0_total", [P, 2])
        rtotal = sb("a0_rtotal", [P, 2])
        q_tile = sb("a0_q_tile", [P, 2, P])
        ps = g["ps"]
        x = g["x"]
        q_tile_ready = sem("a0_q_tile_ready")

        x_in, w_in, ctx_in = sem("a0_x_in"), sem("a0_w_in"), sem("a0_ctx_in")
        chunk_in = [sem(f"a0_chunk_in{i}") for i in range(2)]
        mask_in = [sem(f"a0_mask_in{i}") for i in range(MS)]
        ident_made = sem("a0_ident_made")
        w_turned, w_kept = sem("a0_w_turned"), sem("a0_w_kept")
        var_ready, std_ready, xn_ready = sem("a0_var"), sem("a0_std"), sem("a0_xn_ready")
        xn_turned, xnT_kept = sem("a0_xn_turned"), sem("a0_xnT_kept")
        q1_ready, q1_kept, q_ready, q_kept = sem("a0_q1"), sem("a0_q1k"), sem("a0_q"), sem("a0_qk")
        chunk_turned, chunkT_kept = sem("a0_ct"), sem("a0_ck")
        h_ready, h_kept, k_ready, k_kept = sem("a0_h"), sem("a0_hk"), sem("a0_k"), sem("a0_kk")
        scores_ready, scores_masked = sem("a0_s"), sem("a0_sm")
        max_ready, probs_ready = sem("a0_max"), sem("a0_probs")
        probs_turned, pT_kept, pv_done = sem("a0_pt"), sem("a0_ptk"), sem("a0_pv")
        out_ready, oT_kept, out_turned, x_done = sem("a0_o"), sem("a0_ok"), sem("a0_ot"), sem("a0_xd")
        dve_step, pool_step, dve_passed = sem("a0_dve_step"), sem("a0_pool_step"), sem("a0_dve_passed")

        block = ctx.enter_context(nc.Block())
        FREE = 2

        def turned_rows(kt):
            return P if kt < KF else KR

        @block.sync
        def _(sp):
            sp.dma_start(x[:, :, :], a["x"][0].rearrange("(t p) d -> p t d", p=P)).then_inc(x_in, 16)
            sp.dma_start(w_nat[:, 0, :], a["L0_xattn_W1"]).then_inc(w_in, 16)
            sp.dma_start(w_nat[:, 1, :], a["L0_xattn_W2"]).then_inc(w_in, 16)
            sp.dma_start(bias[:, 0:1], a["L0_xattn_b1"].rearrange("(p o) -> p o", o=1)).then_inc(w_in, 16)
            sp.dma_start(bias[:, 1:2], a["L0_xattn_b2"].rearrange("(p o) -> p o", o=1)).then_inc(w_in, 16)
            ctx_rows = a["ctx_1024"][0]

            def load_chunk(c, slot):
                sp.dma_start(chunk[:, slot, :, :],
                             ctx_rows[bass.ds(c * BANK, BANK), :].rearrange("(n p) d -> p n d", p=P)
                             ).then_inc(chunk_in[slot], 16)

            def load_mask(t, slot):
                sp.dma_start(ms[:, slot, :], a["fside_1xSxS2_0"][0][bass.ds(t * P, P), :]
                             ).then_inc(mask_in[slot], 16)

            for c in range(2):
                load_chunk(c, c)
            load_mask(0, 0)
            sp.dma_start(ctx_nat[:, 0:KF, :],
                         ctx_rows[0:KF * P, :].rearrange("(n p) d -> p n d", p=P)).then_inc(ctx_in, 16)
            sp.dma_start(ctx_nat[0:KR, KF, :], ctx_rows[KF * P:NK, :]).then_inc(ctx_in, 16)
            load_mask(1, 1)
            with sp.Fori(1, NCH // 2) as i:
                for slot in range(2):
                    sp.wait_ge(chunk_turned, 2 * i + slot - 1)
                    load_chunk(2 * i + slot, slot)
            sp.wait_ge(chunk_turned, NCH - 1)
            sp.dma_start(chunk[:, 0, 0:2, :],
                         ctx_rows[NCH * BANK:KF * P, :].rearrange("(n p) d -> p n d", p=P)
                         ).then_inc(chunk_in[0], 16)
            sp.dma_start(chunk[0:KR, 0, 2, :], ctx_rows[KF * P:NK, :]).then_inc(chunk_in[0], 16)
            with sp.Fori(1, ST // 2) as i:
                for slot in range(2):
                    sp.wait_ge(probs_ready, 2 * i + slot - 1)
                    load_mask(2 * i + slot, slot)

        @block.gpsimd
        def _(pool):
            link = Link(pool, pool_step)
            for ident in (g["ident"], g["identb"]):
                link(nc.gpsimd.memset(ident[:, :], 0.0))
                nc.gpsimd.affine_select(out=ident[:, :], in_=ident[:, :], compare_op=ALU.not_equal,
                                        fill=1.0, base=0, pattern=[[-1, P]],
                                        channel_multiplier=1).then_inc(ident_made, 1)

        @block.tensor
        def _(pe):
            ident = g["ident"]
            pe.sem_inc(h_ready, FREE)
            pe.sem_inc(k_ready, FREE)
            pe.wait_ge(ident_made, 2)
            pe.wait_ge(w_in, 64)
            for j in range(2):
                mm = pe.transpose(ps[7][:, j * D:(j + 1) * D], w_nat[:, j, :], ident[:, :])
            mm.then_inc(w_turned, 1)
            pe.wait_ge(w_kept, 1)

            def turn_chunk(c, slot, tiles):
                for j, rows in enumerate(tiles):
                    mm = pe.transpose(ps[slot][:, j * P:j * P + rows], chunk[0:rows, slot, j, :],
                                      ident[0:rows, 0:rows])
                mm.then_inc(chunk_turned, 1)

            def project(c, slot, w, src, src_kept, bank, ready, n):
                pe.wait_ge(src_kept, c + 1 + FREE)
                pe.matmul(ps[bank + slot][:, 0:n], wT[:, w, :], src[:, slot, 0:n],
                          start=True, stop=True).then_inc(ready, 1)

            with pe.Fori(0, NCH // 2) as i:
                for slot in range(2):
                    pe.wait_ge(chunk_in[slot], 16 * i + 16)
                    pe.wait_ge(chunkT_kept, 2 * i + FREE)
                    turn_chunk(2 * i + slot, slot, [P] * 4)
                for slot in range(2):
                    pe.wait_ge(h_kept, 2 * i + FREE)
                    project(2 * i + slot, slot, 0, chunkT, chunkT_kept, 2, h_ready, BANK)
                for slot in range(2):
                    pe.wait_ge(k_kept, 2 * i + FREE)
                    project(2 * i + slot, slot, 1, hT, h_kept, 4, k_ready, BANK)
            pe.wait_ge(chunk_in[0], 16 * (NCH // 2) + 32)
            turn_chunk(NCH, 0, [P] * (KF - 4 * NCH) + [KR])
            project(NCH, 0, 0, chunkT, chunkT_kept, 2, h_ready, CR)
            project(NCH, 0, 1, hT, h_kept, 4, k_ready, CR)

            pe.wait_ge(xn_ready, ST)
            for t in range(ST):
                if t % 4 == 0:
                    pe.wait_ge(k_kept, NCH + 1 + FREE)
                mm = pe.transpose(ps[6 + t // 4][:, (t % 4) * P:(t % 4 + 1) * P], xn[:, t, :], ident[:, :])
                if t % 4 == 3:
                    mm.then_inc(xn_turned, 1)
            for w, src, kept, ready in ((0, xnT, xnT_kept, q1_ready), (1, q1T, q1_kept, q_ready)):
                for j in range(2):
                    pe.wait_ge(kept, j + 1)
                    pe.matmul(ps[6 + j][:, :], wT[:, w, :], src[:, j * BANK:(j + 1) * BANK],
                              start=True, stop=True).then_inc(ready, 1)
            pe.wait_ge(q_kept, 2)

            def scores(t, slot, first=False):
                pe.wait_ge(q_tile_ready, t + 1)
                for c in range(NCH + 1):
                    n = BANK if c < NCH else CR
                    if c >= SB:
                        pe.wait_ge(scores_masked, t * (NCH + 1) + c - SB + 1)
                    elif not first:
                        pe.wait_ge(scores_masked, t * (NCH + 1))
                    pe.matmul(ps[c % SB][:, 0:n], q_tile[:, slot, :], kT[:, c * BANK:c * BANK + n],
                              start=True, stop=True).then_inc(scores_ready, 1)

            def turn_probs(t, slot, gi):
                for j, kt in enumerate(GROUPS[gi]):
                    rows = turned_rows(kt)
                    mm = pe.transpose(ps[SB + gi % TB][0:rows, j * P:(j + 1) * P],
                                      pr[:, slot, kt * P:kt * P + rows], ident[:, :])
                mm.then_inc(probs_turned, 1)

            def weigh(t, slot, first=False):
                pe.wait_ge(probs_ready, t + 1)
                for gi in range(NG + 1):
                    if gi < NG:
                        if gi >= TB:
                            pe.wait_ge(pT_kept, t * NG + gi - TB + 1)
                        elif not first:
                            pe.wait_ge(pT_kept, t * NG)
                        turn_probs(t, slot, gi)
                    if gi >= 1:
                        pe.wait_ge(pT_kept, t * NG + gi)
                        for j, kt in enumerate(GROUPS[gi - 1]):
                            rows = turned_rows(kt)
                            if kt == 0 and not first:
                                pe.wait_ge(x_done, t - 1)
                            mm = pe.matmul(ps[6 + slot][:, 0:P], ctx_nat[0:rows, kt, :],
                                           pT[0:rows, (gi - 1) % TB, j * P:(j + 1) * P],
                                           start=(kt == 0), stop=(kt == KT - 1))
                        mm.then_inc(pv_done, 1)
                pe.wait_ge(oT_kept, t + 1)
                pe.transpose(ps[6 + slot][:, 0:P], oT[:, slot, :], ident[:, :]).then_inc(out_turned, 1)

            pe.wait_ge(ctx_in, 32)
            scores(0, 0, first=True)
            scores(1, 1)
            weigh(0, 0, first=True)
            scores(2, 0)
            weigh(1, 1)
            scores(3, 1)
            with pe.Fori(1, ST // 2 - 1) as i:
                for slot in range(2):
                    weigh(2 * i + slot, slot)
                    scores(2 * i + slot + 2, slot)
            for slot in range(2):
                weigh(ST - 2 + slot, slot)

        @block.vector
        def _(dve):
            link = Link(dve, dve_step)
            dve.sem_inc(chunkT_kept, FREE)
            dve.wait_ge(w_turned, 1)
            dve.tensor_copy(wT[:, :, :], ps[7][:, 0:2 * D].rearrange("p (j d) -> p j d", j=2)).then_inc(w_kept, 1)

            dve.wait_ge(x_in, 16)
            layer_norm_stats(nc, link, x, stats, mv, rstd, ST, var_ready)
            dve.wait_ge(std_ready, 1)
            layer_norm_apply(nc, link, xn, x, mv, rstd, ST, xn_ready)

            def keep_chunk(c, slot, n):
                dve.wait_ge(chunk_turned, c + 1)
                dve.wait_ge(h_ready, c - slot + FREE)
                dve.tensor_copy(chunkT[:, slot, 0:n], ps[slot][:, 0:n]).then_inc(chunkT_kept, 1)

            with dve.Fori(0, NCH // 2) as i:
                for slot in range(2):
                    keep_chunk(2 * i + slot, slot, BANK)
            keep_chunk(NCH, 0, CR)

            for j in range(2):
                dve.wait_ge(xn_turned, j + 1)
                dve.tensor_copy(xnT[:, j * BANK:(j + 1) * BANK], ps[6 + j][:, :]).then_inc(xnT_kept, 1)
            for j in range(2):
                dve.wait_ge(q1_ready, j + 1)
                dve.tensor_scalar(q1T[:, j * BANK:(j + 1) * BANK], ps[6 + j][:, :], bias[:, 0:1], None,
                                  ALU.add).then_inc(q1_kept, 1)
            for j in range(2):
                dve.wait_ge(q_ready, j + 1)
                dve.tensor_scalar(qT[:, j * BANK:(j + 1) * BANK], ps[6 + j][:, :], bias[:, 1:2], SCALE,
                                  ALU.add, ALU.mult).then_inc(q_kept, 1)
            dve.wait_ge(q_kept, 2)
            for t in range(2):
                dve.tensor_copy(q_tile[:, t, :], qT[:, t * P:(t + 1) * P]).then_inc(q_tile_ready, 1)

            def mask(t, slot):
                dve.wait_ge(mask_in[slot], 16 * mask_no(t, slot))
                for c in range(NCH + 1):
                    n = BANK if c < NCH else CR
                    at = slice(c * BANK, c * BANK + n)
                    wait_alone(dve, scores_ready, t * (NCH + 1) + c + 1, dve_passed)
                    dve.tensor_tensor_reduce(ms[:, slot, at], ps[c % SB][:, 0:n], ms[:, slot, at], 1.0, LOWEST,
                                             ALU.add, ALU.max, cmax[:, slot, c:c + 1]).then_inc(scores_masked, 1)
                dve.wait_ge(scores_masked, (t + 1) * (NCH + 1))
                dve.tensor_reduce(nmax[:, slot:slot + 1], cmax[:, slot, :], AX_X, ALU.max,
                                  negate=True).then_inc(max_ready, 1)

            def mask_no(t, slot):
                return t // 2 + 1 if isinstance(t, int) else mask_pass[0] + 1

            mask_pass = [None]

            def next_queries(t, slot):
                dve.wait_ge(scores_ready, (t - 1) * (NCH + 1))
                dve.tensor_copy(q_tile[:, slot, :], qT[:, bass.ds(t * P, P)]).then_inc(q_tile_ready, 1)

            def keep_probs(t, slot):
                for gi in range(NG):
                    full = sum(kt < KF for kt in GROUPS[gi])
                    dve.wait_ge(probs_turned, t * NG + gi + 1)
                    if gi >= TB:
                        dve.wait_ge(pv_done, t * NG + gi - TB + 1)
                    else:
                        dve.wait_ge(pv_done, t * NG)
                    cp = dve.tensor_copy(pT[:, gi % TB, 0:full * P], ps[SB + gi % TB][:, 0:full * P])
                    if full < len(GROUPS[gi]):
                        cp = dve.tensor_copy(pT[0:KR, gi % TB, full * P:(full + 1) * P],
                                             ps[SB + gi % TB][0:KR, full * P:(full + 1) * P])
                    cp.then_inc(pT_kept, 1)
                dve.wait_ge(pv_done, (t + 1) * NG)
                dve.tensor_copy(oT[:, slot, :], ps[6 + slot][:, 0:P]).then_inc(oT_kept, 1)
                dve.wait_ge(out_turned, t + 1)
                link(nc.vector.reciprocal(rtotal[:, slot:slot + 1], total[:, slot:slot + 1]))
                xt = x[:, bass.ds(t, 1), :].rearrange("p t d -> p (t d)")
                dve.scalar_tensor_tensor(out=xt, in0=ps[6 + slot][:, 0:P], scalar=rtotal[:, slot:slot + 1],
                                         in1=xt, op0=ALU.mult, op1=ALU.add).then_inc(x_done, 1)

            mask(0, 0)
            mask(1, 1)
            for t in range(2):
                next_queries(t + 2, t)
                keep_probs(t, t)
                mask(t + 2, t)
            with dve.Fori(1, ST // 2 - 1) as i:
                link.enter(i - 1, 2)
                mask_pass[0] = i + 1
                for slot in range(2):
                    next_queries(2 * i + slot + 2, slot)
                    keep_probs(2 * i + slot, slot)
                    mask(2 * i + slot + 2, slot)
                link.leave(ST // 2 - 2)
            for slot in range(2):
                keep_probs(ST - 2 + slot, slot)

        @block.scalar
        def _(act):
            act.sem_inc(h_kept, FREE)
            act.sem_inc(k_kept, FREE)
            act.wait_ge(var_ready, 1)
            nc.scalar.activation(rstd[:, :], rstd[:, :], ACT.Sqrt).then_inc(std_ready, 1)

            def keep(c, slot, n):
                act.wait_ge(h_ready, c + 1 + FREE)
                act.wait_ge(k_ready, c - slot + FREE)
                nc.scalar.activation(hT[:, slot, 0:n], ps[2 + slot][:, 0:n], ACT.Identity,
                                     bias=bias[:, 0:1]).then_inc(h_kept, 1)

            def keep_k(c, slot, n):
                act.wait_ge(k_ready, c + 1 + FREE)
                nc.scalar.activation(kT[:, bass.ds(c * BANK, n)], ps[4 + slot][:, 0:n], ACT.Identity,
                                     bias=bias[:, 1:2]).then_inc(k_kept, 1)

            with act.Fori(0, NCH // 2) as i:
                for slot in range(2):
                    keep(2 * i + slot, slot, BANK)
                for slot in range(2):
                    keep_k(2 * i + slot, slot, BANK)
            keep(NCH, 0, CR)
            keep_k(NCH, 0, CR)

            def exps(t, slot, first=False):
                act.wait_ge(max_ready, t + 1)
                if not first:
                    act.wait_ge(probs_turned, (t - 1) * NG)
                    act.wait_ge(x_done, t - 1)
                nc.scalar.activation(pr[:, slot, :], ms[:, slot, :], ACT.Exp, bias=nmax[:, slot:slot + 1],
                                     accum_out=total[:, slot:slot + 1]).then_inc(probs_ready, 1)

            for t in range(2):
                exps(t, t, first=True)
            with act.Fori(1, ST // 2) as i:
                for slot in range(2):
                    exps(2 * i + slot, slot)


def wait(eng, sem, value):
    if not isinstance(value, int) or value > 0:
        eng.wait_ge(sem, value)


def wait_alone(eng, sem, value, passed):
    eng.wait_ge(sem, value)
    if not isinstance(value, int):
        eng.sem_inc(passed, 1)


def moe_ffn_0(nc, g, a):
    E = 16
    EA = E + 1
    TOPK = 8
    ROUTE_SCALE = 2.826
    PARTS = 3
    with ExitStack() as ctx:
        def sb(name, shape, dt=F32):
            return ctx.enter_context(nc.sbuf_tensor(name, shape, dt))

        def sem(name):
            return ctx.enter_context(nc.semaphore(name))

        w_nat = sb("m_w", [P, 2, 3, D])
        wT = sb("m_wT", [P, 2, 3, D])
        router = sb("m_router", [E, D])
        routerT = sb("m_routerT", [P, E])
        bias = sb("m_bias", [P, E])
        xn = sb("m_xn", [P, ST, D])
        xnT = sb("m_xnT", [P, S])
        stats = sb("m_stats", [P, ST, 6])
        mv = sb("m_mv", [P, ST, 2])
        rstd = sb("m_rstd", [P, ST])
        prob = sb("m_prob", [P, ST, E])
        sel = sb("m_sel", [P, ST, E])
        top = sb("m_top", [P, ST, TOPK])
        rest = sb("m_rest", [P, ST, E])
        weight = sb("m_weight", [P, ST, EA])
        wsum = sb("m_wsum", [P, ST])
        left = sb("m_left", [P, ST, EA])
        split = sb("m_split", [P, ST, P], BF16)
        splitT = sb("m_splitT", [P, S], BF16)
        pick = sb("m_pick", [P, EA, P], BF16)
        silu = sb("m_silu", [P, 2, BANK])
        h = sb("m_h", [P, 2, BANK])
        hw = sb("m_hw", [P, 2, BANK])
        yT = sb("m_yT", [P, S])
        ps, x = g["ps"], g["x"]
        ident, identb = g["ident"], g["identb"]

        w_in = [sem(f"m_w_in{i}") for i in range(2)]
        small_in = sem("m_small_in")
        pool_made = sem("m_pool_made")
        var_ready, std_ready, xn_ready = sem("m_var"), sem("m_std"), sem("m_xn_ready")
        xn_turned, xnT_kept = sem("m_xn_turned"), sem("m_xnT_kept")
        router_turned, router_kept = sem("m_rt"), sem("m_rk")
        logits_ready, prob_ready, split_ready = sem("m_logits"), sem("m_prob_ready"), sem("m_split_ready")
        split_turned, split_kept = sem("m_split_turned"), sem("m_split_kept")
        w_turned, w_kept = sem("m_w_turned"), sem("m_w_kept")
        gate_ready, up_ready, spread_ready = sem("m_gate"), sem("m_up"), sem("m_spread")
        silu_ready, h_ready, hw_ready = sem("m_silu_ready"), sem("m_h_ready"), sem("m_hw_ready")
        down_done, y_kept, y_turned = sem("m_down"), sem("m_yk"), sem("m_yt")
        dve_step, pool_step = sem("m_dve_step"), sem("m_pool_step")

        block = ctx.enter_context(nc.Block())

        @block.sync
        def _(sp):
            def load(e, slot):
                for j, name in enumerate(("L0_ffn_w_gate", "L0_ffn_w_up", "L0_ffn_w_down")):
                    src = a[name][bass.ds(e, 1), :, :].rearrange("e p d -> (e p) d")
                    sp.dma_start(w_nat[:, slot, j, :], src).then_inc(w_in[slot], 16)

            load(0, 0)
            sp.dma_start(router[:, :], a["L0_ffn_gate_w"]).then_inc(small_in, 16)
            sp.dma_start(bias[:, :], a["L0_ffn_expert_bias"].partition_broadcast(P)).then_inc(small_in, 16)
            load(1, 1)
            with sp.Fori(1, E // 2) as i:
                for slot in range(2):
                    sp.wait_ge(w_turned, 2 * i + slot - 1)
                    load(2 * i + slot, slot)
            sp.wait_ge(w_turned, E - 1)
            for j, name in enumerate(("L0_ffn_shared_gate_w", "L0_ffn_shared_up_w", "L0_ffn_shared_down_w")):
                sp.dma_start(w_nat[:, 0, j, :], a[name]).then_inc(w_in[0], 16)

        @block.gpsimd
        def _(pool):
            link = Link(pool, pool_step)
            nc.gpsimd.memset(split[:, :, :], 0.0).then_inc(pool_made, 1)
            nc.gpsimd.memset(weight[:, :, :], 1.0).then_inc(pool_made, 1)
            link(nc.gpsimd.memset(pick[:, :, :], 0.0))
            for part in range(PARTS):
                made = nc.gpsimd.affine_select(out=pick[:, :, :], in_=pick[:, :, :],
                                               compare_op=ALU.not_equal, fill=1.0, base=-part * EA,
                                               pattern=[[-1, EA], [0, P]], channel_multiplier=1)
                if part < PARTS - 1:
                    link(made)
            made.then_inc(pool_made, 1)

        @block.tensor
        def _(pe):
            pe.wait_ge(small_in, 32)
            pe.transpose(ps[2][:, 0:E], router[:, :], ident[0:E, 0:E]).then_inc(router_turned, 1)
            pe.wait_ge(xn_ready, ST)
            for t in range(ST):
                mm = pe.transpose(ps[t // 4][:, (t % 4) * P:(t % 4 + 1) * P], xn[:, t, :], ident[:, :])
                if t % 4 == 3:
                    mm.then_inc(xn_turned, 1)
            pe.wait_ge(router_kept, 1)
            pe.wait_ge(xnT_kept, 2)
            for t in range(ST):
                mm = pe.matmul(ps[3][:, t * E:(t + 1) * E], xnT[:, t * P:(t + 1) * P], routerT[:, :],
                               start=True, stop=True)
            mm.then_inc(logits_ready, 1)

            def turn_weights(e, slot, loads):
                wait(pe, w_in[slot], 48 * loads)
                wait(pe, w_kept, e)
                for j in range(3):
                    mm = pe.transpose(ps[7][:, j * D:(j + 1) * D], w_nat[:, slot, j, :], ident[:, :])
                mm.then_inc(w_turned, 1)

            def up(e, slot, half):
                n = 2 * e + half
                tok = slice(half * BANK, (half + 1) * BANK)
                if half == 0:
                    pe.wait_ge(w_kept, e + 1)
                wait(pe, silu_ready, n - 1)
                pe.matmul(ps[2 + half][:, :], wT[:, slot, 0, :], xnT[:, tok], start=True, stop=True
                          ).then_inc(gate_ready, 1)
                wait(pe, h_ready, n - 1)
                pe.matmul(ps[4 + half][:, :], wT[:, slot, 1, :], xnT[:, tok], start=True, stop=True
                          ).then_inc(up_ready, 1)
                wait(pe, hw_ready, n)
                pe.matmul(ps[6][:, :], pick[:, bass.ds(e, 1), :].rearrange("p e m -> p (e m)"),
                          splitT[:, tok], start=True, stop=True).then_inc(spread_ready, 1)

            def down(n, slot, half, first=False, last=False):
                pe.wait_ge(hw_ready, n + 1)
                pe.matmul(ps[half][:, :], wT[:, slot, 2, :], hw[:, half, :], start=first, stop=last,
                          skip_group_check=True).then_inc(down_done, 1)

            turn_weights(0, 0, 1)
            pe.wait_ge(split_ready, 1)
            for t in range(ST):
                mm = pe.transpose(ps[6][:, :].bitcast(BF16)[:, t * P:(t + 1) * P], split[:, t, :],
                                  identb[:, :])
            mm.then_inc(split_turned, 1)
            pe.wait_ge(split_kept, 1)
            pe.wait_ge(pool_made, 3)
            pe.wait_ge(prob_ready, 1)
            up(0, 0, 0)
            turn_weights(1, 1, 1)
            up(0, 0, 1)
            down(0, 0, 0, first=True)

            def expert(e, slot, loads, first=False, last=False):
                up(e, slot, 0)
                if not last:
                    turn_weights(e + 1, 1 - slot, loads)
                down(2 * e - 1, 1 - slot, 1, first=first)
                up(e, slot, 1)
                down(2 * e, slot, 0, last=last)

            expert(1, 1, 2, first=True)
            with pe.Fori(1, E // 2) as i:
                for k in range(2):
                    expert(2 * i + k, k, i + 1 + k)
            expert(E, 0, 0, last=True)
            down(2 * E + 1, 0, 1, last=True)
            for t in range(ST):
                if t % 4 == 0:
                    pe.wait_ge(y_kept, t // 4 + 1)
                mm = pe.transpose(ps[2 + t // 4][:, (t % 4) * P:(t % 4 + 1) * P],
                                  yT[:, t * P:(t + 1) * P], ident[:, :])
                if t % 4 == 3:
                    mm.then_inc(y_turned, 1)

        @block.scalar
        def _(act):
            act.wait_ge(var_ready, 1)
            nc.scalar.activation(rstd[:, :], rstd[:, :], ACT.Sqrt).then_inc(std_ready, 1)
            act.wait_ge(logits_ready, 1)
            nc.scalar.activation(prob[:, :, :], ps[3][:, 0:ST * E].rearrange("p (t e) -> p t e", e=E),
                                 ACT.Sigmoid).then_inc(prob_ready, 1)

            def keep_weights(e, slot):
                act.wait_ge(w_turned, e + 1)
                wait(act, down_done, 2 * e - 2)
                nc.scalar.activation(wT[:, slot, :, :], ps[7][:, 0:3 * D].rearrange("p (j d) -> p j d", d=D),
                                     ACT.Copy).then_inc(w_kept, 1)

            def gate(n, half):
                act.wait_ge(gate_ready, n + 1)
                wait(act, h_ready, n - 1)
                nc.scalar.activation(silu[:, half, :], ps[2 + half][:, :], ACT.Silu).then_inc(silu_ready, 1)

            keep_weights(0, 0)
            gate(0, 0)
            keep_weights(1, 1)
            gate(1, 1)
            gate(2, 0)
            keep_weights(2, 0)
            gate(3, 1)
            with act.Fori(1, E // 2) as i:
                for k in range(2):
                    e = 2 * i + k
                    gate(2 * e, 0)
                    keep_weights(e + 1, 1 - k)
                    gate(2 * e + 1, 1)
            gate(2 * E, 0)
            gate(2 * E + 1, 1)

        @block.vector
        def _(dve):
            link = Link(dve, dve_step)
            dve.wait_ge(router_turned, 1)
            nc.vector.tensor_copy(routerT[:, :], ps[2][:, 0:E]).then_inc(router_kept, 1)
            layer_norm_stats(nc, link, x, stats, mv, rstd, ST, var_ready)
            dve.wait_ge(std_ready, 1)
            layer_norm_apply(nc, link, xn, x, mv, rstd, ST, xn_ready)
            for j in range(2):
                dve.wait_ge(xn_turned, j + 1)
                nc.vector.tensor_copy(xnT[:, j * BANK:(j + 1) * BANK], ps[j][:, :]).then_inc(xnT_kept, 1)

            dve.wait_ge(prob_ready, 1)
            dve.wait_ge(small_in, 32)
            link(nc.vector.tensor_tensor(sel[:, :, :], prob[:, :, :],
                                         bias[:, :].unsqueeze(1).to_broadcast([P, ST, E]), ALU.add))
            for t in range(ST):
                link(nc.vector.max(out=top[:, t, :], in_=sel[:, t, :]))
            for t in range(ST):
                link(nc.vector.match_replace(out=rest[:, t, :], in_to_replace=top[:, t, :],
                                             in_values=sel[:, t, :], imm_value=LOWEST))
            link(nc.vector.tensor_tensor(rest[:, :, :], rest[:, :, :], sel[:, :, :], ALU.not_equal))
            dve.wait_ge(pool_made, 2)
            link(nc.vector.tensor_tensor(weight[:, :, 0:E], prob[:, :, :], rest[:, :, :], ALU.mult))
            link(nc.vector.tensor_reduce(wsum[:, :], weight[:, :, 0:E], AX_X, ALU.add))
            link(nc.vector.reciprocal(wsum[:, :], wsum[:, :]))
            link(nc.vector.tensor_scalar(wsum[:, :], wsum[:, :], ROUTE_SCALE, None, ALU.mult))
            link(nc.vector.tensor_tensor(weight[:, :, 0:E], weight[:, :, 0:E],
                                         wsum[:, :].unsqueeze(2).to_broadcast([P, ST, E]), ALU.mult))
            link(nc.vector.tensor_copy(split[:, :, 0:EA], weight[:, :, :]))
            link(nc.vector.tensor_tensor(left[:, :, :], weight[:, :, :], split[:, :, 0:EA], ALU.subtract))
            link(nc.vector.tensor_copy(split[:, :, EA:2 * EA], left[:, :, :]))
            nc.vector.tensor_tensor(split[:, :, 2 * EA:3 * EA], left[:, :, :], split[:, :, EA:2 * EA],
                                    ALU.subtract).then_inc(split_ready, 1)
            dve.wait_ge(split_turned, 1)
            nc.vector.tensor_copy(splitT[:, :], ps[6][:, :].bitcast(BF16)).then_inc(split_kept, 1)

            def combine(n, half):
                dve.wait_ge(silu_ready, n + 1)
                dve.wait_ge(up_ready, n + 1)
                wait(dve, hw_ready, n - 1)
                nc.vector.tensor_tensor(h[:, half, :], silu[:, half, :], ps[4 + half][:, :], ALU.mult
                                        ).then_inc(h_ready, 1)
                dve.wait_ge(h_ready, n + 1)
                dve.wait_ge(spread_ready, n + 1)
                wait(dve, down_done, n - 1)
                nc.vector.tensor_tensor(hw[:, half, :], h[:, half, :], ps[6][:, :], ALU.mult
                                        ).then_inc(hw_ready, 1)

            for n in range(4):
                combine(n, n % 2)
            with dve.Fori(1, E // 2) as i:
                for k in range(4):
                    combine(4 * i + k, k % 2)
            for n in range(2 * E, 2 * EA):
                combine(n, n % 2)
            for j in range(2):
                dve.wait_ge(down_done, 2 * E + 1 + j)
                nc.vector.tensor_copy(yT[:, j * BANK:(j + 1) * BANK], ps[j][:, :]).then_inc(y_kept, 1)
            for j in range(2):
                dve.wait_ge(y_turned, j + 1)
                half = x[:, 4 * j:4 * j + 4, :]
                link(nc.vector.tensor_tensor(half, ps[2 + j][:, :].rearrange("p (t d) -> p t d", d=D),
                                             half, ALU.add))


HEADS = 16
HD = D // HEADS
PAIRS = HEADS // 2
SLOT = P // 2
PARTS = 3
K_PARTS = [(0, 0, 3), (1, 3, 2), (2, 5, 1)]
Q_PARTS = [(0, (0, 3, 5)), (1, (1, 4)), (2, (2,))]
MAX_ROW = 6 * HD


def head_rows(tile, blocks, count=1):
    return tile[:, :, blocks * HD:(blocks + count) * HD]


HG = 4
QT = BANK // P
ROWS = HG * QT


def turn_queries(pe, qn, identb, u, bank, done):
    for pair in range(HG // 2):
        for t in range(QT):
            at = (u * QT + t) * HG + 2 * pair
            mm = pe.transpose(bank.bitcast(BF16)[:, (pair * QT + t) * P:(pair * QT + t + 1) * P],
                              qn[:, bass.ds(at, 2), :].rearrange("p h r -> p (h r)"), identb[:, :])
    mm.then_inc(done, 1)


def padded(q, half):
    return q[SLOT * half:SLOT * half + SLOT, half:HG:2, :]


def turned(bank, half):
    return bank[SLOT * half:SLOT * half + SLOT, :].bitcast(BF16).rearrange("p (a q) -> p a q", a=HG // 2)


def project_keys(nc, g, a):
    GT = BANK // P
    KB, SBK = 4, 6
    GROUPS = PAIRS // 2
    SLICES = 16
    assert SLICES == ROWS
    with ExitStack() as ctx:
        def sb(name, shape, dt=F32):
            return ctx.enter_context(nc.sbuf_tensor(name, shape, dt))

        def sem(name):
            return ctx.enter_context(nc.semaphore(name))

        chunk = sb("p_chunk", [P, 2, GT, D])
        chunkT = sb("p_chunkT", [P, 2, BANK])
        kf = sb("p_kf", [P, 2, GT * HEADS, HD])
        left = sb("p_left", [P, 2, GT * HEADS, HD])
        kn = [sb(f"p_kn{i}", [P, GT * HEADS, SLOT], BF16) for i in range(2)]
        w_nat = sb("p_w", [P, 3, D])
        wT = sb("p_wT", [P, 3, D])
        bias = sb("p_bias", [P, 3, D])
        xn = sb("p_xn", [P, ST, D])
        xnT = sb("p_xnT", [P, S])
        qf = xn[:, :, :].rearrange("p t (h d) -> p t h d", d=HD)
        qleft = sb("p_qleft", [P, ST, HEADS, HD])
        stats = sb("p_stats", [P, ST, 6])
        mv = sb("p_mv", [P, ST, 2])
        rstd = sb("p_rstd", [P, ST])
        ps, x, kT, vn, qn = g["ps"], g["x"], g["kT"], g["vn"], g["qn"]
        qa, cmax = g["qa"], g["cmax0"]
        ident, identb = g["ident"], g["identb"]
        kT_flat = kT[:, :, :].rearrange("p a k -> p (a k)")
        qa_flat = qa[:, :, :].rearrange("p h q -> p (h q)")

        small_in = sem("p_small_in")
        chunk_in = [sem(f"p_chunk_in{i}") for i in range(2)]
        var_ready, std_ready, xn_ready = sem("p_var"), sem("p_std"), sem("p_xn_ready")
        w_turned, w_kept = sem("p_w_turned"), sem("p_w_kept")
        xn_turned, xnT_kept = sem("p_xn_turned"), sem("p_xnT_kept")
        q_ready, q_kept, q_scaled, q_split = sem("p_q_ready"), sem("p_q_kept"), sem("p_q_scaled"), sem("p_q_split")
        qa_turned, qa_kept = sem("p_qa_turned"), sem("p_qa_kept")
        made = sem("p_made")
        chunk_turned, chunkT_kept = sem("p_chunk_turned"), sem("p_chunkT_kept")
        kv_ready, k_kept, v_kept = sem("p_kv"), sem("p_k_kept"), sem("p_v_kept")
        part0, left_ready, part1, part2 = sem("p_part0"), sem("p_left_ready"), sem("p_part1"), sem("p_part2")
        keys_turned, kT_kept = sem("p_keys_turned"), sem("p_kT_kept")
        piece_ready, piece_maxed = sem("p_piece"), sem("p_maxed")
        dve_step, pool_step, pool_passed = sem("p_dve_step"), sem("p_pool_step"), sem("p_pool_passed")

        block = ctx.enter_context(nc.Block())
        LAST_TILES = KT - GT * NCH
        FULL = [P] * GT
        LAST = [P] * (LAST_TILES - 1) + [KR]
        LOOP_FROM, LOOP_TO = 1, 9

        def exists(c, ahead):
            return not isinstance(c, int) or 0 <= c + ahead <= NCH

        def tiles_of(c):
            return LAST if isinstance(c, int) and c == NCH else FULL

        def width(c):
            return CR if isinstance(c, int) and c == NCH else BANK

        @block.sync
        def _(sp):
            ctx_rows = a["ctx_1024"][0]

            def load_chunk(c, slot):
                sp.dma_start(chunk[:, slot, :, :],
                             ctx_rows[bass.ds(c * BANK, BANK), :].rearrange("(n p) d -> p n d", p=P)
                             ).then_inc(chunk_in[slot], 16)

            for j, name in enumerate(("q", "k", "v")):
                sp.dma_start(w_nat[:, j, :], a[f"L1_xattn_W{name}"]).then_inc(small_in, 16)
                sp.dma_start(bias[:, j, :], a[f"L1_xattn_b{name}"].partition_broadcast(P)).then_inc(small_in, 16)
            for c in range(2):
                load_chunk(c, c)
            with sp.Fori(1, NCH // 2) as i:
                for slot in range(2):
                    sp.wait_ge(chunk_turned, 2 * i + slot - 1)
                    load_chunk(2 * i + slot, slot)
            sp.wait_ge(chunk_turned, NCH - 1)
            sp.dma_start(chunk[:, 0, 0:LAST_TILES - 1, :],
                         ctx_rows[NCH * BANK:KF * P, :].rearrange("(n p) d -> p n d", p=P)
                         ).then_inc(chunk_in[0], 16)
            sp.dma_start(chunk[0:KR, 0, LAST_TILES - 1, :], ctx_rows[KF * P:NK, :]).then_inc(chunk_in[0], 16)

        def put_rows(tiles):
            return [(0, GT, P)] if len(tiles) == GT else [(0, len(tiles) - 1, P), (len(tiles) - 1, 1, KR)]

        def q_rows(hg, blk):
            return qn[:, hg * ST * HG:(hg + 1) * ST * HG, blk * HD:(blk + 1) * HD].rearrange(
                "p (t h) d -> p t h d", h=HG)

        def split_queries(eng, link, hg):
            heads = slice(HG * hg, HG * hg + HG)
            src = qf[:, :, heads, :]
            rest = qleft[:, :, heads, :]
            for part in range(PARTS):
                for blk in Q_PARTS[part][1]:
                    link(eng.tensor_copy(q_rows(hg, blk), src))
                if part < PARTS - 1:
                    link(eng.tensor_tensor(rest, src, q_rows(hg, Q_PARTS[part][1][0]), ALU.subtract))
                    src = rest

        @block.gpsimd
        def _(pool):
            link = Link(pool, pool_step)
            for i in range(2):
                nc.gpsimd.memset(kn[i][:, :, MAX_ROW:MAX_ROW + PARTS], 1.0).then_inc(made, 1)
                nc.gpsimd.memset(kn[i][:, :, MAX_ROW + PARTS:SLOT], 0.0).then_inc(made, 1)
            nc.gpsimd.memset(qn[:, :, MAX_ROW:SLOT], 0.0).then_inc(made, 1)
            nc.gpsimd.memset(vn[:, :, :, HD:HD + 1], 1.0).then_inc(made, 1)
            nc.gpsimd.memset(qa[:, :, :], 0.0).then_inc(made, 1)

            def leave(c, slot):
                wait_alone(pool, part0, c + 1, pool_passed)
                if not isinstance(c, int) or c >= 2:
                    wait_alone(pool, part2, c - 1, pool_passed)
                for first, n, rows in put_rows(tiles_of(c)):
                    hs = slice(first * HEADS, (first + n) * HEADS)
                    ins = nc.gpsimd.tensor_tensor(left[0:rows, slot, hs, :], kf[0:rows, slot, hs, :],
                                                  kn[slot][0:rows, hs, 0:HD], ALU.subtract)
                ins.then_inc(left_ready, 1)

            def third(c, slot):
                wait_alone(pool, part1, c + 1, pool_passed)
                wait_alone(pool, left_ready, c + 1, pool_passed)
                for first, n, rows in put_rows(tiles_of(c)):
                    hs = slice(first * HEADS, (first + n) * HEADS)
                    ins = nc.gpsimd.tensor_tensor(kn[slot][0:rows, hs, 5 * HD:6 * HD], left[0:rows, slot, hs, :],
                                                  kn[slot][0:rows, hs, 3 * HD:4 * HD], ALU.subtract)
                ins.then_inc(part2, 1)

            def step(c, slot):
                if exists(c, 1):
                    leave(c + 1, 1 - slot)
                    third(c + 1, 1 - slot)

            leave(0, 0)
            third(0, 0)
            step(0, 0)
            with pool.Fori(0, (LOOP_TO - LOOP_FROM) // 2) as i:
                for k in range(2):
                    step(2 * i + (LOOP_FROM + k), (LOOP_FROM + k) % 2)
            pool.wait_ge(q_scaled, 1)
            for c in range(LOOP_TO, NCH + 2):
                step(c, c % 2)
                hg = c - LOOP_TO + 1
                if hg < HEADS // HG:
                    split_queries(nc.gpsimd, link, hg)

        @block.tensor
        def _(pe):
            def turn_chunk(c, slot, loads):
                pe.wait_ge(chunk_in[slot], 16 * loads)
                wait(pe, chunkT_kept, c - 1)
                for j, rows in enumerate(tiles_of(c)):
                    mm = pe.transpose(ps[slot][:, j * P:j * P + rows], chunk[0:rows, slot, j, :],
                                      ident[0:rows, 0:rows])
                mm.then_inc(chunk_turned, 1)

            def project(c, slot, j):
                tiles = tiles_of(c)
                if j >= len(tiles):
                    return
                if j == 0:
                    pe.wait_ge(chunkT_kept, c + 1)
                    wait(pe, k_kept, c)
                    wait(pe, v_kept, c)
                rows = tiles[j]
                mm = pe.matmul(ps[2 + j // 2][0:rows, (j % 2) * 2 * D:(j % 2 + 1) * 2 * D],
                               chunkT[:, slot, j * P:j * P + rows], wT[:, 1:3, :], start=True, stop=True)
                if j == len(tiles) - 1:
                    mm.then_inc(kv_ready, 1)

            def turn_keys(c, slot, b, i):
                if i == 0:
                    if b == 0:
                        pe.wait_ge(part2, c + 1)
                    wait(pe, kT_kept, GROUPS * c + b - 1)
                for j, rows in enumerate(tiles_of(c)):
                    h0 = j * HEADS + 2 * (2 * b + i)
                    mm = pe.transpose(
                        ps[KB + b % 2][:, :].bitcast(BF16)[:, i * BANK + j * P:i * BANK + j * P + rows],
                        kn[slot][0:rows, h0:h0 + 2, :].rearrange("p h r -> p (h r)"), identb[0:rows, 0:rows])
                if i == 1:
                    mm.then_inc(keys_turned, 1)

            def piece(c, r):
                if r == 0:
                    pe.wait_ge(kT_kept, GROUPS * c + 1)
                pe.wait_ge(piece_maxed, ROWS * c + r + 1)
                n = width(c)
                pe.matmul(ps[SBK + r % 2][:, 0:n], qa_flat[:, r * P:(r + 1) * P],
                          kT_flat[:, bass.ds((r // (ROWS // 2)) * NK + c * BANK, n)],
                          start=True, stop=True).then_inc(piece_ready, 1)

            def step(c, slot):
                for k in range(SLICES):
                    if exists(c, -1):
                        piece(c - 1, k)
                    if exists(c, 1) and k < 4:
                        project(c + 1, 1 - slot, k)
                    if exists(c, 2) and k == 4:
                        n = turns(c, slot)
                        turn_chunk(c + 2, slot, n)
                    if exists(c, 0) and 5 <= k < 5 + 2 * GROUPS:
                        turn_keys(c, slot, (k - 5) // 2, (k - 5) % 2)

            now = [None]

            def turns(c, slot):
                if isinstance(c, int):
                    return (c + 2) // 2 + 1 + (c + 2 == NCH)
                return now[0] + ((LOOP_FROM + 2) // 2 + 1 if slot == LOOP_FROM % 2 else (LOOP_FROM + 3) // 2 + 1)

            def enter(i):
                now[0] = i

            pe.wait_ge(small_in, 96)
            for j in range(3):
                mm = pe.transpose(ps[7][:, j * D:(j + 1) * D], w_nat[:, j, :], ident[:, :])
            mm.then_inc(w_turned, 1)
            turn_chunk(0, 0, 1)
            turn_chunk(1, 1, 1)
            pe.wait_ge(w_kept, 1)
            for j in range(GT):
                project(0, 0, j)
            pe.wait_ge(xn_ready, ST)
            for t in range(ST):
                mm = pe.transpose(ps[4 + t // 4][:, (t % 4) * P:(t % 4 + 1) * P], xn[:, t, :], ident[:, :])
                if t % 4 == 3:
                    mm.then_inc(xn_turned, 1)
            pe.wait_ge(xnT_kept, 2)
            for t in range(ST):
                mm = pe.matmul(ps[6 + t // 4][:, (t % 4) * D:(t % 4 + 1) * D], xnT[:, t * P:(t + 1) * P],
                               wT[:, 0, :], start=True, stop=True)
                if t % 4 == 3:
                    mm.then_inc(q_ready, 1)
            step(0, 0)
            pe.wait_ge(q_split, 1)
            turn_queries(pe, qn, identb, 0, ps[SBK], qa_turned)
            pe.wait_ge(qa_kept, 2)
            with pe.Fori(0, (LOOP_TO - LOOP_FROM) // 2) as i:
                enter(i)
                for k in range(2):
                    step(2 * i + (LOOP_FROM + k), (LOOP_FROM + k) % 2)
            for c in range(LOOP_TO, NCH + 2):
                step(c, c % 2)

        @block.scalar
        def _(act):
            act.wait_ge(made, 7)

            def keep_chunk(c, slot):
                n = width(c)
                act.wait_ge(chunk_turned, c + 1)
                wait(act, kv_ready, c - 1)
                nc.scalar.activation(chunkT[:, slot, 0:n], ps[slot][:, 0:n], ACT.Copy).then_inc(chunkT_kept, 1)

            def first_part(c, slot):
                act.wait_ge(k_kept, c + 1)
                wait(act, keys_turned, GROUPS * (c - 1))
                for first, n, rows in put_rows(tiles_of(c)):
                    hs = slice(first * HEADS, (first + n) * HEADS)
                    ins = nc.scalar.activation(
                        kn[slot][0:rows, hs, 0:3 * HD].rearrange("p h (r d) -> p h r d", d=HD),
                        kf[0:rows, slot, hs, :].unsqueeze(2).to_broadcast([rows, n * HEADS, 3, HD]), ACT.Copy)
                ins.then_inc(part0, 1)

            def second_part(c, slot):
                act.wait_ge(left_ready, c + 1)
                for first, n, rows in put_rows(tiles_of(c)):
                    hs = slice(first * HEADS, (first + n) * HEADS)
                    ins = nc.scalar.activation(
                        kn[slot][0:rows, hs, 3 * HD:5 * HD].rearrange("p h (r d) -> p h r d", d=HD),
                        left[0:rows, slot, hs, :].unsqueeze(2).to_broadcast([rows, n * HEADS, 2, HD]), ACT.Copy)
                ins.then_inc(part1, 1)

            def keep(c, b):
                n = width(c)
                act.wait_ge(keys_turned, GROUPS * c + b + 1)
                nc.scalar.activation(
                    kT[:, 2 * b:2 * b + 2, bass.ds(c * BANK, n)],
                    ps[KB + b % 2][:, :].bitcast(BF16).rearrange("p (i n) -> p i n", i=2)[:, :, 0:n],
                    ACT.Copy).then_inc(kT_kept, 1)

            def step(c, slot):
                if exists(c, 1):
                    first_part(c + 1, 1 - slot)
                if exists(c, 2):
                    keep_chunk(c + 2, slot)
                if exists(c, 0):
                    keep(c, 0)
                    keep(c, 1)
                if exists(c, 1):
                    second_part(c + 1, 1 - slot)
                if exists(c, 0):
                    keep(c, 2)
                    keep(c, 3)

            act.wait_ge(var_ready, 1)
            nc.scalar.activation(rstd[:, :], rstd[:, :], ACT.Sqrt).then_inc(std_ready, 1)
            keep_chunk(0, 0)
            keep_chunk(1, 1)
            first_part(0, 0)
            second_part(0, 0)
            step(0, 0)
            act.wait_ge(qa_turned, 1)
            nc.scalar.activation(padded(qa, 1), turned(ps[SBK], 1), ACT.Copy).then_inc(qa_kept, 1)
            with act.Fori(0, (LOOP_TO - LOOP_FROM) // 2) as i:
                for k in range(2):
                    step(2 * i + (LOOP_FROM + k), (LOOP_FROM + k) % 2)
            for c in range(LOOP_TO, NCH + 2):
                step(c, c % 2)

        @block.vector
        def _(dve):
            link = Link(dve, dve_step)

            def keep_kv(c, slot):
                dve.wait_ge(kv_ready, c + 1)
                wait(dve, left_ready, c - 1)
                todo = []
                for first, n, rows in put_rows(tiles_of(c)):
                    while n > 0:
                        m = min(n, 2 - first % 2)
                        todo.append((first, m, rows))
                        first, n = first + m, n - m
                for what in range(2):
                    for first, m, rows in todo:
                        src = ps[2 + first // 2][0:rows, (first % 2) * 2 * D:(first % 2 + m) * 2 * D].rearrange(
                            "p (j w d) -> p j w d", w=2, d=D)[:, :, what, :]
                        b = bias[0:rows, 1 + what:2 + what, :].to_broadcast([rows, m, D])
                        if what == 0:
                            dst = kf[0:rows, slot, first * HEADS:(first + m) * HEADS, :].rearrange(
                                "p (j h) d -> p j (h d)", h=HEADS)
                            ins = nc.vector.tensor_tensor(dst, src, b, ALU.add)
                        else:
                            dst = vn[0:rows, bass.ds(c * GT + first, m), :, 0:HD]
                            ins = nc.vector.tensor_tensor(
                                dst, src.rearrange("p j (h d) -> p j h d", d=HD),
                                b.rearrange("p j (h d) -> p j h d", d=HD), ALU.add)
                    ins.then_inc((k_kept, v_kept)[what], 1)

            def reduce_piece(c, r):
                dve.wait_ge(piece_ready, ROWS * c + r + 1)
                nc.vector.tensor_reduce(cmax[:, r, bass.ds(c, 1)], ps[SBK + r % 2][:, 0:width(c)], AX_X,
                                        ALU.max).then_inc(piece_maxed, 1)

            def step(c, slot):
                for k in range(SLICES):
                    if exists(c, -1):
                        reduce_piece(c - 1, k)
                    if exists(c, 1) and k == 4:
                        keep_kv(c + 1, 1 - slot)
    
            dve.sem_inc(piece_maxed, 2)
            layer_norm_stats(nc, link, x, stats, mv, rstd, ST, var_ready)
            dve.wait_ge(w_turned, 1)
            nc.vector.tensor_copy(wT[:, :, :], ps[7][:, 0:3 * D].rearrange("p (j d) -> p j d", d=D)
                                  ).then_inc(w_kept, 1)
            dve.wait_ge(std_ready, 1)
            layer_norm_apply(nc, link, xn, x, mv, rstd, ST, xn_ready)
            dve.wait_ge(made, 7)
            dve.wait_ge(small_in, 96)
            keep_kv(0, 0)
            for j in range(2):
                dve.wait_ge(xn_turned, j + 1)
                nc.vector.tensor_copy(xnT[:, j * BANK:(j + 1) * BANK], ps[4 + j][:, :]).then_inc(xnT_kept, 1)
            for j in range(2):
                dve.wait_ge(q_ready, j + 1)
                half = xn[:, 4 * j:4 * j + 4, :]
                nc.vector.tensor_tensor(half, ps[6 + j][:, :].rearrange("p (t d) -> p t d", d=D),
                                        bias[:, 0:1, :].to_broadcast([P, 4, D]), ALU.add).then_inc(q_kept, 1)
            dve.wait_ge(q_kept, 2)
            nc.vector.tensor_scalar(xn[:, :, :], xn[:, :, :], float(HD) ** -0.5, None, ALU.mult).then_inc(q_scaled, 1)
            dve.wait_ge(q_scaled, 1)
            split_queries(nc.vector, link, 0)
            dve.sem_inc(q_split, 1)
            step(0, 0)
            dve.wait_ge(qa_turned, 1)
            nc.vector.tensor_copy(padded(qa, 0), turned(ps[SBK], 0)).then_inc(qa_kept, 1)
            with dve.Fori(0, (LOOP_TO - LOOP_FROM) // 2) as i:
                for k in range(2):
                    step(2 * i + (LOOP_FROM + k), (LOOP_FROM + k) % 2)
            for c in range(LOOP_TO, NCH + 2):
                step(c, c % 2)


def cross_attention_1(nc, g, a):
    QH = S // BANK
    PIECES = 16
    PN = -(-NK // PIECES)
    MB = 4
    STEPS = HG * KT
    SB, PB, VB = 3, 12, 3
    TILES = 3
    PER = TILES * HG
    HEAD = 2
    MAXB, SCB, ACC = 0, 4, 7
    assert PER % SB == 0 and PER % PB == 0 and TILES % VB == 0 and HEAD + ROWS * TILES + 1 == KT
    with ExitStack() as ctx:
        def sb(name, shape, dt=F32):
            return ctx.enter_context(nc.sbuf_tensor(name, shape, dt))

        def sem(name):
            return ctx.enter_context(nc.semaphore(name))

        qb = sb("x_qb", [P, QH, HG, BANK], BF16)
        probs = sb("x_probs", [P, PB, BANK])
        vt = sb("x_vt", [P, VB, HG, 32])
        cmax = sb("x_cmax", [P, ROWS, PIECES])
        nmax = sb("x_nmax", [P, ROWS])
        mleft = sb("x_mleft", [P, ROWS])
        oT = sb("x_oT", [P, BANK])
        rtotal = sb("x_rtotal", [P, QT, HG])
        ps, big = g["ps"], g["big"]
        kT, vn, qn, on, qa = g["kT"], g["vn"], g["qn"], g["on"], g["qa"]
        ident, identb = g["ident"], g["identb"]
        kT_flat = kT[:, :, :].rearrange("p a k -> p (a k)")
        qa_flat = qa[:, :, :].rearrange("p h q -> p (h q)")

        zeroed = sem("x_zeroed")
        qa_turned, qa_kept, qb_turned, qb_kept = sem("x_qat"), sem("x_qak"), sem("x_qbt"), sem("x_qbk")
        piece_ready, piece_maxed, max_split = sem("x_piece"), sem("x_maxed"), sem("x_max_split")
        scores_ready, probs_ready, pv_done = sem("x_scores"), sem("x_probs_ready"), sem("x_pv")
        v_ready, oT_kept, o_turned, o_done = sem("x_v"), sem("x_oT_kept"), sem("x_o_turned"), sem("x_o_done")
        dve_step = sem("x_dve_step")
        pe_passed, pool_passed = sem("x_pe_passed"), sem("x_pool_passed")

        block = ctx.enter_context(nc.Block())

        def tile_rows(kt):
            return P if kt < KF else KR

        @block.gpsimd
        def _(pool):
            nc.gpsimd.memset(qb[:, 0, :, :], 0.0).then_inc(zeroed, 1)
            nc.gpsimd.memset(vt[:, :, :, :], 0.0).then_inc(zeroed, 1)
            nc.gpsimd.memset(qb[:, 1, :, :], 0.0).then_inc(zeroed, 1)
            pool.wait_ge(zeroed, 3)

            def fetch(u, hg, kt, slot, rows=P):
                back = HG * (kt - VB + 1)
                wait_alone(pool, pv_done, u * STEPS + 1 + (max(back, 0) if isinstance(back, int) else back),
                           pool_passed)
                nc.gpsimd.tensor_copy(
                    vt[0:rows, slot, :, 0:HD + 1],
                    vn[0:rows, bass.ds(kt, 1), bass.ds(hg * HG, HG), :].rearrange("p t h d -> p (t h) d")
                ).then_inc(v_ready, 1)

            with pool.Fori(0, HEADS // HG) as hg:
                for qh in range(QH):
                    u = hg * QH + qh
                    for kt in range(VB):
                        fetch(u, hg, kt, kt)
                    with pool.Fori(1, KT // VB - 1) as i:
                        for j in range(VB):
                            fetch(u, hg, VB * i + j, j)
                    for kt in range(KT - VB, KT):
                        fetch(u, hg, kt, kt % VB, tile_rows(kt))

        @block.tensor
        def _(pe):
            pe.sem_inc(pv_done, 1)

            def piece(u, hg, half, r, j):
                row = half * (ROWS // 2) + r
                pe.wait_ge(piece_maxed, ((u - 1) * ROWS + row) * PIECES + j + 1)
                pe.matmul(ps[MAXB + j % MB][:, 0:PN], qa_flat[:, bass.ds(row * P, P)],
                          kT_flat[:, bass.ds((hg * 2 + half) * NK + min(j * PN, NK - PN), PN)],
                          start=True, stop=True).then_inc(piece_ready, 1)

            def score(u, qh, hg, n, kt, s, rows=P):
                h = s % HG
                back = n - SB + 1
                value = u * STEPS + 1 + (max(back, 0) if isinstance(back, int) else back)
                if rows < P:
                    wait_alone(pe, probs_ready, value, pe_passed)
                else:
                    pe.wait_ge(probs_ready, value)
                pe.matmul(ps[SCB + s % SB][0:rows, :],
                          kT_flat[:, bass.ds((hg * 2 + h // 2) * NK + kt * P, rows)],
                          qb[:, qh, h, :], start=True, stop=True).then_inc(scores_ready, 1)

            def weigh(u, kt, s, rows=P):
                if isinstance(kt, int) and kt == 0:
                    wait_alone(pe, o_done, u + 1, pe_passed)
                for h in range(HG):
                    pe.matmul(ps[ACC][32 * h:32 * h + 32, :], vt[0:rows, s % VB, h, :],
                              probs[0:rows, (s * HG + h) % PB, :], start=isinstance(kt, int) and kt == 0,
                              stop=isinstance(kt, int) and kt == KT - 1,
                              skip_group_check=True).then_inc(pv_done, 1)

            def unit(u, qh, hg, next_u=None, next_hg=None, after=None):
                pe.wait_ge(qb_kept, 2 * u + 2)
                for kt in range(HEAD):
                    for h in range(HG):
                        score(u, qh, hg, kt * HG + h, kt, kt * HG + h)
                    if kt > 0:
                        weigh(u, kt - 1, kt - 1)
                if next_u is not None:
                    wait_alone(pe, qa_kept, 2 * next_u, pe_passed)
                with pe.Fori(0, 2) as half:
                    with pe.Fori(0, ROWS // 2) as r:
                        i = half * (ROWS // 2) + r
                        pieces = 0
                        for k in range(TILES):
                            s = HEAD + k
                            for h in range(HG):
                                score(u, qh, hg, i * PER + s * HG + h, i * TILES + s, s * HG + h)
                                while next_u is not None and (k * HG + h + 1) * PIECES > pieces * PER:
                                    piece(next_u, next_hg, half, r, pieces)
                                    pieces += 1
                            weigh(u, i * TILES + s - 1, s - 1)
                for h in range(HG):
                    score(u, qh, hg, (KT - 1) * HG + h, KT - 1, (KT - 1) * HG + h, KR)
                weigh(u, KT - 2, KT - 2)
                if next_u is not None:
                    wait_alone(pe, max_split, next_u + 1, pe_passed)
                    turn_queries(pe, qn, identb, next_u, ps[MAXB], qb_turned)
                if after is not None:
                    turn_queries(pe, qn, identb, after, ps[MAXB + 2], qa_turned)
                wait_alone(pe, probs_ready, (u + 1) * STEPS + 1, pe_passed)
                weigh(u, KT - 1, KT - 1, KR)
                pe.wait_ge(oT_kept, u + 1)
                for t in range(QT):
                    mm = pe.transpose(ps[ACC][:, t * P:(t + 1) * P], oT[:, t * P:(t + 1) * P], ident[:, :])
                mm.then_inc(o_turned, 1)

            pe.wait_ge(max_split, 1)
            turn_queries(pe, qn, identb, 0, ps[MAXB], qb_turned)
            turn_queries(pe, qn, identb, 1, ps[MAXB + 2], qa_turned)
            G = HEADS // HG
            with pe.Fori(0, G - 1) as hg:
                unit(hg * QH, 0, hg, hg * QH + 1, hg, hg * QH + 2)
                unit(hg * QH + 1, 1, hg, hg * QH + 2, hg + 1, hg * QH + 3)
            unit((G - 1) * QH, 0, G - 1, (G - 1) * QH + 1, G - 1)
            unit((G - 1) * QH + 1, 1, G - 1)

        @block.scalar
        def _(act):
            def keep_queries(n, q, bank, done, kept):
                act.wait_ge(done, n + 1)
                nc.scalar.activation(padded(q, 1), turned(ps[bank], 1), ACT.Copy).then_inc(kept, 1)

            def exp(u, n, s, rows=P):
                act.wait_ge(scores_ready, u * STEPS + n + 1)
                if s % HG == 0:
                    back = n + HG - PB
                    act.wait_ge(pv_done, u * STEPS + 1 + (max(back, 0) if isinstance(back, int) else back))
                if s % HG == 1:
                    act.wait_ge(v_ready, u * KT + (n - 1) // HG + 1 if isinstance(n, int) else
                                u * KT + v_at[0] + s // HG + 1)
                nc.scalar.activation(probs[0:rows, s % PB, :], ps[SCB + s % SB][0:rows, :], ACT.Exp
                                     ).then_inc(probs_ready, 1)

            v_at = [None]

            def unit(u, nxt=True, after=True):
                for n in range(PER):
                    exp(u, n, n)
                with act.Fori(1, STEPS // PER - 1) as i:
                    v_at[0] = i * TILES
                    for s in range(PER):
                        exp(u, i * PER + s, s)
                for n in range(STEPS - PER, STEPS):
                    exp(u, n, n, tile_rows(n // HG))

            act.sem_inc(probs_ready, 1)
            act.wait_ge(zeroed, 1)
            keep_queries(0, qb[:, 0], MAXB, qb_turned, qb_kept)
            act.wait_ge(zeroed, 3)
            keep_queries(0, qa, MAXB + 2, qa_turned, qa_kept)
            G = HEADS // HG

            def between(u, qh, last=False):
                keep_queries(u + 1, qb[:, 1 - qh], MAXB, qb_turned, qb_kept)
                if not last:
                    keep_queries(u + 1, qa, MAXB + 2, qa_turned, qa_kept)

            with act.Fori(0, G - 1) as hg:
                for qh in range(QH):
                    unit(hg * QH + qh)
                    between(hg * QH + qh, qh)
            unit((G - 1) * QH)
            between((G - 1) * QH, 0, last=True)
            unit((G - 1) * QH + 1)

        @block.vector
        def _(dve):
            link = Link(dve, dve_step)

            def keep_queries(n, q, bank, done, kept):
                dve.wait_ge(done, n + 1)
                nc.vector.tensor_copy(padded(q, 0), turned(ps[bank], 0)).then_inc(kept, 1)

            def maxima(u):
                with dve.Fori(0, ROWS) as row:
                    for j in range(PIECES):
                        dve.wait_ge(piece_ready, ((u - 1) * ROWS + row) * PIECES + j + 1)
                        nc.vector.tensor_reduce(
                            cmax[:, bass.ds(row, 1), j:j + 1].rearrange("p r j -> p (r j)"),
                            ps[MAXB + j % MB][:, 0:PN], AX_X, ALU.max).then_inc(piece_maxed, 1)
                dve.wait_ge(piece_maxed, u * ROWS * PIECES + MB)
                split_maxima(u, cmax)

            def split_maxima(u, cmax):
                link(nc.vector.tensor_reduce(nmax[:, :], cmax[:, :, :], AX_X, ALU.max, negate=True))

                def row_of(part):
                    return qn[:, bass.ds(u * ROWS, ROWS), MAX_ROW + part:MAX_ROW + part + 1].rearrange(
                        "p (t h) o -> p h (t o)", h=HG)

                def by_head(v):
                    return v[:, :].rearrange("p (h t) -> p h t", h=HG)

                link(nc.vector.tensor_copy(row_of(0), by_head(nmax)))
                link(nc.vector.tensor_tensor(by_head(mleft), by_head(nmax), row_of(0), ALU.subtract))
                link(nc.vector.tensor_copy(row_of(1), by_head(mleft)))
                nc.vector.tensor_tensor(row_of(2), by_head(mleft), row_of(1), ALU.subtract
                                        ).then_inc(max_split, 1)

            def outputs(u, qh, hg):
                dve.wait_ge(pv_done, (u + 1) * STEPS + 1)
                nc.vector.tensor_copy(oT[:, :], ps[ACC][:, :]).then_inc(oT_kept, 1)
                dve.wait_ge(o_turned, u + 1)
                o = ps[ACC][:, :].rearrange("p (t h r) -> p t h r", t=QT, h=HG)
                link(nc.vector.reciprocal(rtotal[:, :, :], o[:, :, :, HD:HD + 1].rearrange("p t h o -> p t (h o)")))
                nc.vector.tensor_tensor(
                    on[:, qh * QT:(qh + 1) * QT, bass.ds(hg * HG, HG), :], o[:, :, :, 0:HD],
                    rtotal[:, :, :].unsqueeze(3).to_broadcast([P, QT, HG, HD]), ALU.mult).then_inc(o_done, 1)

            dve.sem_inc(piece_maxed, MB)
            dve.sem_inc(o_done, 1)
            dve.wait_ge(zeroed, 1)
            split_maxima(0, g["cmax0"])
            keep_queries(0, qb[:, 0], MAXB, qb_turned, qb_kept)
            dve.wait_ge(zeroed, 3)
            keep_queries(0, qa, MAXB + 2, qa_turned, qa_kept)
            G = HEADS // HG

            def unit(u, qh, hg, last=False):
                maxima(u + 1)
                keep_queries(u + 1, qb[:, 1 - qh], MAXB, qb_turned, qb_kept)
                outputs(u, qh, hg)
                if not last:
                    keep_queries(u + 1, qa, MAXB + 2, qa_turned, qa_kept)

            PER_UNIT = 5
            with dve.Fori(0, G - 1) as hg:
                link.enter(hg, QH * PER_UNIT)
                for qh in range(QH):
                    unit(hg * QH + qh, qh, hg)
            link.leave(G - 1)
            unit((G - 1) * QH, 0, G - 1, last=True)
            outputs((G - 1) * QH + 1, 1, G - 1)


def moe_by_argmax(nc, g, a, out):
    PATHS, DM = 9, D // 4
    LOADS = 14
    HW = PATHS * DM
    KC = [(0, P), (P, P), (2 * P, HW + PATHS - 2 * P)]
    with ExitStack() as ctx:
        def sb(name, shape, dt=F32):
            return ctx.enter_context(nc.sbuf_tensor(name, shape, dt))

        def sem(name):
            return ctx.enter_context(nc.semaphore(name))

        wo_nat = sb("f_wo", [P, D])
        woT = sb("f_woT", [P, D])
        bo = sb("f_bo", [P, 1, D])
        onT = sb("f_onT", [P, S])
        y = sb("f_y", [P, ST, D])
        yT = sb("f_yT", [P, S + 2])
        mixw = sb("f_mixw", [P, 3])
        mixT = sb("f_mixT", [P, S])
        w1 = sb("f_w1", [P, HW + DM])
        b1 = sb("f_b1", [P, HW + DM])
        w2 = sb("f_w2", [P, 3, D])
        wo2 = sb("f_wo2", [DM, PATHS])
        bo2 = sb("f_bo2", [P, 1, PATHS])
        gb = sb("f_gb", [P, 2, D])
        hid = sb("f_hid", [P, ST, HW + DM])
        tanhT = sb("f_tanhT", [DM, S])
        score = sb("f_score", [P, ST, PATHS])
        top = sb("f_top", [P, ST, 8])
        top_at = sb("f_top_at", [P, ST, 8], U32)
        best = sb("f_best", [P, ST])
        iota = sb("f_iota", [P, PATHS])
        kept = sb("f_kept", [P, ST, HW + PATHS])
        keptT = sb("f_keptT", [P, 2, 3, P])
        z = sb("f_z", [P, ST, D])
        stats = sb("f_stats", [P, ST, 6])
        mv = sb("f_mv", [P, ST, 2])
        rstd = sb("f_rstd", [P, ST])
        ps, x, on, ident = g["ps"], g["x"], g["on"], g["ident"]

        small_in, made = sem("f_small_in"), sem("f_made")
        wo_turned, wo_kept, on_turned, onT_kept = sem("f_wt"), sem("f_wk"), sem("f_ot"), sem("f_ok")
        attn_ready = sem("f_attn")
        var_ready, std_ready, y_ready = sem("f_var"), sem("f_std"), sem("f_y_ready")
        y_turned, yT_kept, mix_ready = sem("f_yt"), sem("f_yk"), sem("f_mix")
        hid_ready, hid_kept, tanh_ready = sem("f_hid_ready"), sem("f_hid_kept"), sem("f_tanh")
        tanh_turned, tanhT_kept, score_ready = sem("f_tt"), sem("f_tk"), sem("f_score_ready")
        chosen, kept_turned, keptT_kept = sem("f_chosen"), sem("f_kt"), sem("f_kk")
        path_done, var2_ready, std2_ready = sem("f_path"), sem("f_var2"), sem("f_std2")
        normed, out_ready, out_done = sem("f_normed"), sem("f_out_ready"), sem("f_out_done")
        dve_step = sem("f_dve_step")

        block = ctx.enter_context(nc.Block())

        @block.sync
        def _(sp):
            loads = [
                (wo_nat[:, :], a["L1_xattn_Wo"]),
                (bo[:, 0, :], a["L1_xattn_bo"].partition_broadcast(P)),
                (mixw[:, :], a["L1_ffn_mix_kernel"].rearrange("j d -> d j")),
                (w1[:, 0:HW].rearrange("d (p m) -> d p m", p=PATHS), a["L1_ffn_W1"].rearrange("p d m -> d p m")),
                (w1[:, HW:HW + DM], a["L1_ffn_Wo1"]),
                (b1[:, 0:HW], a["L1_ffn_b1"].rearrange("p m -> (p m)").partition_broadcast(P)),
                (b1[:, HW:HW + DM], a["L1_ffn_bo1"].partition_broadcast(P)),
                (w2[:, 0:2, :], a["L1_ffn_W2"].rearrange("p m d -> (p m) d")[0:2 * P, :].rearrange(
                    "(c k) d -> k c d", k=P)),
                (w2[0:HW - 2 * P, 2, :], a["L1_ffn_W2"].rearrange("p m d -> (p m) d")[2 * P:HW, :]),
                (w2[HW - 2 * P:HW - 2 * P + PATHS, 2, :], a["L1_ffn_b2"]),
                (wo2[:, :], a["L1_ffn_Wo2"]),
                (bo2[:, 0, :], a["L1_ffn_bo2"].partition_broadcast(P)),
                (gb[:, 0, :], a["L1_ffn_gamma"].partition_broadcast(P)),
                (gb[:, 1, :], a["L1_ffn_beta"].partition_broadcast(P)),
            ]
            assert len(loads) == LOADS
            with nc.allow_non_contiguous_dma(reason="small weights"):
                for dst, src in loads:
                    sp.dma_start(dst, src).then_inc(small_in, 16)
            out_v = out.rearrange("b (t p) d -> p (b t) d", p=P)
            for j in range(2):
                sp.wait_ge(out_ready, j + 1)
                sp.dma_start(out_v[:, 4 * j:4 * j + 4, :], z[:, 4 * j:4 * j + 4, :]).then_inc(out_done, 16)
            sp.wait_ge(out_done, 32)

        @block.gpsimd
        def _(pool):
            nc.gpsimd.memset(yT[:, 0:1], 0.0).then_inc(made, 1)
            nc.gpsimd.memset(yT[:, S + 1:S + 2], 0.0).then_inc(made, 1)
            nc.gpsimd.iota(iota[:, :], pattern=[[1, PATHS]], base=0, channel_multiplier=0,
                           allow_small_or_imprecise_dtypes=True).then_inc(made, 1)

        @block.tensor
        def _(pe):
            pe.wait_ge(small_in, 16 * LOADS)
            pe.transpose(ps[2][:, 0:D], wo_nat[:, :], ident[:, :]).then_inc(wo_turned, 1)
            for t in range(ST):
                mm = pe.transpose(ps[t // 4][:, (t % 4) * P:(t % 4 + 1) * P],
                                  on[:, t, :, :].rearrange("p h d -> p (h d)"), ident[:, :])
                if t % 4 == 3:
                    mm.then_inc(on_turned, 1)
            pe.wait_ge(wo_kept, 1)
            for t in range(ST):
                if t % 4 == 0:
                    pe.wait_ge(onT_kept, t // 4 + 1)
                mm = pe.matmul(ps[4 + t // 4][:, (t % 4) * D:(t % 4 + 1) * D], onT[:, t * P:(t + 1) * P],
                               woT[:, :], start=True, stop=True)
                if t % 4 == 3:
                    mm.then_inc(attn_ready, 1)
            pe.wait_ge(y_ready, ST)
            for t in range(ST):
                mm = pe.transpose(ps[t // 4][:, (t % 4) * P:(t % 4 + 1) * P], y[:, t, :], ident[:, :])
                if t % 4 == 3:
                    mm.then_inc(y_turned, 1)
            pe.wait_ge(mix_ready, 1)
            for t in range(ST):
                if t >= 4:
                    pe.wait_ge(hid_kept, t - 3)
                pe.matmul(ps[t % 4][:, 0:HW + DM], mixT[:, t * P:(t + 1) * P], w1[:, :], start=True,
                          stop=True).then_inc(hid_ready, 1)
            for t in range(ST):
                pe.wait_ge(tanh_ready, t + 1)
                mm = pe.transpose(ps[4 + t // 4][0:DM, (t % 4) * P:(t % 4 + 1) * P], hid[:, t, HW:HW + DM],
                                  ident[:, :])
                if t % 4 == 3:
                    mm.then_inc(tanh_turned, 1)
            for t in range(ST):
                if t % 4 == 0:
                    pe.wait_ge(tanhT_kept, t // 4 + 1)
                mm = pe.matmul(ps[6][:, t * PATHS:(t + 1) * PATHS], tanhT[:, t * P:(t + 1) * P], wo2[:, :],
                               start=True, stop=True)
            mm.then_inc(score_ready, 1)

            def turn_kept(t):
                pe.wait_ge(chosen, t + 1)
                wait(pe, keptT_kept, t - 1)
                for c, (k0, k) in enumerate(KC):
                    mm = pe.transpose(ps[t % 2][0:k, c * P:(c + 1) * P], kept[:, t, k0:k0 + k], ident[:, :])
                mm.then_inc(kept_turned, 1)

            turn_kept(0)
            for t in range(ST):
                if t + 1 < ST:
                    turn_kept(t + 1)
                pe.wait_ge(keptT_kept, t + 1)
                for c, (k0, k) in enumerate(KC):
                    mm = pe.matmul(ps[4 + t // 4][:, (t % 4) * D:(t % 4 + 1) * D], keptT[0:k, t % 2, c, :],
                                   w2[0:k, c, :], start=(c == 0), stop=(c == 2))
                mm.then_inc(path_done, 1)

        @block.scalar
        def _(act):
            act.wait_ge(var_ready, 1)
            nc.scalar.activation(rstd[:, :], rstd[:, :], ACT.Sqrt).then_inc(std_ready, 1)
            for t in range(ST):
                act.wait_ge(hid_kept, t + 1)
                nc.scalar.activation(hid[:, t, HW:HW + DM], hid[:, t, HW:HW + DM], ACT.Tanh
                                     ).then_inc(tanh_ready, 1)
            for t in range(ST):
                act.wait_ge(kept_turned, t + 1)
                wait(act, path_done, t - 1)
                nc.scalar.activation(keptT[:, t % 2, 0:2, :], ps[t % 2][:, 0:2 * P].rearrange(
                    "p (c q) -> p c q", c=2), ACT.Copy)
                k = KC[2][1]
                nc.scalar.activation(keptT[0:k, t % 2, 2, :], ps[t % 2][0:k, 2 * P:3 * P], ACT.Copy
                                     ).then_inc(keptT_kept, 1)
            act.wait_ge(var2_ready, 1)
            nc.scalar.activation(rstd[:, :], rstd[:, :], ACT.Sqrt).then_inc(std2_ready, 1)

        @block.vector
        def _(dve):
            link = Link(dve, dve_step)

            def tiles_of(bank):
                return ps[bank][:, :].rearrange("p (t d) -> p t d", d=D)

            dve.wait_ge(wo_turned, 1)
            nc.vector.tensor_copy(woT[:, :], ps[2][:, 0:D]).then_inc(wo_kept, 1)
            for j in range(2):
                dve.wait_ge(on_turned, j + 1)
                nc.vector.tensor_copy(onT[:, j * BANK:(j + 1) * BANK], ps[j][:, :]).then_inc(onT_kept, 1)
            dve.wait_ge(small_in, 16 * LOADS)
            link(nc.vector.tensor_tensor(x[:, :, :], x[:, :, :], bo[:, :, :].to_broadcast([P, ST, D]), ALU.add))
            for j in range(2):
                dve.wait_ge(attn_ready, j + 1)
                half = x[:, 4 * j:4 * j + 4, :]
                link(nc.vector.tensor_tensor(half, tiles_of(4 + j), half, ALU.add))
            layer_norm_stats(nc, link, x, stats, mv, rstd, ST, var_ready)
            dve.wait_ge(std_ready, 1)
            layer_norm_apply(nc, link, y, x, mv, rstd, ST, y_ready)
            for j in range(2):
                dve.wait_ge(y_turned, j + 1)
                nc.vector.tensor_copy(yT[:, 1 + j * BANK:1 + (j + 1) * BANK], ps[j][:, :]).then_inc(yT_kept, 1)
            dve.wait_ge(yT_kept, 2)
            dve.wait_ge(made, 3)
            link(nc.vector.tensor_scalar(mixT[:, :], yT[:, 1:S + 1], mixw[:, 1:2], None, ALU.mult))
            link(nc.vector.scalar_tensor_tensor(out=mixT[:, :], in0=yT[:, 0:S], scalar=mixw[:, 0:1],
                                                in1=mixT[:, :], op0=ALU.mult, op1=ALU.add))
            nc.vector.scalar_tensor_tensor(out=mixT[:, :], in0=yT[:, 2:S + 2], scalar=mixw[:, 2:3],
                                           in1=mixT[:, :], op0=ALU.mult, op1=ALU.add).then_inc(mix_ready, 1)
            for t in range(ST):
                dve.wait_ge(hid_ready, t + 1)
                nc.vector.tensor_tensor(hid[:, t, :], ps[t % 4][:, 0:HW + DM], b1[:, :], ALU.add
                                        ).then_inc(hid_kept, 1)
            for j in range(2):
                dve.wait_ge(tanh_turned, j + 1)
                nc.vector.tensor_copy(tanhT[:, j * BANK:(j + 1) * BANK], ps[4 + j][0:DM, :]).then_inc(tanhT_kept, 1)
            dve.wait_ge(score_ready, 1)
            link(nc.vector.tensor_tensor(score[:, :, :], ps[6][:, 0:ST * PATHS].rearrange(
                "p (t e) -> p t e", e=PATHS), bo2[:, :, :].to_broadcast([P, ST, PATHS]), ALU.add))
            for t in range(ST):
                link(nc.vector.max(out=top[:, t, :], in_=score[:, t, :]))
            for t in range(ST):
                link(nc.vector.max_index(out=top_at[:, t, :], in_max=top[:, t, :], in_values=score[:, t, :]))
            link(nc.vector.tensor_copy(best[:, :], top_at[:, :, 0]))
            link(nc.vector.tensor_tensor(kept[:, :, HW:HW + PATHS],
                                         iota[:, :].unsqueeze(1).to_broadcast([P, ST, PATHS]),
                                         best[:, :].unsqueeze(2).to_broadcast([P, ST, PATHS]), ALU.is_equal))
            dve.wait_ge(hid_kept, ST)
            for t in range(ST):
                nc.vector.tensor_tensor(
                    kept[:, t, 0:HW].rearrange("p (e m) -> p e m", e=PATHS),
                    hid[:, t, 0:HW].rearrange("p (e m) -> p e m", e=PATHS),
                    kept[:, t, HW:HW + PATHS].unsqueeze(2).to_broadcast([P, PATHS, DM]), ALU.mult
                ).then_inc(chosen, 1)
            for j in range(2):
                dve.wait_ge(path_done, 4 * j + 4)
                link(nc.vector.tensor_tensor(z[:, 4 * j:4 * j + 4, :], tiles_of(4 + j),
                                             y[:, 4 * j:4 * j + 4, :], ALU.add))
            layer_norm_stats(nc, link, z, stats, mv, rstd, ST, var2_ready)
            dve.wait_ge(std2_ready, 1)
            layer_norm_apply(nc, link, z, z, mv, rstd, ST, normed)
            dve.wait_ge(normed, ST)
            for j in range(2):
                half = z[:, 4 * j:4 * j + 4, :]
                link(nc.vector.tensor_tensor(half, half, gb[:, 0:1, :].to_broadcast([P, 4, D]), ALU.mult))
                link(nc.vector.tensor_tensor(half, half, gb[:, 1:2, :].to_broadcast([P, 4, D]), ALU.add))
                nc.vector.tensor_tensor(half, half, x[:, 4 * j:4 * j + 4, :], ALU.add).then_inc(out_ready, 1)


def build(nc, a, out, stop=None):
    with ExitStack() as ctx:
        big = ctx.enter_context(nc.psum_tensor("banks", [P, 8, BANK], F32))
        g = {
            "x": ctx.enter_context(nc.sbuf_tensor("x_sb", [P, ST, D], F32)),
            "ident": ctx.enter_context(nc.sbuf_tensor("ident", [P, P], F32)),
            "identb": ctx.enter_context(nc.sbuf_tensor("identb", [P, P], BF16)),
            "on": ctx.enter_context(nc.sbuf_tensor("o_nat", [P, ST, HEADS, HD], F32)),
            "big": big, "ps": [big[:, i, :] for i in range(8)],
        }
        cross_attention_0(nc, g, a)
        if stop != "x1":
            moe_ffn_0(nc, g, a)
        if stop not in ("x1", "x2"):
            with ExitStack() as attn:
                g["kT"] = attn.enter_context(nc.sbuf_tensor("kT", [P, PAIRS, NK], BF16))
                g["vn"] = attn.enter_context(nc.sbuf_tensor("v_nat", [P, KT, HEADS, HD + 1], F32))
                g["qn"] = attn.enter_context(nc.sbuf_tensor("q_nat", [P, ST * HEADS, SLOT], BF16))
                g["qa"] = attn.enter_context(nc.sbuf_tensor("qa", [P, HG, BANK], BF16))
                g["cmax0"] = attn.enter_context(nc.sbuf_tensor("cmax0", [P, ROWS, NCH + 1], F32))
                project_keys(nc, g, a)
                if stop != "prep": cross_attention_1(nc, g, a)
            if stop is None:
                moe_by_argmax(nc, g, a, out)
                return
        s = ctx.enter_context(nc.semaphore("out_done"))
        with nc.Block() as block:
            @block.sync
            def _(sp):
                src = g["on"][:, :, :, :].rearrange("p t h d -> p t (h d)") if stop == "o" else g["x"][:, :, :]
                sp.dma_start(out.rearrange("(t p) d -> p t d", p=P), src).then_inc(s, 16)
                sp.wait_ge(s, 16)


def kernel(**inputs):
    import numpy as _np
    import concourse.bacc as _bacc
    from concourse import mybir as _mybir
    from concourse.bass_utils import run_bass_kernel_spmd as _run

    nc = _bacc.Bacc("TRN2", target_bir_lowering=False, num_devices=1)
    arrays, args = {}, {}
    for name, value in inputs.items():
        arrays[f"in_{name}_dram"] = _np.ascontiguousarray(value)
        args[name] = nc.dram_tensor(f"in_{name}_dram", arrays[f"in_{name}_dram"].shape,
                                    _mybir.dt.from_np(arrays[f"in_{name}_dram"].dtype),
                                    kind="ExternalInput").ap()
    out = nc.dram_tensor("out_0_dram", (1, S, D), _mybir.dt.float32, kind="ExternalOutput").ap()
    build(nc, args, out)
    r = _run(nc, [arrays], core_ids=[0])
    return r.results[0]["out_0_dram"]
```

```python
from contextlib import ExitStack

import concourse.bass as bass
from concourse import mybir

F32 = mybir.dt.float32
BF16 = mybir.dt.bfloat16
U32 = mybir.dt.uint32
ALU = mybir.AluOpType
ACT = mybir.ActivationFunctionType
AX_X = mybir.AxisListType.X

P = 128
D = 128
S = 1024
ST = S // P
NK = 6404
KF = NK // P
KR = NK - KF * P
KT = KF + 1
BANK = 512
NCH = NK // BANK
CR = NK - NCH * BANK
EPS = 1e-5
LOWEST = -3.0e38


class Link:

    def __init__(self, eng, sem):
        self.eng, self.sem, self.base, self.n = eng, sem, 0, 0

    def add(self, ins):
        self.n += 1
        ins.then_inc(self.sem, 1)

    def sync(self):
        self.eng.wait_ge(self.sem, self.base + self.n)

    def __call__(self, ins):
        self.add(ins)
        self.sync()

    def enter(self, i, per):
        self.start = self.base + self.n
        self.per = per
        self.base, self.n = self.start + i * per, 0

    def leave(self, passes):
        assert self.n == self.per, (self.n, self.per)
        self.base, self.n = self.start + passes * self.per, 0


def layer_norm_stats(nc, link, src, stats, mv, var, tiles, ready):
    for t in range(tiles):
        link.add(nc.vector.bn_stats(out=stats[:, t, :], in_=src[:, t, :]))
    link.sync()
    for t in range(tiles):
        link.add(nc.vector.bn_aggr(out=mv[:, t, :], in_=stats[:, t, :]))
    link.sync()
    nc.vector.tensor_scalar(var[:, :], mv[:, :, 1], EPS, None, ALU.add).then_inc(ready, 1)


def layer_norm_apply(nc, link, dst, src, mv, rstd, tiles, ready):
    link(nc.vector.reciprocal(rstd[:, :], rstd[:, :]))
    for t in range(tiles):
        nc.vector.tensor_scalar(dst[:, t, :], src[:, t, :], mv[:, t, 0:1], rstd[:, t:t + 1],
                                ALU.subtract, ALU.mult).then_inc(ready, 1)


def cross_attention_0(nc, g, a):
    SCALE = float(D) ** -0.5
    CB = 4
    MS = 2
    SB = 3
    TB = 3
    GROUPS = [list(range(4 * i, min(4 * i + 4, KT))) for i in range((KT + 3) // 4)]
    NG = len(GROUPS)
    with ExitStack() as ctx:
        def sb(name, shape, dt=F32):
            return ctx.enter_context(nc.sbuf_tensor(name, shape, dt))

        def sem(name):
            return ctx.enter_context(nc.semaphore(name))

        ctx_nat = sb("a0_ctx", [P, KT, D])
        kT = sb("a0_kT", [P, NK])
        ms = sb("a0_ms", [P, MS, NK])
        pr = sb("a0_pr", [P, MS, NK])
        chunk = sb("a0_chunk", [P, CB, 4, D])
        chunkT = sb("a0_chunkT", [P, 2, BANK])
        pT = sb("a0_pT", [P, TB, BANK])
        w_nat = sb("a0_w", [P, 2, D])
        w2T = sb("a0_w2T", [P, D])
        wT = sb("a0_wT", [P, D])
        bias = sb("a0_bias", [P, 2])
        bias21 = sb("a0_bias21", [P, 1])
        xn = sb("a0_xn", [P, ST, D])
        xnT = sb("a0_xnT", [P, S])
        qT = sb("a0_qT", [P, S])
        oT = sb("a0_oT", [P, 2, P])
        stats = sb("a0_stats", [P, ST, 6])
        mv = sb("a0_mv", [P, ST, 2])
        rstd = sb("a0_rstd", [P, ST])
        cmax = sb("a0_cmax", [P, 2, NCH + 1])
        nmax = sb("a0_nmax", [P, 2])
        total = sb("a0_total", [P, 2])
        rtotal = sb("a0_rtotal", [P, 2])
        q_tile = sb("a0_q_tile", [P, 2, P])
        ps = g["ps"]
        x = g["x"]
        q_tile_ready = sem("a0_q_tile_ready")

        x_in, w_in, ctx_in = sem("a0_x_in"), sem("a0_w_in"), sem("a0_ctx_in")
        chunk_in = [sem(f"a0_chunk_in{i}") for i in range(CB)]
        mask_in = [sem(f"a0_mask_in{i}") for i in range(MS)]
        part_in = [sem(f"a0_part_in{i}") for i in range(2)]
        ident_made = sem("a0_ident_made")
        w_turned, w_kept = sem("a0_w_turned"), sem("a0_w_kept")
        w_fused, wT_kept, bias_ready = sem("a0_w_fused"), sem("a0_wT_kept"), sem("a0_bias_ready")
        var_ready, std_ready, xn_ready = sem("a0_var"), sem("a0_std"), sem("a0_xn_ready")
        xn_turned, xnT_kept = sem("a0_xn_turned"), sem("a0_xnT_kept")
        q_ready, q_kept = sem("a0_q"), sem("a0_qk")
        chunk_turned, chunkT_kept = sem("a0_ct"), sem("a0_ck")
        k_ready, k_kept = sem("a0_k"), sem("a0_kk")
        scores_ready, scores_masked = sem("a0_s"), sem("a0_sm")
        max_ready, probs_ready = sem("a0_max"), sem("a0_probs")
        probs_turned, pT_kept, pv_done = sem("a0_pt"), sem("a0_ptk"), sem("a0_pv")
        out_ready, oT_kept, out_turned, x_done = sem("a0_o"), sem("a0_ok"), sem("a0_ot"), sem("a0_xd")
        dve_step, pool_step, dve_passed = sem("a0_dve_step"), sem("a0_pool_step"), sem("a0_dve_passed")

        block = ctx.enter_context(nc.Block())
        PART = 2 * BANK
        IN_LOOP = NCH // CB - 1
        LOADED_IN_PARTS = (0, 2 * IN_LOOP + 1)
        assert NCH % CB == 0 and CB == 4

        def chunk_width(c):
            return CR if isinstance(c, int) and c == NCH else BANK

        def turned_rows(kt):
            return P if kt < KF else KR

        @block.sync
        def _(sp):
            sp.dma_start(x[:, :, :], a["x"][0].rearrange("(t p) d -> p t d", p=P)).then_inc(x_in, 16)
            sp.dma_start(w_nat[:, 0, :], a["L0_xattn_W1"]).then_inc(w_in, 16)
            sp.dma_start(w_nat[:, 1, :], a["L0_xattn_W2"]).then_inc(w_in, 16)
            sp.dma_start(bias[:, 0:1], a["L0_xattn_b1"].rearrange("(p o) -> p o", o=1)).then_inc(w_in, 16)
            sp.dma_start(bias[:, 1:2], a["L0_xattn_b2"].rearrange("(p o) -> p o", o=1)).then_inc(w_in, 16)
            ctx_rows = a["ctx_1024"][0]

            def load_chunk(c, slot):
                sp.dma_start(chunk[:, slot, :, :],
                             ctx_rows[bass.ds(c * BANK, BANK), :].rearrange("(n p) d -> p n d", p=P)
                             ).then_inc(chunk_in[slot], 16)

            def load_mask(t, slot):
                sp.dma_start(ms[:, slot, :], a["fside_1xSxS2_0"][0][bass.ds(t * P, P), :]
                             ).then_inc(mask_in[slot], 16)

            def load_mask_part(t, first, n, into):
                sp.dma_start(ms[:, t, bass.ds(first, n)], a["fside_1xSxS2_0"][0][t * P:(t + 1) * P, bass.ds(first, n)]
                             ).then_inc(into, 16)

            for c in range(CB):
                load_chunk(c, c)
            for j in range(2):
                load_mask_part(0, j * PART, PART, part_in[j])
            with sp.Fori(1, NCH // CB) as i:
                for slot in range(CB):
                    sp.wait_ge(chunk_turned, CB * i + slot - CB + 1)
                    load_chunk(CB * i + slot, slot)
                    if slot % 2 == 0:
                        sp.wait_ge(part_in[slot // 2], 16 * i)
                        load_mask_part(0, (2 * i + slot // 2) * PART, PART, part_in[slot // 2])
                    else:
                        load_mask_part(1, (2 * i + slot // 2 - 2) * PART, PART, mask_in[1])
            sp.wait_ge(chunk_turned, NCH - CB + 1)
            sp.dma_start(chunk[:, 0, 0:2, :],
                         ctx_rows[NCH * BANK:KF * P, :].rearrange("(n p) d -> p n d", p=P)
                         ).then_inc(chunk_in[0], 16)
            sp.dma_start(chunk[0:KR, 0, 2, :], ctx_rows[KF * P:NK, :]).then_inc(chunk_in[0], 16)
            sp.wait_ge(part_in[0], 16 * (NCH // CB))
            load_mask_part(0, NCH * BANK, CR, part_in[0])
            load_mask_part(1, 2 * IN_LOOP * PART, NK - 2 * IN_LOOP * PART, mask_in[1])
            sp.dma_start(ctx_nat[:, 0:KF, :],
                         ctx_rows[0:KF * P, :].rearrange("(n p) d -> p n d", p=P)).then_inc(ctx_in, 16)
            sp.dma_start(ctx_nat[0:KR, KF, :], ctx_rows[KF * P:NK, :]).then_inc(ctx_in, 16)
            with sp.Fori(1, ST // 2) as i:
                for slot in range(2):
                    sp.wait_ge(probs_ready, 2 * i + slot - 1)
                    load_mask(2 * i + slot, slot)

        @block.gpsimd
        def _(pool):
            link = Link(pool, pool_step)
            for ident in (g["ident"], g["identb"]):
                link(nc.gpsimd.memset(ident[:, :], 0.0))
                nc.gpsimd.affine_select(out=ident[:, :], in_=ident[:, :], compare_op=ALU.not_equal,
                                        fill=1.0, base=0, pattern=[[-1, P]],
                                        channel_multiplier=1).then_inc(ident_made, 1)

        @block.tensor
        def _(pe):
            ident = g["ident"]
            pe.wait_ge(ident_made, 2)
            pe.wait_ge(w_in, 64)
            pe.transpose(ps[7][:, 0:D], w_nat[:, 1, :], ident[:, :]).then_inc(w_turned, 1)
            pe.wait_ge(w_kept, 1)
            pe.matmul(ps[6][:, 0:D], w_nat[:, 0, :], w2T[:, :], start=True, stop=True)
            pe.matmul(ps[6][:, D:D + 1], w2T[:, :], bias[:, 0:1], start=True, stop=True).then_inc(w_fused, 1)

            def turn_chunk(c, slot, loads):
                pe.wait_ge(chunk_in[slot], 16 * loads)
                wait(pe, chunkT_kept, c - 1)
                left = chunk_width(c)
                for j in range(-(-left // P)):
                    rows = min(P, left - j * P)
                    mm = pe.transpose(ps[slot % 2][:, j * P:j * P + rows], chunk[0:rows, slot, j, :],
                                      ident[0:rows, 0:rows])
                mm.then_inc(chunk_turned, 1)

            def project(c, slot):
                pe.wait_ge(chunkT_kept, c + 1)
                wait(pe, k_kept, c - 1)
                n = chunk_width(c)
                pe.matmul(ps[2 + slot % 2][:, 0:n], wT[:, :], chunkT[:, slot % 2, 0:n],
                          start=True, stop=True).then_inc(k_ready, 1)

            def first_scores(c, slot):
                pe.wait_ge(k_kept, c + 1)
                wait(pe, scores_masked, c - 1)
                n = chunk_width(c)
                pe.matmul(ps[4 + slot % 2][:, 0:n], q_tile[:, 0, :], kT[:, bass.ds(c * BANK, n)],
                          start=True, stop=True).then_inc(scores_ready, 1)

            turn_chunk(0, 0, 1)
            turn_chunk(1, 1, 1)
            pe.wait_ge(wT_kept, 1)
            project(0, 0)
            project(1, 1)
            pe.wait_ge(xn_ready, ST)
            for t in range(ST):
                mm = pe.transpose(ps[6 + t // 4][:, (t % 4) * P:(t % 4 + 1) * P], xn[:, t, :], ident[:, :])
                if t % 4 == 3:
                    mm.then_inc(xn_turned, 1)
            for j in range(2):
                pe.wait_ge(xnT_kept, j + 1)
                pe.matmul(ps[6 + j][:, :], wT[:, :], xnT[:, j * BANK:(j + 1) * BANK],
                          start=True, stop=True).then_inc(q_ready, 1)
            turn_chunk(2, 2, 1)
            project(2, 2)
            turn_chunk(3, 3, 1)
            project(3, 3)
            pe.wait_ge(q_tile_ready, 1)
            first_scores(0, 0)
            first_scores(1, 1)
            with pe.Fori(1, NCH // CB) as i:
                for slot in range(CB):
                    turn_chunk(CB * i + slot, slot, i + 1)
                    first_scores(CB * i + slot - 2, slot)
                    project(CB * i + slot, slot)
            turn_chunk(NCH, 0, NCH // CB + 2)
            first_scores(NCH - 2, 0)
            project(NCH, 0)
            first_scores(NCH - 1, 1)
            first_scores(NCH, 0)

            def turn_output(t, slot):
                pe.wait_ge(oT_kept, t + 1)
                pe.transpose(ps[6 + slot][:, 0:P], oT[:, slot, :], ident[:, :]).then_inc(out_turned, 1)

            def scores(t, slot, output=None):
                pe.wait_ge(q_tile_ready, t + 1)
                for c in range(NCH + 1):
                    n = BANK if c < NCH else CR
                    if c == SB and output is not None:
                        turn_output(output, slot)
                    pe.wait_ge(scores_masked, t * (NCH + 1) + max(c - SB + 1, 0))
                    pe.matmul(ps[c % SB][:, 0:n], q_tile[:, slot, :], kT[:, c * BANK:c * BANK + n],
                              start=True, stop=True).then_inc(scores_ready, 1)

            def turn_probs(t, slot, gi):
                for j, kt in enumerate(GROUPS[gi]):
                    rows = turned_rows(kt)
                    mm = pe.transpose(ps[SB + gi % TB][0:rows, j * P:(j + 1) * P],
                                      pr[:, slot, kt * P:kt * P + rows], ident[:, :])
                mm.then_inc(probs_turned, 1)

            def weigh(t, slot, first=False):
                pe.wait_ge(probs_ready, t + 1)
                for gi in range(NG + 1):
                    if gi < NG:
                        if gi >= TB:
                            pe.wait_ge(pT_kept, t * NG + gi - TB + 1)
                        elif not first:
                            pe.wait_ge(pT_kept, t * NG)
                        turn_probs(t, slot, gi)
                    if gi >= 1:
                        pe.wait_ge(pT_kept, t * NG + gi)
                        for j, kt in enumerate(GROUPS[gi - 1]):
                            rows = turned_rows(kt)
                            if kt == 0 and not first:
                                pe.wait_ge(x_done, t - 1)
                            mm = pe.matmul(ps[6 + slot][:, 0:P], ctx_nat[0:rows, kt, :],
                                           pT[0:rows, (gi - 1) % TB, j * P:(j + 1) * P],
                                           start=(kt == 0), stop=(kt == KT - 1))
                        mm.then_inc(pv_done, 1)

            scores(1, 1)
            pe.wait_ge(ctx_in, 32)
            weigh(0, 0, first=True)
            scores(2, 0, output=0)
            weigh(1, 1)
            scores(3, 1, output=1)
            with pe.Fori(1, ST // 2 - 1) as i:
                for slot in range(2):
                    weigh(2 * i + slot, slot)
                    scores(2 * i + slot + 2, slot, output=2 * i + slot)
            for slot in range(2):
                weigh(ST - 2 + slot, slot)
                turn_output(ST - 2 + slot, slot)

        @block.vector
        def _(dve):
            link = Link(dve, dve_step)
            dve.wait_ge(w_turned, 1)
            nc.vector.tensor_copy(w2T[:, :], ps[7][:, 0:D]).then_inc(w_kept, 1)
            dve.wait_ge(x_in, 16)
            layer_norm_stats(nc, link, x, stats, mv, rstd, ST, var_ready)

            def keep_chunk(c, slot):
                dve.wait_ge(chunk_turned, c + 1)
                wait(dve, k_ready, c - 1)
                n = chunk_width(c)
                nc.vector.tensor_copy(chunkT[:, slot % 2, 0:n], ps[slot % 2][:, 0:n]).then_inc(chunkT_kept, 1)

            dve.wait_ge(w_fused, 1)
            nc.vector.tensor_copy(wT[:, :], ps[6][:, 0:D]).then_inc(wT_kept, 1)
            link(nc.vector.tensor_tensor(bias21[:, :], ps[6][:, D:D + 1], bias[:, 1:2], ALU.add))
            dve.sem_inc(bias_ready, 1)
            keep_chunk(0, 0)
            keep_chunk(1, 1)
            dve.wait_ge(std_ready, 1)
            layer_norm_apply(nc, link, xn, x, mv, rstd, ST, xn_ready)
            for j in range(2):
                dve.wait_ge(xn_turned, j + 1)
                nc.vector.tensor_copy(xnT[:, j * BANK:(j + 1) * BANK], ps[6 + j][:, :]).then_inc(xnT_kept, 1)
            for j in range(2):
                dve.wait_ge(q_ready, j + 1)
                nc.vector.tensor_scalar(qT[:, j * BANK:(j + 1) * BANK], ps[6 + j][:, :], bias21[:, 0:1], SCALE,
                                        ALU.add, ALU.mult).then_inc(q_kept, 1)
            dve.wait_ge(q_kept, 2)
            for t in range(2):
                nc.vector.tensor_copy(q_tile[:, t, :], qT[:, t * P:(t + 1) * P]).then_inc(q_tile_ready, 1)

            def mask(t, slot, output=None):
                dve.wait_ge(mask_in[slot], 16 * (mask_no(t) + LOADED_IN_PARTS[slot]))
                for c in range(NCH + 1):
                    if c == SB + 1 and output is not None:
                        add_output(output, slot)
                    n = BANK if c < NCH else CR
                    at = slice(c * BANK, c * BANK + n)
                    wait_alone(dve, scores_ready, t * (NCH + 1) + c + 1, dve_passed)
                    dve.tensor_tensor_reduce(ms[:, slot, at], ps[c % SB][:, 0:n], ms[:, slot, at], 1.0, LOWEST,
                                             ALU.add, ALU.max, cmax[:, slot, c:c + 1]).then_inc(scores_masked, 1)

            def row_max(t, slot):
                dve.wait_ge(scores_masked, (t + 1) * (NCH + 1))
                dve.tensor_reduce(nmax[:, slot:slot + 1], cmax[:, slot, :], AX_X, ALU.max,
                                  negate=True).then_inc(max_ready, 1)

            def mask_no(t):
                return t // 2 if isinstance(t, int) else mask_pass[0]

            mask_pass = [None]

            def next_queries(t, slot):
                dve.wait_ge(scores_ready, (t - 1) * (NCH + 1))
                dve.tensor_copy(q_tile[:, slot, :], qT[:, bass.ds(t * P, P)]).then_inc(q_tile_ready, 1)

            def keep_probs(t, slot, following=2):
                for gi in range(NG):
                    if gi == 2 and following >= 1:
                        row_max(t + 1, 1 - slot)
                    if gi == 3 and following >= 2:
                        next_queries(t + 2, slot)
                    full = sum(kt < KF for kt in GROUPS[gi])
                    dve.wait_ge(probs_turned, t * NG + gi + 1)
                    if gi >= TB:
                        dve.wait_ge(pv_done, t * NG + gi - TB + 1)
                    else:
                        dve.wait_ge(pv_done, t * NG)
                    cp = dve.tensor_copy(pT[:, gi % TB, 0:full * P], ps[SB + gi % TB][:, 0:full * P])
                    if full < len(GROUPS[gi]):
                        cp = dve.tensor_copy(pT[0:KR, gi % TB, full * P:(full + 1) * P],
                                             ps[SB + gi % TB][0:KR, full * P:(full + 1) * P])
                    cp.then_inc(pT_kept, 1)
                dve.wait_ge(pv_done, (t + 1) * NG)
                dve.tensor_copy(oT[:, slot, :], ps[6 + slot][:, 0:P]).then_inc(oT_kept, 1)

            def add_output(t, slot):
                dve.wait_ge(out_turned, t + 1)
                link(nc.vector.reciprocal(rtotal[:, slot:slot + 1], total[:, slot:slot + 1]))
                xt = x[:, bass.ds(t, 1), :].rearrange("p t d -> p (t d)")
                dve.scalar_tensor_tensor(out=xt, in0=ps[6 + slot][:, 0:P], scalar=rtotal[:, slot:slot + 1],
                                         in1=xt, op0=ALU.mult, op1=ALU.add).then_inc(x_done, 1)

            def mask_first(c, slot, part, loads):
                dve.wait_ge(part_in[part], 16 * loads)
                wait_alone(dve, scores_ready, c + 1, dve_passed)
                n = chunk_width(c)
                at = bass.ds(c * BANK, n)
                dve.tensor_tensor_reduce(ms[:, 0, at], ps[4 + slot % 2][:, 0:n], ms[:, 0, at], 1.0, LOWEST,
                                         ALU.add, ALU.max, cmax[:, 0, bass.ds(c, 1)]).then_inc(scores_masked, 1)

            keep_chunk(2, 2)
            keep_chunk(3, 3)
            mask_first(0, 0, 0, 1)
            mask_first(1, 1, 0, 1)
            for c in range(CB, NCH):
                keep_chunk(c, c % CB)
                mask_first(c - 2, c % CB, (c - 2) // 2 % 2, (c - 2) // 4 + 1)
            keep_chunk(NCH, 0)
            for c in range(NCH - 2, NCH + 1):
                mask_first(c, c % CB, c // 2 % 2, c // 4 + 1)
            row_max(0, 0)
            mask(1, 1)
            for t in range(2):
                keep_probs(t, t)
                mask(t + 2, t, output=t)
            with dve.Fori(1, ST // 2 - 1) as i:
                link.enter(i - 1, 2)
                mask_pass[0] = i + 1
                for slot in range(2):
                    keep_probs(2 * i + slot, slot)
                    mask(2 * i + slot + 2, slot, output=2 * i + slot)
                link.leave(ST // 2 - 2)
            for slot in range(2):
                keep_probs(ST - 2 + slot, slot, following=1 - slot)
                add_output(ST - 2 + slot, slot)

        @block.scalar
        def _(act):
            act.wait_ge(var_ready, 1)
            nc.scalar.activation(rstd[:, :], rstd[:, :], ACT.Sqrt).then_inc(std_ready, 1)

            def keep_k(c, slot):
                act.wait_ge(k_ready, c + 1)
                n = chunk_width(c)
                nc.scalar.activation(kT[:, bass.ds(c * BANK, n)], ps[2 + slot % 2][:, 0:n], ACT.Identity,
                                     bias=bias21[:, 0:1]).then_inc(k_kept, 1)

            act.wait_ge(bias_ready, 1)
            for c in range(CB):
                keep_k(c, c)
            with act.Fori(1, NCH // CB) as i:
                for slot in range(CB):
                    keep_k(CB * i + slot, slot)
            keep_k(NCH, 0)

            def exps(t, slot, first=False):
                act.wait_ge(max_ready, t + 1)
                if not first:
                    act.wait_ge(probs_turned, (t - 1) * NG)
                    act.wait_ge(x_done, t - 1)
                nc.scalar.activation(pr[:, slot, :], ms[:, slot, :], ACT.Exp, bias=nmax[:, slot:slot + 1],
                                     accum_out=total[:, slot:slot + 1]).then_inc(probs_ready, 1)

            for t in range(2):
                exps(t, t, first=True)
            with act.Fori(1, ST // 2) as i:
                for slot in range(2):
                    exps(2 * i + slot, slot)


def wait(eng, sem, value):
    if not isinstance(value, int) or value > 0:
        eng.wait_ge(sem, value)


def wait_alone(eng, sem, value, passed):
    eng.wait_ge(sem, value)
    if not isinstance(value, int):
        eng.sem_inc(passed, 1)


def moe_ffn_0(nc, g, a):
    E = 16
    EA = E + 1
    TOPK = 8
    ROUTE_SCALE = 2.826
    PARTS = 3
    with ExitStack() as ctx:
        def sb(name, shape, dt=F32):
            return ctx.enter_context(nc.sbuf_tensor(name, shape, dt))

        def sem(name):
            return ctx.enter_context(nc.semaphore(name))

        w_nat = sb("m_w", [P, 2, 3, D])
        wT = sb("m_wT", [P, 2, 3, D])
        router = sb("m_router", [E, D])
        routerT = sb("m_routerT", [P, E])
        bias = sb("m_bias", [P, E])
        xn = sb("m_xn", [P, ST, D])
        xnT = sb("m_xnT", [P, S])
        stats = sb("m_stats", [P, ST, 6])
        mv = sb("m_mv", [P, ST, 2])
        rstd = sb("m_rstd", [P, ST])
        prob = sb("m_prob", [P, ST, E])
        sel = sb("m_sel", [P, ST, E])
        top = sb("m_top", [P, ST, TOPK])
        rest = sb("m_rest", [P, ST, E])
        weight = sb("m_weight", [P, ST, EA])
        wsum = sb("m_wsum", [P, ST])
        left = sb("m_left", [P, ST, EA])
        split = sb("m_split", [P, ST, P], BF16)
        splitT = sb("m_splitT", [P, S], BF16)
        pick = sb("m_pick", [P, EA, P], BF16)
        silu = sb("m_silu", [P, 2, BANK])
        h = sb("m_h", [P, 2, BANK])
        hw = xn[:, :, :].rearrange("p (s t) d -> p s (t d)", s=2)
        yT = xnT
        ps, x = g["ps"], g["x"]
        ident, identb = g["ident"], g["identb"]

        w_in = [sem(f"m_w_in{i}") for i in range(2)]
        small_in = sem("m_small_in")
        pool_made = sem("m_pool_made")
        var_ready, std_ready, xn_ready = sem("m_var"), sem("m_std"), sem("m_xn_ready")
        xn_turned, xnT_kept = sem("m_xn_turned"), sem("m_xnT_kept")
        router_turned, router_kept = sem("m_rt"), sem("m_rk")
        logits_ready, prob_ready, split_ready = sem("m_logits"), sem("m_prob_ready"), sem("m_split_ready")
        split_turned, split_kept = sem("m_split_turned"), sem("m_split_kept")
        w_turned, w_kept = sem("m_w_turned"), sem("m_w_kept")
        gate_ready, up_ready, spread_ready = sem("m_gate"), sem("m_up"), sem("m_spread")
        silu_ready, h_ready, hw_ready = sem("m_silu_ready"), sem("m_h_ready"), sem("m_hw_ready")
        down_done, y_kept, y_turned = sem("m_down"), sem("m_yk"), sem("m_yt")
        dve_step, pool_step = sem("m_dve_step"), sem("m_pool_step")

        block = ctx.enter_context(nc.Block())

        @block.sync
        def _(sp):
            def load(e, slot):
                for j, name in enumerate(("L0_ffn_w_gate", "L0_ffn_w_up", "L0_ffn_w_down")):
                    src = a[name][bass.ds(e, 1), :, :].rearrange("e p d -> (e p) d")
                    sp.dma_start(w_nat[:, slot, j, :], src).then_inc(w_in[slot], 16)

            load(0, 0)
            sp.dma_start(router[:, :], a["L0_ffn_gate_w"]).then_inc(small_in, 16)
            sp.dma_start(bias[:, :], a["L0_ffn_expert_bias"].partition_broadcast(P)).then_inc(small_in, 16)
            load(1, 1)
            with sp.Fori(1, E // 2) as i:
                for slot in range(2):
                    sp.wait_ge(w_turned, 2 * i + slot - 1)
                    load(2 * i + slot, slot)
            sp.wait_ge(w_turned, E - 1)
            for j, name in enumerate(("L0_ffn_shared_gate_w", "L0_ffn_shared_up_w", "L0_ffn_shared_down_w")):
                sp.dma_start(w_nat[:, 0, j, :], a[name]).then_inc(w_in[0], 16)
            g["prefetched"].load_small(sp, a)
            for c in range(2):
                g["prefetched"].load_chunk(sp, a, c, c)

        @block.gpsimd
        def _(pool):
            link = Link(pool, pool_step)
            nc.gpsimd.memset(split[:, :, :], 0.0).then_inc(pool_made, 1)
            nc.gpsimd.memset(weight[:, :, :], 1.0).then_inc(pool_made, 1)
            link(nc.gpsimd.memset(pick[:, :, :], 0.0))
            for part in range(PARTS):
                made = nc.gpsimd.affine_select(out=pick[:, :, :], in_=pick[:, :, :],
                                               compare_op=ALU.not_equal, fill=1.0, base=-part * EA,
                                               pattern=[[-1, EA], [0, P]], channel_multiplier=1)
                if part < PARTS - 1:
                    link(made)
            made.then_inc(pool_made, 1)
            g["prefetched"].constants(nc, g)

        @block.tensor
        def _(pe):
            def turn_weights(e, slot, loads):
                wait(pe, w_in[slot], 48 * loads)
                wait(pe, w_kept, e)
                for j in range(3):
                    mm = pe.transpose(ps[7][:, j * D:(j + 1) * D], w_nat[:, slot, j, :], ident[:, :])
                mm.then_inc(w_turned, 1)

            def gate_up(e, slot, half):
                n = 2 * e + half
                tok = slice(half * BANK, (half + 1) * BANK)
                if half == 0:
                    pe.wait_ge(w_kept, e + 1)
                wait(pe, silu_ready, n - 1)
                pe.matmul(ps[2 + half][:, :], wT[:, slot, 0, :], xnT[:, tok], start=True, stop=True
                          ).then_inc(gate_ready, 1)
                wait(pe, h_ready, n - 1)
                pe.matmul(ps[4 + half][:, :], wT[:, slot, 1, :], xnT[:, tok], start=True, stop=True
                          ).then_inc(up_ready, 1)

            def spread(e, half):
                tok = slice(half * BANK, (half + 1) * BANK)
                wait(pe, hw_ready, 2 * e + half)
                pe.matmul(ps[6][:, :], pick[:, bass.ds(e, 1), :].rearrange("p e m -> p (e m)"),
                          splitT[:, tok], start=True, stop=True).then_inc(spread_ready, 1)

            def down(n, slot, half, first=False, last=False):
                pe.wait_ge(hw_ready, n + 1)
                pe.matmul(ps[half][:, :], wT[:, slot, 2, :], hw[:, half, :], start=first, stop=last,
                          skip_group_check=True).then_inc(down_done, 1)

            pe.wait_ge(small_in, 32)
            pe.transpose(ps[2][:, 0:E], router[:, :], ident[0:E, 0:E]).then_inc(router_turned, 1)
            turn_weights(0, 0, 1)
            pe.wait_ge(xn_ready, ST)
            for t in range(ST):
                mm = pe.transpose(ps[t // 4][:, (t % 4) * P:(t % 4 + 1) * P], xn[:, t, :], ident[:, :])
                if t % 4 == 3:
                    mm.then_inc(xn_turned, 1)
            pe.wait_ge(router_kept, 1)
            pe.wait_ge(xnT_kept, 2)
            for t in range(ST):
                mm = pe.matmul(ps[6][:, t * E:(t + 1) * E], xnT[:, t * P:(t + 1) * P], routerT[:, :],
                               start=True, stop=True)
            mm.then_inc(logits_ready, 1)

            gate_up(0, 0, 0)
            gate_up(0, 0, 1)
            turn_weights(1, 1, 1)
            pe.wait_ge(split_ready, 1)
            for t in range(ST):
                mm = pe.transpose(ps[6][:, :].bitcast(BF16)[:, t * P:(t + 1) * P], split[:, t, :],
                                  identb[:, :])
            mm.then_inc(split_turned, 1)
            pe.wait_ge(split_kept, 1)
            pe.wait_ge(pool_made, 3)
            spread(0, 0)
            spread(0, 1)
            down(0, 0, 0, first=True)

            def expert(e, slot, loads, first=False, last=False):
                gate_up(e, slot, 0)
                spread(e, 0)
                if not last:
                    turn_weights(e + 1, 1 - slot, loads)
                down(2 * e - 1, 1 - slot, 1, first=first)
                gate_up(e, slot, 1)
                spread(e, 1)
                down(2 * e, slot, 0, last=last)

            expert(1, 1, 2, first=True)
            with pe.Fori(1, E // 2) as i:
                for k in range(2):
                    expert(2 * i + k, k, i + 1 + k)
            expert(E, 0, 0, last=True)
            down(2 * E + 1, 0, 1, last=True)
            for t in range(ST):
                if t % 4 == 0:
                    pe.wait_ge(y_kept, t // 4 + 1)
                mm = pe.transpose(ps[2 + t // 4][:, (t % 4) * P:(t % 4 + 1) * P],
                                  yT[:, t * P:(t + 1) * P], ident[:, :])
                if t % 4 == 3:
                    mm.then_inc(y_turned, 1)

        @block.scalar
        def _(act):
            act.wait_ge(var_ready, 1)
            nc.scalar.activation(rstd[:, :], rstd[:, :], ACT.Sqrt).then_inc(std_ready, 1)

            def keep_weights(e, slot):
                act.wait_ge(w_turned, e + 1)
                wait(act, down_done, 2 * e - 2)
                nc.scalar.activation(wT[:, slot, :, :], ps[7][:, 0:3 * D].rearrange("p (j d) -> p j d", d=D),
                                     ACT.Copy).then_inc(w_kept, 1)

            keep_weights(0, 0)
            act.wait_ge(logits_ready, 1)
            nc.scalar.activation(prob[:, :, :], ps[6][:, 0:ST * E].rearrange("p (t e) -> p t e", e=E),
                                 ACT.Sigmoid).then_inc(prob_ready, 1)

            def gate(n, half):
                act.wait_ge(gate_ready, n + 1)
                wait(act, h_ready, n - 1)
                nc.scalar.activation(silu[:, half, :], ps[2 + half][:, :], ACT.Silu).then_inc(silu_ready, 1)

            gate(0, 0)
            keep_weights(1, 1)
            gate(1, 1)
            gate(2, 0)
            keep_weights(2, 0)
            gate(3, 1)
            with act.Fori(1, E // 2) as i:
                for k in range(2):
                    e = 2 * i + k
                    gate(2 * e, 0)
                    keep_weights(e + 1, 1 - k)
                    gate(2 * e + 1, 1)
            gate(2 * E, 0)
            gate(2 * E + 1, 1)

        @block.vector
        def _(dve):
            link = Link(dve, dve_step)
            layer_norm_stats(nc, link, x, stats, mv, rstd, ST, var_ready)
            dve.wait_ge(router_turned, 1)
            nc.vector.tensor_copy(routerT[:, :], ps[2][:, 0:E]).then_inc(router_kept, 1)
            dve.wait_ge(std_ready, 1)
            layer_norm_apply(nc, link, xn, x, mv, rstd, ST, xn_ready)
            for j in range(2):
                dve.wait_ge(xn_turned, j + 1)
                nc.vector.tensor_copy(xnT[:, j * BANK:(j + 1) * BANK], ps[j][:, :]).then_inc(xnT_kept, 1)

            dve.wait_ge(prob_ready, 1)
            dve.wait_ge(small_in, 32)
            link(nc.vector.tensor_tensor(sel[:, :, :], prob[:, :, :],
                                         bias[:, :].unsqueeze(1).to_broadcast([P, ST, E]), ALU.add))
            for t in range(ST):
                link.add(nc.vector.max(out=top[:, t, :], in_=sel[:, t, :]))
            link.sync()
            for t in range(ST):
                link.add(nc.vector.match_replace(out=rest[:, t, :], in_to_replace=top[:, t, :],
                                                 in_values=sel[:, t, :], imm_value=LOWEST))
            link.sync()
            link(nc.vector.tensor_tensor(rest[:, :, :], rest[:, :, :], sel[:, :, :], ALU.not_equal))
            dve.wait_ge(pool_made, 2)
            link(nc.vector.tensor_tensor(weight[:, :, 0:E], prob[:, :, :], rest[:, :, :], ALU.mult))
            link(nc.vector.tensor_reduce(wsum[:, :], weight[:, :, 0:E], AX_X, ALU.add))
            link(nc.vector.reciprocal(wsum[:, :], wsum[:, :]))
            link(nc.vector.tensor_scalar(wsum[:, :], wsum[:, :], ROUTE_SCALE, None, ALU.mult))
            link(nc.vector.tensor_tensor(weight[:, :, 0:E], weight[:, :, 0:E],
                                         wsum[:, :].unsqueeze(2).to_broadcast([P, ST, E]), ALU.mult))
            link(nc.vector.tensor_copy(split[:, :, 0:EA], weight[:, :, :]))
            link(nc.vector.tensor_tensor(left[:, :, :], weight[:, :, :], split[:, :, 0:EA], ALU.subtract))
            link(nc.vector.tensor_copy(split[:, :, EA:2 * EA], left[:, :, :]))
            nc.vector.tensor_tensor(split[:, :, 2 * EA:3 * EA], left[:, :, :], split[:, :, EA:2 * EA],
                                    ALU.subtract).then_inc(split_ready, 1)
            dve.wait_ge(split_turned, 1)
            nc.vector.tensor_copy(splitT[:, :], ps[6][:, :].bitcast(BF16)).then_inc(split_kept, 1)

            def combine(n, half):
                dve.wait_ge(silu_ready, n + 1)
                dve.wait_ge(up_ready, n + 1)
                wait(dve, hw_ready, n - 1)
                nc.vector.tensor_tensor(h[:, half, :], silu[:, half, :], ps[4 + half][:, :], ALU.mult
                                        ).then_inc(h_ready, 1)
                dve.wait_ge(h_ready, n + 1)
                dve.wait_ge(spread_ready, n + 1)
                wait(dve, down_done, n - 1)
                nc.vector.tensor_tensor(hw[:, half, :], h[:, half, :], ps[6][:, :], ALU.mult
                                        ).then_inc(hw_ready, 1)

            for n in range(4):
                combine(n, n % 2)
            with dve.Fori(1, E // 2) as i:
                for k in range(4):
                    combine(4 * i + k, k % 2)
            for n in range(2 * E, 2 * EA):
                combine(n, n % 2)
            for j in range(2):
                dve.wait_ge(down_done, 2 * E + 1 + j)
                nc.vector.tensor_copy(yT[:, j * BANK:(j + 1) * BANK], ps[j][:, :]).then_inc(y_kept, 1)
            for j in range(2):
                dve.wait_ge(y_turned, j + 1)
                half = x[:, 4 * j:4 * j + 4, :]
                link(nc.vector.tensor_tensor(half, ps[2 + j][:, :].rearrange("p (t d) -> p t d", d=D),
                                             half, ALU.add))


HEADS = 16
HD = D // HEADS
PAIRS = HEADS // 2
SLOT = P // 2
PARTS = 3
K_PARTS = [(0, 0, 3), (1, 3, 2), (2, 5, 1)]
Q_PARTS = [(0, (0, 3, 5)), (1, (1, 4)), (2, (2,))]
MAX_ROW = 6 * HD


def head_rows(tile, blocks, count=1):
    return tile[:, :, blocks * HD:(blocks + count) * HD]


HG = 4
QT = BANK // P
ROWS = HG * QT


def turn_queries(pe, qn, identb, u, bank, done):
    for pair in range(HG // 2):
        for t in range(QT):
            at = (u * QT + t) * HG + 2 * pair
            mm = pe.transpose(bank.bitcast(BF16)[:, (pair * QT + t) * P:(pair * QT + t + 1) * P],
                              qn[:, bass.ds(at, 2), :].rearrange("p h r -> p (h r)"), identb[:, :])
    mm.then_inc(done, 1)


def padded(q, half):
    return q[SLOT * half:SLOT * half + SLOT, half:HG:2, :]


def turned(bank, half):
    return bank[SLOT * half:SLOT * half + SLOT, :].bitcast(BF16).rearrange("p (a q) -> p a q", a=HG // 2)


def project_keys(nc, g, a):
    GT = BANK // P
    KB, SBK = 4, 6
    GROUPS = PAIRS // 2
    SLICES = 16
    PROJECT_AT, TURN_AT = 7, 12
    assert SLICES == ROWS
    with ExitStack() as ctx:
        def sb(name, shape, dt=F32):
            return ctx.enter_context(nc.sbuf_tensor(name, shape, dt))

        def sem(name):
            return ctx.enter_context(nc.semaphore(name))

        chunkT = sb("p_chunkT", [P, 2, BANK])
        kf = sb("p_kf", [P, 2, GT * HEADS, HD])
        left = g["on"][:, :, :, :].rearrange("p (s j) h d -> p s (j h) d", s=2)
        kn = [sb(f"p_kn{i}", [P, GT * HEADS, SLOT], BF16) for i in range(2)]
        wT = sb("p_wT", [P, 3, D])
        xn = sb("p_xn", [P, ST, D])
        xnT = sb("p_xnT", [P, S])
        qf = xn[:, :, :].rearrange("p t (h d) -> p t h d", d=HD)
        qleft = xnT[:, :].rearrange("p (t h d) -> p t h d", h=HEADS, d=HD)
        stats = sb("p_stats", [P, ST, 6])
        mv = sb("p_mv", [P, ST, 2])
        rstd = sb("p_rstd", [P, ST])
        ps, x, kT, vn, qn = g["ps"], g["x"], g["kT"], g["vn"], g["qn"]
        qa, cmax = g["qa"], g["cmax0"]
        ident, identb = g["ident"], g["identb"]
        kT_flat = kT[:, :, :].rearrange("p a k -> p (a k)")
        qa_flat = qa[:, :, :].rearrange("p h q -> p (h q)")
        kv = g["big"][:, 2:4, :].rearrange("p b (j w d) -> p (b j) w d", w=2, d=D)

        ahead = g["prefetched"]
        chunk, w_nat, bias, small_in, chunk_in, made = (
            ahead.chunk, ahead.w_nat, ahead.bias, ahead.small_in, ahead.chunk_in, ahead.made)
        var_ready, std_ready, xn_ready = sem("p_var"), sem("p_std"), sem("p_xn_ready")
        w_turned, w_kept = sem("p_w_turned"), sem("p_w_kept")
        xn_turned, xnT_kept = sem("p_xn_turned"), sem("p_xnT_kept")
        q_ready, q_kept, q_scaled, q_split = sem("p_q_ready"), sem("p_q_kept"), sem("p_q_scaled"), sem("p_q_split")
        qa_turned, qa_kept = sem("p_qa_turned"), sem("p_qa_kept")
        chunk_turned, chunkT_kept = sem("p_chunk_turned"), sem("p_chunkT_kept")
        kv_ready, k_kept, v_kept = sem("p_kv"), sem("p_k_kept"), sem("p_v_kept")
        part0, left_ready, part1, part2 = sem("p_part0"), sem("p_left_ready"), sem("p_part1"), sem("p_part2")
        keys_turned, kT_kept = sem("p_keys_turned"), sem("p_kT_kept")
        piece_ready, piece_maxed = sem("p_piece"), sem("p_maxed")
        dve_step, pool_step, pool_passed = sem("p_dve_step"), sem("p_pool_step"), sem("p_pool_passed")

        block = ctx.enter_context(nc.Block())
        LAST_TILES = KT - GT * NCH
        FULL = [P] * GT
        LAST = [P] * (LAST_TILES - 1) + [KR]
        LOOP_FROM, LOOP_TO = 1, 9

        def exists(c, ahead):
            return not isinstance(c, int) or 0 <= c + ahead <= NCH

        def tiles_of(c):
            return LAST if isinstance(c, int) and c == NCH else FULL

        def width(c):
            return CR if isinstance(c, int) and c == NCH else BANK

        @block.sync
        def _(sp):
            ctx_rows = a["ctx_1024"][0]

            with sp.Fori(1, NCH // 2) as i:
                for slot in range(2):
                    sp.wait_ge(chunk_turned, 2 * i + slot - 1)
                    ahead.load_chunk(sp, a, 2 * i + slot, slot)
            sp.wait_ge(chunk_turned, NCH - 1)
            sp.dma_start(chunk[:, 0, 0:LAST_TILES - 1, :],
                         ctx_rows[NCH * BANK:KF * P, :].rearrange("(n p) d -> p n d", p=P)
                         ).then_inc(chunk_in[0], 16)
            sp.dma_start(chunk[0:KR, 0, LAST_TILES - 1, :], ctx_rows[KF * P:NK, :]).then_inc(chunk_in[0], 16)

        def put_rows(tiles):
            return [(0, GT, P)] if len(tiles) == GT else [(0, len(tiles) - 1, P), (len(tiles) - 1, 1, KR)]

        def q_rows(hg, blk):
            return qn[:, hg * ST * HG:(hg + 1) * ST * HG, blk * HD:(blk + 1) * HD].rearrange(
                "p (t h) d -> p t h d", h=HG)

        def split_queries(eng, link, hg):
            heads = slice(HG * hg, HG * hg + HG)
            src = qf[:, :, heads, :]
            rest = qleft[:, :, heads, :]
            for part in range(PARTS):
                for blk in Q_PARTS[part][1]:
                    link.add(eng.tensor_copy(q_rows(hg, blk), src))
                link.sync()
                if part < PARTS - 1:
                    link(eng.tensor_tensor(rest, src, q_rows(hg, Q_PARTS[part][1][0]), ALU.subtract))
                    src = rest

        @block.gpsimd
        def _(pool):
            link = Link(pool, pool_step)
            for i in range(2):
                nc.gpsimd.memset(kn[i][:, :, MAX_ROW:MAX_ROW + PARTS], 1.0).then_inc(made, 1)
                nc.gpsimd.memset(kn[i][:, :, MAX_ROW + PARTS:SLOT], 0.0).then_inc(made, 1)

            def leave(c, slot):
                wait_alone(pool, part0, c + 1, pool_passed)
                if not isinstance(c, int) or c >= 2:
                    wait_alone(pool, part2, c - 1, pool_passed)
                for first, n, rows in put_rows(tiles_of(c)):
                    hs = slice(first * HEADS, (first + n) * HEADS)
                    ins = nc.gpsimd.tensor_tensor(left[0:rows, slot, hs, :], kf[0:rows, slot, hs, :],
                                                  kn[slot][0:rows, hs, 0:HD], ALU.subtract)
                ins.then_inc(left_ready, 1)

            def third(c, slot):
                wait_alone(pool, part1, c + 1, pool_passed)
                wait_alone(pool, left_ready, c + 1, pool_passed)
                for first, n, rows in put_rows(tiles_of(c)):
                    hs = slice(first * HEADS, (first + n) * HEADS)
                    ins = nc.gpsimd.tensor_tensor(kn[slot][0:rows, hs, 5 * HD:6 * HD], left[0:rows, slot, hs, :],
                                                  kn[slot][0:rows, hs, 3 * HD:4 * HD], ALU.subtract)
                ins.then_inc(part2, 1)

            def step(c, slot):
                if exists(c, 2):
                    leave(c + 2, slot)
                    third(c + 2, slot)

            for c in range(2):
                leave(c, c)
                third(c, c)
            step(0, 0)
            with pool.Fori(0, (LOOP_TO - LOOP_FROM) // 2) as i:
                for k in range(2):
                    step(2 * i + (LOOP_FROM + k), (LOOP_FROM + k) % 2)
            pool.wait_ge(q_scaled, 1)
            for c in range(LOOP_TO, NCH + 2):
                step(c, c % 2)
                hg = c - LOOP_TO + 1
                if hg < HEADS // HG:
                    split_queries(nc.gpsimd, link, hg)

        @block.tensor
        def _(pe):
            def turn_chunk(c, slot, loads):
                pe.wait_ge(chunk_in[slot], 16 * loads)
                wait(pe, chunkT_kept, c - 1)
                for j, rows in enumerate(tiles_of(c)):
                    mm = pe.transpose(ps[slot][:, j * P:j * P + rows], chunk[0:rows, slot, j, :],
                                      ident[0:rows, 0:rows])
                mm.then_inc(chunk_turned, 1)

            def project(c, slot, j):
                tiles = tiles_of(c)
                if j >= len(tiles):
                    return
                if j == 0:
                    pe.wait_ge(chunkT_kept, c + 1)
                    wait(pe, k_kept, c)
                    wait(pe, v_kept, c)
                rows = tiles[j]
                mm = pe.matmul(ps[2 + j // 2][0:rows, (j % 2) * 2 * D:(j % 2 + 1) * 2 * D],
                               chunkT[:, slot, j * P:j * P + rows], wT[:, 1:3, :], start=True, stop=True)
                if j == len(tiles) - 1:
                    mm.then_inc(kv_ready, 1)

            def turn_keys(c, slot, b, i):
                if i == 0:
                    if b == 0:
                        pe.wait_ge(part2, c + 1)
                    wait(pe, kT_kept, GROUPS * c + b - 1)
                for j, rows in enumerate(tiles_of(c)):
                    h0 = j * HEADS + 2 * (2 * b + i)
                    mm = pe.transpose(
                        ps[KB + b % 2][:, :].bitcast(BF16)[:, i * BANK + j * P:i * BANK + j * P + rows],
                        kn[slot][0:rows, h0:h0 + 2, :].rearrange("p h r -> p (h r)"), identb[0:rows, 0:rows])
                if i == 1:
                    mm.then_inc(keys_turned, 1)

            def piece(c, r):
                if r == 0:
                    pe.wait_ge(kT_kept, GROUPS * c + 1)
                pe.wait_ge(piece_maxed, ROWS * c + r + 1)
                n = width(c)
                pe.matmul(ps[SBK + r % 2][:, 0:n], qa_flat[:, r * P:(r + 1) * P],
                          kT_flat[:, bass.ds((r // (ROWS // 2)) * NK + c * BANK, n)],
                          start=True, stop=True).then_inc(piece_ready, 1)

            def step(c, slot):
                for k in range(SLICES):
                    if exists(c, -1):
                        piece(c - 1, k)
                    if exists(c, 0) and k < 2 * GROUPS:
                        turn_keys(c, slot, k // 2, k % 2)
                    if exists(c, 2) and 0 <= k - PROJECT_AT < GT:
                        project(c + 2, slot, k - PROJECT_AT)
                    if exists(c, 3) and k == TURN_AT:
                        turn_chunk(c + 3, 1 - slot, loads_of(c + 3))

            now = [None]

            def loads_of(c):
                if isinstance(c, int):
                    return c // 2 + 1 + (c == NCH)
                return now[0] + (LOOP_FROM + 3) // 2 + 1

            def enter(i):
                now[0] = i

            pe.wait_ge(small_in, ahead.SMALL)
            for j in range(3):
                mm = pe.transpose(ps[7][:, j * D:(j + 1) * D], w_nat[:, j, :], ident[:, :])
            mm.then_inc(w_turned, 1)
            turn_chunk(0, 0, 1)
            turn_chunk(1, 1, 1)
            pe.wait_ge(w_kept, 1)
            for j in range(GT):
                project(0, 0, j)
            turn_chunk(2, 0, 2)
            pe.wait_ge(xn_ready, ST)
            for t in range(ST):
                mm = pe.transpose(ps[4 + t // 4][:, (t % 4) * P:(t % 4 + 1) * P], xn[:, t, :], ident[:, :])
                if t % 4 == 3:
                    mm.then_inc(xn_turned, 1)
            pe.wait_ge(xnT_kept, 2)
            for t in range(ST):
                mm = pe.matmul(ps[6 + t // 4][:, (t % 4) * D:(t % 4 + 1) * D], xnT[:, t * P:(t + 1) * P],
                               wT[:, 0, :], start=True, stop=True)
                if t % 4 == 3:
                    mm.then_inc(q_ready, 1)
            for j in range(GT):
                project(1, 1, j)
            pe.wait_ge(q_split, 1)
            turn_queries(pe, qn, identb, 0, ps[SBK], qa_turned)
            step(0, 0)
            pe.wait_ge(qa_kept, 2)
            with pe.Fori(0, (LOOP_TO - LOOP_FROM) // 2) as i:
                enter(i)
                for k in range(2):
                    step(2 * i + (LOOP_FROM + k), (LOOP_FROM + k) % 2)
            for c in range(LOOP_TO, NCH + 2):
                step(c, c % 2)

        @block.scalar
        def _(act):

            def keep_chunk(c, slot):
                n = width(c)
                act.wait_ge(chunk_turned, c + 1)
                wait(act, kv_ready, c - 1)
                nc.scalar.activation(chunkT[:, slot, 0:n], ps[slot][:, 0:n], ACT.Copy).then_inc(chunkT_kept, 1)

            def first_part(c, slot):
                act.wait_ge(k_kept, c + 1)
                wait(act, keys_turned, GROUPS * (c - 1))
                for first, n, rows in put_rows(tiles_of(c)):
                    hs = slice(first * HEADS, (first + n) * HEADS)
                    ins = nc.scalar.activation(
                        kn[slot][0:rows, hs, 0:3 * HD].rearrange("p h (r d) -> p h r d", d=HD),
                        kf[0:rows, slot, hs, :].unsqueeze(2).to_broadcast([rows, n * HEADS, 3, HD]), ACT.Copy)
                ins.then_inc(part0, 1)

            def keep_v(c):
                act.wait_ge(k_kept, c + 1)
                for first, n, rows in put_rows(tiles_of(c)):
                    ins = nc.scalar.activation(
                        vn[0:rows, bass.ds(c * GT + first, n), :, 0:HD],
                        kv[0:rows, first:first + n, 1, :].rearrange("p j (h d) -> p j h d", d=HD), ACT.Copy)
                ins.then_inc(v_kept, 1)

            def second_part(c, slot):
                act.wait_ge(left_ready, c + 1)
                for first, n, rows in put_rows(tiles_of(c)):
                    hs = slice(first * HEADS, (first + n) * HEADS)
                    ins = nc.scalar.activation(
                        kn[slot][0:rows, hs, 3 * HD:5 * HD].rearrange("p h (r d) -> p h r d", d=HD),
                        left[0:rows, slot, hs, :].unsqueeze(2).to_broadcast([rows, n * HEADS, 2, HD]), ACT.Copy)
                ins.then_inc(part1, 1)

            def keep(c, b):
                n = width(c)
                act.wait_ge(keys_turned, GROUPS * c + b + 1)
                nc.scalar.activation(
                    kT[:, 2 * b:2 * b + 2, bass.ds(c * BANK, n)],
                    ps[KB + b % 2][:, :].bitcast(BF16).rearrange("p (i n) -> p i n", i=2)[:, :, 0:n],
                    ACT.Copy).then_inc(kT_kept, 1)

            def step(c, slot):
                if exists(c, 0):
                    for b in range(GROUPS):
                        keep(c, b)
                if exists(c, 2):
                    first_part(c + 2, slot)
                    keep_v(c + 2)
                    second_part(c + 2, slot)
                if exists(c, 3):
                    keep_chunk(c + 3, 1 - slot)

            act.wait_ge(var_ready, 1)
            nc.scalar.activation(rstd[:, :], rstd[:, :], ACT.Sqrt).then_inc(std_ready, 1)
            keep_chunk(0, 0)
            keep_chunk(1, 1)
            act.wait_ge(made, 7)
            first_part(0, 0)
            keep_v(0)
            keep_chunk(2, 0)
            second_part(0, 0)
            first_part(1, 1)
            keep_v(1)
            second_part(1, 1)
            act.wait_ge(qa_turned, 1)
            nc.scalar.activation(padded(qa, 1), turned(ps[SBK], 1), ACT.Copy).then_inc(qa_kept, 1)
            step(0, 0)
            with act.Fori(0, (LOOP_TO - LOOP_FROM) // 2) as i:
                for k in range(2):
                    step(2 * i + (LOOP_FROM + k), (LOOP_FROM + k) % 2)
            for c in range(LOOP_TO, NCH + 2):
                step(c, c % 2)

        @block.vector
        def _(dve):
            link = Link(dve, dve_step)

            def keep_k(c, slot):
                dve.wait_ge(kv_ready, c + 1)
                wait(dve, left_ready, c - 1)
                for first, n, rows in put_rows(tiles_of(c)):
                    dst = kf[0:rows, slot, first * HEADS:(first + n) * HEADS, :].rearrange(
                        "p (j h) d -> p j (h d)", h=HEADS)
                    ins = nc.vector.tensor_tensor(dst, kv[0:rows, first:first + n, 0, :],
                                                  bias[0:rows, 1:2, :].to_broadcast([rows, n, D]), ALU.add)
                ins.then_inc(k_kept, 1)

            def reduce_piece(c, r):
                dve.wait_ge(piece_ready, ROWS * c + r + 1)
                nc.vector.tensor_reduce(cmax[:, r, bass.ds(c, 1)], ps[SBK + r % 2][:, 0:width(c)], AX_X,
                                        ALU.max).then_inc(piece_maxed, 1)

            def step(c, slot):
                for k in range(SLICES):
                    if exists(c, -1):
                        reduce_piece(c - 1, k)
                    if exists(c, 2) and k == PROJECT_AT + GT:
                        keep_k(c + 2, slot)
    
            dve.sem_inc(piece_maxed, 2)
            layer_norm_stats(nc, link, x, stats, mv, rstd, ST, var_ready)
            dve.wait_ge(w_turned, 1)
            nc.vector.tensor_copy(wT[:, :, :], ps[7][:, 0:3 * D].rearrange("p (j d) -> p j d", d=D)
                                  ).then_inc(w_kept, 1)
            dve.wait_ge(std_ready, 1)
            layer_norm_apply(nc, link, xn, x, mv, rstd, ST, xn_ready)
            dve.wait_ge(small_in, ahead.SMALL)
            keep_k(0, 0)
            for j in range(2):
                dve.wait_ge(xn_turned, j + 1)
                nc.vector.tensor_copy(xnT[:, j * BANK:(j + 1) * BANK], ps[4 + j][:, :]).then_inc(xnT_kept, 1)
            for j in range(2):
                dve.wait_ge(q_ready, j + 1)
                half = xn[:, 4 * j:4 * j + 4, :]
                nc.vector.tensor_tensor(half, ps[6 + j][:, :].rearrange("p (t d) -> p t d", d=D),
                                        bias[:, 0:1, :].to_broadcast([P, 4, D]), ALU.add).then_inc(q_kept, 1)
            dve.wait_ge(q_kept, 2)
            nc.vector.tensor_scalar(xn[:, :, :], xn[:, :, :], float(HD) ** -0.5, None, ALU.mult).then_inc(q_scaled, 1)
            keep_k(1, 1)
            dve.wait_ge(q_scaled, 1)
            dve.wait_ge(made, 7)
            split_queries(nc.vector, link, 0)
            dve.sem_inc(q_split, 1)
            dve.wait_ge(qa_turned, 1)
            nc.vector.tensor_copy(padded(qa, 0), turned(ps[SBK], 0)).then_inc(qa_kept, 1)
            step(0, 0)
            with dve.Fori(0, (LOOP_TO - LOOP_FROM) // 2) as i:
                for k in range(2):
                    step(2 * i + (LOOP_FROM + k), (LOOP_FROM + k) % 2)
            for c in range(LOOP_TO, NCH + 2):
                step(c, c % 2)


PATHS, DM = 9, D // 4
HW = PATHS * DM


class Prefetched:

    def __init__(self, nc, ctx):
        self.chunk = ctx.enter_context(nc.sbuf_tensor("p_chunk", [P, 2, BANK // P, D], F32))
        self.w_nat = ctx.enter_context(nc.sbuf_tensor("p_w", [P, 3, D], F32))
        self.bias = ctx.enter_context(nc.sbuf_tensor("p_bias", [P, 2, D], F32))
        self.small_in = ctx.enter_context(nc.semaphore("p_small_in"))
        self.chunk_in = [ctx.enter_context(nc.semaphore(f"p_chunk_in{i}")) for i in range(2)]
        self.made = ctx.enter_context(nc.semaphore("p_made"))
    SMALL = 16 * 5

    def load_chunk(self, sp, a, c, slot):
        sp.dma_start(self.chunk[:, slot, :, :],
                     a["ctx_1024"][0][bass.ds(c * BANK, BANK), :].rearrange("(n p) d -> p n d", p=P)
                     ).then_inc(self.chunk_in[slot], 16)

    def load_small(self, sp, a):
        for j, name in enumerate(("q", "k", "v")):
            sp.dma_start(self.w_nat[:, j, :], a[f"L1_xattn_W{name}"]).then_inc(self.small_in, 16)
            if name != "v":
                sp.dma_start(self.bias[:, j, :], a[f"L1_xattn_b{name}"].partition_broadcast(P)
                             ).then_inc(self.small_in, 16)

    def constants(self, nc, g):
        nc.gpsimd.memset(g["qn"][:, :, MAX_ROW:SLOT], 0.0).then_inc(self.made, 1)
        nc.gpsimd.memset(g["vn"][:, :, :, HD:HD + 1], 1.0).then_inc(self.made, 1)
        nc.gpsimd.memset(g["qa"][:, :, :], 0.0).then_inc(self.made, 1)


class LastWeights:
    LOADS = 15

    def __init__(self, nc, ctx):
        def sb(name, shape):
            return ctx.enter_context(nc.sbuf_tensor(name, shape, F32))

        self.wo_nat = sb("f_wo", [P, D])
        self.bo = sb("f_bo", [P, 1, D])
        self.bv = sb("f_bv", [P, 1])
        self.mixw = sb("f_mixw", [P, 3])
        self.w1 = sb("f_w1", [P, HW + DM])
        self.b1 = sb("f_b1", [P, HW + DM])
        self.w2 = sb("f_w2", [P, 3, D])
        self.wo2 = sb("f_wo2", [DM, PATHS])
        self.bo2 = sb("f_bo2", [P, 1, PATHS])
        self.gb = sb("f_gb", [P, 2, D])
        self.loaded = ctx.enter_context(nc.semaphore("f_loaded"))


def load_last_weights(nc, sp, w, a):
    wo_nat, bo, mixw, w1, b1, w2, wo2, bo2, gb = (
        w.wo_nat, w.bo, w.mixw, w.w1, w.b1, w.w2, w.wo2, w.bo2, w.gb)
    loads = [
        (wo_nat[:, :], a["L1_xattn_Wo"]),
        (bo[:, 0, :], a["L1_xattn_bo"].partition_broadcast(P)),
        (w.bv[:, :], a["L1_xattn_bv"].rearrange("(p o) -> p o", o=1)),
        (mixw[:, :], a["L1_ffn_mix_kernel"].rearrange("j d -> d j")),
        (w1[:, 0:HW].rearrange("d (p m) -> d p m", p=PATHS), a["L1_ffn_W1"].rearrange("p d m -> d p m")),
        (w1[:, HW:HW + DM], a["L1_ffn_Wo1"]),
        (b1[:, 0:HW], a["L1_ffn_b1"].rearrange("p m -> (p m)").partition_broadcast(P)),
        (b1[:, HW:HW + DM], a["L1_ffn_bo1"].partition_broadcast(P)),
        (w2[:, 0:2, :], a["L1_ffn_W2"].rearrange("p m d -> (p m) d")[0:2 * P, :].rearrange(
            "(c k) d -> k c d", k=P)),
        (w2[0:HW - 2 * P, 2, :], a["L1_ffn_W2"].rearrange("p m d -> (p m) d")[2 * P:HW, :]),
        (w2[HW - 2 * P:HW - 2 * P + PATHS, 2, :], a["L1_ffn_b2"]),
        (wo2[:, :], a["L1_ffn_Wo2"]),
        (bo2[:, 0, :], a["L1_ffn_bo2"].partition_broadcast(P)),
        (gb[:, 0, :], a["L1_ffn_gamma"].partition_broadcast(P)),
        (gb[:, 1, :], a["L1_ffn_beta"].partition_broadcast(P)),
    ]
    assert len(loads) == w.LOADS
    with nc.allow_non_contiguous_dma(reason="small weights"):
        for dst, src in loads:
            sp.dma_start(dst, src).then_inc(w.loaded, 16)


def cross_attention_1(nc, g, a):
    QH = S // BANK
    PIECES = 16
    PN = -(-NK // PIECES)
    MB = 4
    STEPS = HG * KT
    SB, PB, VB = 3, 12, 3
    TILES = 3
    PER = TILES * HG
    HEAD = 2
    AHEAD = 6
    MAXB, SCB, ACC = 0, 4, 7
    SCORE_BANKS = [SCB + i for i in range(SB)]
    LAST_BANKS = [MAXB + 1 + i for i in range(3)] + SCORE_BANKS
    assert SB <= HG and PER % len(LAST_BANKS) == 0 and PER % SB == 0 and PER % PB == 0 and TILES % VB == 0 and HEAD + ROWS * TILES + 1 == KT
    with ExitStack() as ctx:
        def sb(name, shape, dt=F32):
            return ctx.enter_context(nc.sbuf_tensor(name, shape, dt))

        def sem(name):
            return ctx.enter_context(nc.semaphore(name))

        qb = sb("x_qb", [P, QH, HG, BANK], BF16)
        probs = sb("x_probs", [P, PB, BANK])
        vt = sb("x_vt", [P, VB, HG, 32])
        cmax = sb("x_cmax", [P, ROWS, PIECES])
        nmax = sb("x_nmax", [P, ROWS])
        mleft = sb("x_mleft", [P, ROWS])
        oT = sb("x_oT", [P, BANK])
        rtotal = sb("x_rtotal", [P, QT, HG])
        ps, big = g["ps"], g["big"]
        kT, vn, qn, on, qa = g["kT"], g["vn"], g["qn"], g["on"], g["qa"]
        ident, identb = g["ident"], g["identb"]
        kT_flat = kT[:, :, :].rearrange("p a k -> p (a k)")
        qa_flat = qa[:, :, :].rearrange("p h q -> p (h q)")

        zeroed, first_zeroed, bo_added = sem("x_zeroed"), sem("x_first_zeroed"), sem("x_bo_added")
        qa_turned, qa_kept, qb_turned, qb_kept = sem("x_qat"), sem("x_qak"), sem("x_qbt"), sem("x_qbk")
        piece_ready, piece_maxed, max_split = sem("x_piece"), sem("x_maxed"), sem("x_max_split")
        scores_ready, probs_ready, pv_done = sem("x_scores"), sem("x_probs_ready"), sem("x_pv")
        v_ready, oT_kept, o_turned, o_done = sem("x_v"), sem("x_oT_kept"), sem("x_o_turned"), sem("x_o_done")
        dve_step = sem("x_dve_step")
        pe_passed, pool_passed = sem("x_pe_passed"), sem("x_pool_passed")

        block = ctx.enter_context(nc.Block())

        def tile_rows(kt):
            return P if kt < KF else KR

        @block.sync
        def _(sp):
            load_last_weights(nc, sp, g["last"], a)

        @block.gpsimd
        def _(pool):
            nc.gpsimd.memset(vt[:, :, :, :], 0.0).then_inc(zeroed, 1)
            nc.gpsimd.memset(qb[:, 1, :, :], 0.0).then_inc(zeroed, 1)
            pool.wait_ge(zeroed, 2)

            def fetch(u, hg, kt, slot, rows=P):
                back = HG * (kt - VB + 1)
                wait_alone(pool, pv_done, u * STEPS + 1 + (max(back, 0) if isinstance(back, int) else back),
                           pool_passed)
                nc.gpsimd.tensor_copy(
                    vt[0:rows, slot, :, 0:HD + 1],
                    vn[0:rows, bass.ds(kt, 1), bass.ds(hg * HG, HG), :].rearrange("p t h d -> p (t h) d")
                ).then_inc(v_ready, 1)

            with pool.Fori(0, HEADS // HG) as hg:
                for qh in range(QH):
                    u = hg * QH + qh
                    for kt in range(VB):
                        fetch(u, hg, kt, kt)
                    with pool.Fori(1, KT // VB - 1) as i:
                        for j in range(VB):
                            fetch(u, hg, VB * i + j, j)
                    for kt in range(KT - VB, KT):
                        fetch(u, hg, kt, kt % VB, tile_rows(kt))
            pool.wait_ge(g["last"].loaded, 16 * g["last"].LOADS)
            nc.gpsimd.tensor_tensor(g["x"][:, :, :], g["x"][:, :, :],
                                    g["last"].bo[:, :, :].to_broadcast([P, ST, D]), ALU.add).then_inc(bo_added, 1)

        @block.tensor
        def _(pe):
            pe.sem_inc(pv_done, 1)

            def piece(u, hg, half, r, j):
                row = half * (ROWS // 2) + r
                pe.wait_ge(piece_maxed, ((u - 1) * ROWS + row) * PIECES + j + 1)
                pe.matmul(ps[MAXB + j % MB][:, 0:PN], qa_flat[:, bass.ds(row * P, P)],
                          kT_flat[:, bass.ds((hg * 2 + half) * NK + min(j * PN, NK - PN), PN)],
                          start=True, stop=True).then_inc(piece_ready, 1)

            def score(u, qh, hg, n, kt, s, banks, rows=P):
                h = s % HG
                back = n - len(banks) + 1
                value = u * STEPS + 1 + (max(back, 0) if isinstance(back, int) else back)
                if rows < P:
                    wait_alone(pe, probs_ready, value, pe_passed)
                else:
                    pe.wait_ge(probs_ready, value)
                pe.matmul(ps[banks[s % len(banks)]][0:rows, :],
                          kT_flat[:, bass.ds((hg * 2 + h // 2) * NK + kt * P, rows)],
                          qb[:, qh, h, :], start=True, stop=True).then_inc(scores_ready, 1)

            def weigh(u, kt, s, banks, rows=P):
                if len(banks) > HG or rows < P:
                    wait_alone(pe, probs_ready, u * STEPS + (kt + 1) * HG + 1, pe_passed)
                if isinstance(kt, int) and kt == 0:
                    wait_alone(pe, o_done, u + 1, pe_passed)
                for h in range(HG):
                    mm = pe.matmul(ps[ACC][32 * h:32 * h + 32, :], vt[0:rows, s % VB, h, :],
                                   probs[0:rows, (s * HG + h) % PB, :], start=isinstance(kt, int) and kt == 0,
                                   stop=isinstance(kt, int) and kt == KT - 1, skip_group_check=True)
                mm.then_inc(pv_done, HG)

            def unit(u, qh, hg, next_u=None, next_hg=None, after=None, banks=SCORE_BANKS):
                with_next = next_u is not None

                def pieces_by(pieces, done, steps, of):
                    while done < len(pieces) and steps * PIECES > done * of:
                        piece(next_u, next_hg, *pieces[done])
                        done += 1
                    return done

                pe.wait_ge(qb_kept, 2 * u + 2)
                ahead = [(0, 0, j) for j in range(AHEAD)] if with_next else []
                done = 0
                for kt in range(HEAD):
                    for h in range(HG):
                        score(u, qh, hg, kt * HG + h, kt, kt * HG + h, banks)
                        if with_next and kt == 0 and h == 0:
                            wait_alone(pe, qa_kept, 2 * next_u, pe_passed)
                        done = pieces_by(ahead, done, kt * HG + h + 1, PER)
                    if kt > 0:
                        weigh(u, kt - 1, kt - 1, banks)
                assert done == len(ahead)

                def tiles_beside_row(half, r, next_row):
                    i = half * (ROWS // 2) + r
                    pieces = []
                    if with_next:
                        pieces = [(half, r, j) for j in range(AHEAD, PIECES)]
                    if with_next and next_row is not None:
                        pieces += [(*next_row, j) for j in range(AHEAD)]
                    done = 0
                    for k in range(TILES):
                        s = HEAD + k
                        for h in range(HG):
                            score(u, qh, hg, i * PER + s * HG + h, i * TILES + s, s * HG + h, banks)
                            done = pieces_by(pieces, done, k * HG + h + 1, PER)
                        weigh(u, i * TILES + s - 1, s - 1, banks)

                if with_next:
                    for half in range(2):
                        with pe.Fori(0, ROWS // 2 - 1) as r:
                            tiles_beside_row(half, r, (half, r + 1))
                        tiles_beside_row(half, ROWS // 2 - 1, (1, 0) if half == 0 else None)
                else:
                    with pe.Fori(0, ROWS) as r:
                        tiles_beside_row(0, r, None)
                for h in range(HG):
                    score(u, qh, hg, (KT - 1) * HG + h, KT - 1, (KT - 1) * HG + h, banks, KR)
                weigh(u, KT - 2, KT - 2, banks)
                if with_next:
                    wait_alone(pe, max_split, next_u + 1, pe_passed)
                    turn_queries(pe, qn, identb, next_u, ps[MAXB], qb_turned)
                weigh(u, KT - 1, KT - 1, banks, KR)
                if after is not None:
                    turn_queries(pe, qn, identb, after, ps[MAXB + 2], qa_turned)
                pe.wait_ge(oT_kept, u + 1)
                for t in range(QT):
                    mm = pe.transpose(ps[ACC][:, t * P:(t + 1) * P], oT[:, t * P:(t + 1) * P], ident[:, :])
                mm.then_inc(o_turned, 1)

            pe.wait_ge(max_split, 1)
            turn_queries(pe, qn, identb, 0, ps[MAXB], qb_turned)
            turn_queries(pe, qn, identb, 1, ps[MAXB + 2], qa_turned)
            G = HEADS // HG
            with pe.Fori(0, G - 1) as hg:
                unit(hg * QH, 0, hg, hg * QH + 1, hg, hg * QH + 2)
                unit(hg * QH + 1, 1, hg, hg * QH + 2, hg + 1, hg * QH + 3)
            unit((G - 1) * QH, 0, G - 1, (G - 1) * QH + 1, G - 1)
            unit((G - 1) * QH + 1, 1, G - 1, banks=LAST_BANKS)

        @block.scalar
        def _(act):
            def keep_queries(n, q, bank, done, kept):
                act.wait_ge(done, n + 1)
                nc.scalar.activation(padded(q, 1), turned(ps[bank], 1), ACT.Copy).then_inc(kept, 1)

            def exp(u, n, s, banks, count, rows=P):
                act.wait_ge(scores_ready, u * STEPS + n + count)
                if s % HG == 0:
                    back = n + HG - PB
                    act.wait_ge(pv_done, u * STEPS + 1 + (max(back, 0) if isinstance(back, int) else back))
                if s % HG == count:
                    act.wait_ge(v_ready, u * KT + (n // HG if isinstance(n, int) else v_at[0] + s // HG) + 1)
                bank = banks[s % len(banks)]
                nc.scalar.activation(probs[0:rows, s % PB:s % PB + count, :], big[0:rows, bank:bank + count, :],
                                     ACT.Exp).then_inc(probs_ready, count)

            v_at = [None]

            def unit(u, banks=SCORE_BANKS, count=1):
                for n in range(0, PER, count):
                    exp(u, n, n, banks, count)
                with act.Fori(1, STEPS // PER - 1) as i:
                    v_at[0] = i * TILES
                    for s in range(0, PER, count):
                        exp(u, i * PER + s, s, banks, count)
                for n in range(STEPS - PER, STEPS, count):
                    exp(u, n, n, banks, count, tile_rows(n // HG))

            act.sem_inc(probs_ready, 1)
            act.wait_ge(first_zeroed, 1)
            keep_queries(0, qb[:, 0], MAXB, qb_turned, qb_kept)
            act.wait_ge(zeroed, 2)
            keep_queries(0, qa, MAXB + 2, qa_turned, qa_kept)
            G = HEADS // HG

            def between(u, qh, last=False):
                keep_queries(u + 1, qb[:, 1 - qh], MAXB, qb_turned, qb_kept)
                if not last:
                    keep_queries(u + 1, qa, MAXB + 2, qa_turned, qa_kept)

            with act.Fori(0, G - 1) as hg:
                for qh in range(QH):
                    unit(hg * QH + qh)
                    between(hg * QH + qh, qh)
            unit((G - 1) * QH)
            between((G - 1) * QH, 0, last=True)
            unit((G - 1) * QH + 1, LAST_BANKS, count=2)

        @block.vector
        def _(dve):
            link = Link(dve, dve_step)

            def keep_queries(n, q, bank, done, kept):
                dve.wait_ge(done, n + 1)
                nc.vector.tensor_copy(padded(q, 0), turned(ps[bank], 0)).then_inc(kept, 1)

            def maxima(u):
                with dve.Fori(0, ROWS) as row:
                    for j in range(PIECES):
                        dve.wait_ge(piece_ready, ((u - 1) * ROWS + row) * PIECES + j + 1)
                        nc.vector.tensor_reduce(
                            cmax[:, bass.ds(row, 1), j:j + 1].rearrange("p r j -> p (r j)"),
                            ps[MAXB + j % MB][:, 0:PN], AX_X, ALU.max).then_inc(piece_maxed, 1)
                dve.wait_ge(piece_maxed, u * ROWS * PIECES + MB)
                split_maxima(u, cmax)

            def split_maxima(u, cmax):
                link(nc.vector.tensor_reduce(nmax[:, :], cmax[:, :, :], AX_X, ALU.max, negate=True))

                def row_of(part):
                    return qn[:, bass.ds(u * ROWS, ROWS), MAX_ROW + part:MAX_ROW + part + 1].rearrange(
                        "p (t h) o -> p h (t o)", h=HG)

                def by_head(v):
                    return v[:, :].rearrange("p (h t) -> p h t", h=HG)

                link(nc.vector.tensor_copy(row_of(0), by_head(nmax)))
                link(nc.vector.tensor_tensor(by_head(mleft), by_head(nmax), row_of(0), ALU.subtract))
                link(nc.vector.tensor_copy(row_of(1), by_head(mleft)))
                nc.vector.tensor_tensor(row_of(2), by_head(mleft), row_of(1), ALU.subtract
                                        ).then_inc(max_split, 1)

            def keep_output(u):
                dve.wait_ge(pv_done, (u + 1) * STEPS + 1)
                nc.vector.tensor_copy(oT[:, :], ps[ACC][:, :]).then_inc(oT_kept, 1)

            def outputs(u, qh, hg):
                dve.wait_ge(o_turned, u + 1)
                o = ps[ACC][:, :].rearrange("p (t h r) -> p t h r", t=QT, h=HG)
                link(nc.vector.reciprocal(rtotal[:, :, :], o[:, :, :, HD:HD + 1].rearrange("p t h o -> p t (h o)")))
                nc.vector.tensor_tensor(
                    on[:, qh * QT:(qh + 1) * QT, bass.ds(hg * HG, HG), :], o[:, :, :, 0:HD],
                    rtotal[:, :, :].unsqueeze(3).to_broadcast([P, QT, HG, HD]), ALU.mult).then_inc(o_done, 1)

            dve.sem_inc(piece_maxed, MB)
            dve.sem_inc(o_done, 1)
            nc.vector.memset(qb[:, 0, :, :], 0.0).then_inc(first_zeroed, 1)
            split_maxima(0, g["cmax0"])
            dve.wait_ge(first_zeroed, 1)
            keep_queries(0, qb[:, 0], MAXB, qb_turned, qb_kept)
            dve.wait_ge(zeroed, 2)
            keep_queries(0, qa, MAXB + 2, qa_turned, qa_kept)
            G = HEADS // HG

            def unit(u, qh, hg, last=False):
                maxima(u + 1)
                keep_queries(u + 1, qb[:, 1 - qh], MAXB, qb_turned, qb_kept)
                keep_output(u)
                if not last:
                    keep_queries(u + 1, qa, MAXB + 2, qa_turned, qa_kept)
                outputs(u, qh, hg)

            PER_UNIT = 5
            with dve.Fori(0, G - 1) as hg:
                link.enter(hg, QH * PER_UNIT)
                for qh in range(QH):
                    unit(hg * QH + qh, qh, hg)
            link.leave(G - 1)
            unit((G - 1) * QH, 0, G - 1, last=True)
            keep_output((G - 1) * QH + 1)
            outputs((G - 1) * QH + 1, 1, G - 1)


def moe_by_argmax(nc, g, a, out):
    KC = [(0, P), (P, P), (2 * P, HW + PATHS - 2 * P)]
    with ExitStack() as ctx:
        def sb(name, shape, dt=F32):
            return ctx.enter_context(nc.sbuf_tensor(name, shape, dt))

        def sem(name):
            return ctx.enter_context(nc.semaphore(name))

        woT = sb("f_woT", [P, D])
        onT = sb("f_onT", [P, S])
        y = sb("f_y", [P, ST, D])
        yT = sb("f_yT", [P, S + 2])
        mixT = sb("f_mixT", [P, S])
        hid = sb("f_hid", [P, ST, HW + DM])
        tanhT = sb("f_tanhT", [DM, S])
        score = sb("f_score", [P, ST, PATHS])
        top = sb("f_top", [P, ST, 8])
        top_at = sb("f_top_at", [P, ST, 8], U32)
        best = sb("f_best", [P, ST])
        iota = sb("f_iota", [P, PATHS])
        kept = sb("f_kept", [P, ST, HW + PATHS])
        keptT = sb("f_keptT", [P, 2, 3, P])
        z = sb("f_z", [P, ST, D])
        stats = sb("f_stats", [P, ST, 6])
        mv = sb("f_mv", [P, ST, 2])
        rstd = sb("f_rstd", [P, ST])
        ps, x, on, ident = g["ps"], g["x"], g["on"], g["ident"]
        w = g["last"]
        wo_nat, bo, mixw, w1, b1, w2, wo2, bo2, gb = (
            w.wo_nat, w.bo, w.mixw, w.w1, w.b1, w.w2, w.wo2, w.bo2, w.gb)

        made = sem("f_made")
        wo_turned, wo_kept, on_turned, onT_kept = sem("f_wt"), sem("f_wk"), sem("f_ot"), sem("f_ok")
        attn_ready = sem("f_attn")
        var_ready, std_ready, y_ready = sem("f_var"), sem("f_std"), sem("f_y_ready")
        y_turned, yT_kept, mix_ready = sem("f_yt"), sem("f_yk"), sem("f_mix")
        hid_ready, hid_kept, tanh_ready = sem("f_hid_ready"), sem("f_hid_kept"), sem("f_tanh")
        tanh_turned, tanhT_kept, score_ready = sem("f_tt"), sem("f_tk"), sem("f_score_ready")
        chosen, kept_turned = sem("f_chosen"), sem("f_kept_turned")
        keptT_kept = [sem("f_keptT_kept_even"), sem("f_keptT_kept_odd")]
        xb_ready, centred = sem("f_xb_ready"), sem("f_centred")
        path_done, var2_ready, std2_ready = sem("f_path"), sem("f_var2"), sem("f_std2")
        out_ready, out_done = sem("f_out_ready"), sem("f_out_done")
        dve_step = sem("f_dve_step")

        block = ctx.enter_context(nc.Block())

        @block.sync
        def _(sp):
            out_v = out.rearrange("b (t p) d -> p (b t) d", p=P)
            for j in range(2):
                sp.wait_ge(out_ready, 4 * j + 4)
                sp.dma_start(out_v[:, 4 * j:4 * j + 4, :], z[:, 4 * j:4 * j + 4, :]).then_inc(out_done, 16)
            sp.wait_ge(out_done, 32)

        @block.gpsimd
        def _(pool):
            nc.gpsimd.memset(yT[:, 0:1], 0.0).then_inc(made, 1)
            nc.gpsimd.memset(yT[:, S + 1:S + 2], 0.0).then_inc(made, 1)
            nc.gpsimd.iota(iota[:, :], pattern=[[1, PATHS]], base=0, channel_multiplier=0,
                           allow_small_or_imprecise_dtypes=True).then_inc(made, 1)
            pool.wait_ge(y_ready, ST)
            nc.gpsimd.tensor_tensor(x[:, :, :], x[:, :, :], gb[:, 1:2, :].to_broadcast([P, ST, D]), ALU.add
                                    ).then_inc(xb_ready, 1)

        @block.tensor
        def _(pe):
            pe.wait_ge(w.loaded, 16 * w.LOADS)
            pe.transpose(ps[2][:, 0:D], wo_nat[:, :], ident[:, :]).then_inc(wo_turned, 1)
            for t in range(ST):
                mm = pe.transpose(ps[t // 4][:, (t % 4) * P:(t % 4 + 1) * P],
                                  on[:, t, :, :].rearrange("p h d -> p (h d)"), ident[:, :])
                if t % 4 == 3:
                    mm.then_inc(on_turned, 1)
            pe.wait_ge(wo_kept, 1)
            for t in range(ST):
                if t % 4 == 0:
                    pe.wait_ge(onT_kept, t // 4 + 1)
                mm = pe.matmul(ps[4 + t // 4][:, (t % 4) * D:(t % 4 + 1) * D], onT[:, t * P:(t + 1) * P],
                               woT[:, :], start=True, stop=True)
                if t % 4 == 3:
                    mm.then_inc(attn_ready, 1)
            pe.wait_ge(y_ready, ST)
            for t in range(ST):
                mm = pe.transpose(ps[t // 4][:, (t % 4) * P:(t % 4 + 1) * P], y[:, t, :], ident[:, :])
                if t % 4 == 3:
                    mm.then_inc(y_turned, 1)
            pe.wait_ge(mix_ready, 1)
            for t in range(ST):
                if t >= 4:
                    pe.wait_ge(hid_kept, t - 3)
                pe.matmul(ps[t % 4][:, 0:HW + DM], mixT[:, t * P:(t + 1) * P], w1[:, :], start=True,
                          stop=True).then_inc(hid_ready, 1)
            for t in range(ST):
                pe.wait_ge(tanh_ready, t + 1)
                mm = pe.transpose(ps[4 + t // 4][0:DM, (t % 4) * P:(t % 4 + 1) * P], hid[:, t, HW:HW + DM],
                                  ident[:, :])
                if t % 4 == 3:
                    mm.then_inc(tanh_turned, 1)
            for t in range(ST):
                if t % 4 == 0:
                    pe.wait_ge(tanhT_kept, t // 4 + 1)
                mm = pe.matmul(ps[6][:, t * PATHS:(t + 1) * PATHS], tanhT[:, t * P:(t + 1) * P], wo2[:, :],
                               start=True, stop=True)
            mm.then_inc(score_ready, 1)

            def turn_kept(t):
                pe.wait_ge(chosen, t + 1)
                wait(pe, keptT_kept[t % 2], t // 2)
                for c, (k0, k) in enumerate(KC):
                    mm = pe.transpose(ps[t % 2][0:k, c * P:(c + 1) * P], kept[:, t, k0:k0 + k], ident[:, :])
                mm.then_inc(kept_turned, 1)

            turn_kept(0)
            for t in range(ST):
                if t + 1 < ST:
                    turn_kept(t + 1)
                pe.wait_ge(keptT_kept[t % 2], t // 2 + 1)
                for c, (k0, k) in enumerate(KC):
                    mm = pe.matmul(ps[4 + t // 4][:, (t % 4) * D:(t % 4 + 1) * D], keptT[0:k, t % 2, c, :],
                                   w2[0:k, c, :], start=(c == 0), stop=(c == 2))
                mm.then_inc(path_done, 1)

        @block.scalar
        def _(act):
            act.wait_ge(var_ready, 1)
            nc.scalar.activation(rstd[:, :], rstd[:, :], ACT.Sqrt).then_inc(std_ready, 1)
            for t in range(ST):
                act.wait_ge(hid_kept, t + 1)
                nc.scalar.activation(hid[:, t, HW:HW + DM], hid[:, t, HW:HW + DM], ACT.Tanh
                                     ).then_inc(tanh_ready, 1)
            for t in range(0, ST, 2):
                act.wait_ge(kept_turned, t + 1)
                wait(act, path_done, t - 1)
                nc.scalar.activation(keptT[:, t % 2, 0:2, :], ps[t % 2][:, 0:2 * P].rearrange(
                    "p (c q) -> p c q", c=2), ACT.Copy)
                k = KC[2][1]
                nc.scalar.activation(keptT[0:k, t % 2, 2, :], ps[t % 2][0:k, 2 * P:3 * P], ACT.Copy
                                     ).then_inc(keptT_kept[0], 1)
            act.wait_ge(var2_ready, 1)
            nc.scalar.activation(rstd[:, :], rstd[:, :], ACT.Sqrt).then_inc(std2_ready, 1)

        @block.vector
        def _(dve):
            link = Link(dve, dve_step)

            def tiles_of(bank):
                return ps[bank][:, :].rearrange("p (t d) -> p t d", d=D)

            dve.wait_ge(w.loaded, 16 * w.LOADS)
            dve.wait_ge(wo_turned, 1)
            nc.vector.tensor_copy(woT[:, :], ps[2][:, 0:D]).then_inc(wo_kept, 1)
            for j in range(2):
                dve.wait_ge(on_turned, j + 1)
                nc.vector.tensor_scalar(onT[:, j * BANK:(j + 1) * BANK], ps[j][:, :], w.bv[:, 0:1], None,
                                        ALU.add).then_inc(onT_kept, 1)
            for j in range(2):
                dve.wait_ge(attn_ready, j + 1)
                half = x[:, 4 * j:4 * j + 4, :]
                link(nc.vector.tensor_tensor(half, tiles_of(4 + j), half, ALU.add))
            layer_norm_stats(nc, link, x, stats, mv, rstd, ST, var_ready)
            dve.wait_ge(std_ready, 1)
            layer_norm_apply(nc, link, y, x, mv, rstd, ST, y_ready)
            for j in range(2):
                dve.wait_ge(y_turned, j + 1)
                nc.vector.tensor_copy(yT[:, 1 + j * BANK:1 + (j + 1) * BANK], ps[j][:, :]).then_inc(yT_kept, 1)
            dve.wait_ge(yT_kept, 2)
            dve.wait_ge(made, 3)
            link(nc.vector.tensor_scalar(mixT[:, :], yT[:, 1:S + 1], mixw[:, 1:2], None, ALU.mult))
            link(nc.vector.scalar_tensor_tensor(out=mixT[:, :], in0=yT[:, 0:S], scalar=mixw[:, 0:1],
                                                in1=mixT[:, :], op0=ALU.mult, op1=ALU.add))
            nc.vector.scalar_tensor_tensor(out=mixT[:, :], in0=yT[:, 2:S + 2], scalar=mixw[:, 2:3],
                                           in1=mixT[:, :], op0=ALU.mult, op1=ALU.add).then_inc(mix_ready, 1)
            for t in range(ST):
                dve.wait_ge(hid_ready, t + 1)
                nc.vector.tensor_tensor(hid[:, t, :], ps[t % 4][:, 0:HW + DM], b1[:, :], ALU.add
                                        ).then_inc(hid_kept, 1)
            for j in range(2):
                dve.wait_ge(tanh_turned, j + 1)
                nc.vector.tensor_copy(tanhT[:, j * BANK:(j + 1) * BANK], ps[4 + j][0:DM, :]).then_inc(tanhT_kept, 1)
            dve.wait_ge(score_ready, 1)
            link(nc.vector.tensor_tensor(score[:, :, :], ps[6][:, 0:ST * PATHS].rearrange(
                "p (t e) -> p t e", e=PATHS), bo2[:, :, :].to_broadcast([P, ST, PATHS]), ALU.add))
            for t in range(ST):
                link.add(nc.vector.max(out=top[:, t, :], in_=score[:, t, :]))
            link.sync()
            for t in range(ST):
                link.add(nc.vector.max_index(out=top_at[:, t, :], in_max=top[:, t, :], in_values=score[:, t, :]))
            link.sync()
            link(nc.vector.tensor_copy(best[:, :], top_at[:, :, 0]))
            link(nc.vector.tensor_tensor(kept[:, :, HW:HW + PATHS],
                                         iota[:, :].unsqueeze(1).to_broadcast([P, ST, PATHS]),
                                         best[:, :].unsqueeze(2).to_broadcast([P, ST, PATHS]), ALU.is_equal))
            dve.wait_ge(hid_kept, ST)
            for t in range(ST):
                nc.vector.tensor_tensor(
                    kept[:, t, 0:HW].rearrange("p (e m) -> p e m", e=PATHS),
                    hid[:, t, 0:HW].rearrange("p (e m) -> p e m", e=PATHS),
                    kept[:, t, HW:HW + PATHS].unsqueeze(2).to_broadcast([P, PATHS, DM]), ALU.mult
                ).then_inc(chosen, 1)
            for t in range(1, ST, 2):
                dve.wait_ge(kept_turned, t + 1)
                wait(dve, path_done, t - 1)
                nc.vector.tensor_copy(keptT[:, t % 2, 0:2, :], ps[t % 2][:, 0:2 * P].rearrange(
                    "p (c q) -> p c q", c=2))
                k = KC[2][1]
                nc.vector.tensor_copy(keptT[0:k, t % 2, 2, :], ps[t % 2][0:k, 2 * P:3 * P]
                                      ).then_inc(keptT_kept[1], 1)
            for j in range(2):
                dve.wait_ge(path_done, 4 * j + 4)
                link(nc.vector.tensor_tensor(z[:, 4 * j:4 * j + 4, :], tiles_of(4 + j),
                                             y[:, 4 * j:4 * j + 4, :], ALU.add))
            layer_norm_stats(nc, link, z, stats, mv, rstd, ST, var2_ready)
            dve.wait_ge(std2_ready, 1)
            link(nc.vector.reciprocal(rstd[:, :], rstd[:, :]))
            for t in range(ST):
                nc.vector.scalar_tensor_tensor(out=z[:, t, :], in0=z[:, t, :], scalar=mv[:, t, 0:1],
                                               in1=gb[:, 0, :], op0=ALU.subtract, op1=ALU.mult
                                               ).then_inc(centred, 1)
            dve.wait_ge(xb_ready, 1)
            for t in range(ST):
                dve.wait_ge(centred, t + 1)
                nc.vector.scalar_tensor_tensor(out=z[:, t, :], in0=z[:, t, :], scalar=rstd[:, t:t + 1],
                                               in1=x[:, t, :], op0=ALU.mult, op1=ALU.add
                                               ).then_inc(out_ready, 1)


def build(nc, a, out):
    with ExitStack() as ctx:
        big = ctx.enter_context(nc.psum_tensor("banks", [P, 8, BANK], F32))
        g = {
            "x": ctx.enter_context(nc.sbuf_tensor("x_sb", [P, ST, D], F32)),
            "ident": ctx.enter_context(nc.sbuf_tensor("ident", [P, P], F32)),
            "identb": ctx.enter_context(nc.sbuf_tensor("identb", [P, P], BF16)),
            "on": ctx.enter_context(nc.sbuf_tensor("o_nat", [P, ST, HEADS, HD], F32)),
            "big": big, "ps": [big[:, i, :] for i in range(8)],
        }
        cross_attention_0(nc, g, a)
        g["last"] = LastWeights(nc, ctx)
        with ExitStack() as attn:
            g["kT"] = attn.enter_context(nc.sbuf_tensor("kT", [P, PAIRS, NK], BF16))
            g["vn"] = attn.enter_context(nc.sbuf_tensor("v_nat", [P, KT, HEADS, HD + 1], F32))
            g["qn"] = attn.enter_context(nc.sbuf_tensor("q_nat", [P, ST * HEADS, SLOT], BF16))
            g["qa"] = attn.enter_context(nc.sbuf_tensor("qa", [P, HG, BANK], BF16))
            g["cmax0"] = attn.enter_context(nc.sbuf_tensor("cmax0", [P, ROWS, NCH + 1], F32))
            g["prefetched"] = Prefetched(nc, attn)
            moe_ffn_0(nc, g, a)
            project_keys(nc, g, a)
            cross_attention_1(nc, g, a)
        moe_by_argmax(nc, g, a, out)


def kernel(**inputs):
    import numpy as _np
    import concourse.bacc as _bacc
    from concourse import mybir as _mybir
    from concourse.bass_utils import run_bass_kernel_spmd as _run

    nc = _bacc.Bacc("TRN2", target_bir_lowering=False, num_devices=1)
    arrays, args = {}, {}
    for name, value in inputs.items():
        arrays[f"in_{name}_dram"] = _np.ascontiguousarray(value)
        args[name] = nc.dram_tensor(f"in_{name}_dram", arrays[f"in_{name}_dram"].shape,
                                    _mybir.dt.from_np(arrays[f"in_{name}_dram"].dtype),
                                    kind="ExternalInput").ap()
    out = nc.dram_tensor("out_0_dram", (1, S, D), _mybir.dt.float32, kind="ExternalOutput").ap()
    build(nc, args, out)
    r = _run(nc, [arrays], core_ids=[0])
    return r.results[0]["out_0_dram"]
```
